# Optimizing a Trainium2 kernel written in Bass

```python
import numpy as np
import jax
import jax.numpy as jnp

def _softmax(x, axis=-1):
    return jax.nn.softmax(x, axis=axis)

def _gelu(x):
    return jax.nn.gelu(x, approximate=True)

def _silu(x):
    return jax.nn.silu(x)

def _sigmoid(x):
    return jax.nn.sigmoid(x)

def _layernorm(x, axis=-1, eps=1e-05):
    m = jnp.mean(x, axis=axis, keepdims=True)
    v = jnp.var(x, axis=axis, keepdims=True)
    return (x - m) / jnp.sqrt(v + eps)

def _scatter_add(tgt, idx, src, axis=0):
    return tgt.at[idx].add(src)

def _segment_sum(src, seg, n):
    return jax.ops.segment_sum(src, seg, n)
kernel_name = 'mk_flamingo_gated_d2_seqx_r8_1856b7'

def setup_inputs(seed: int=0):
    np.random.seed(seed)
    _w = jnp.asarray

    def _rec_inputs():
        import jax
        import jax.numpy as jnp
        _rk = jax.random.key(seed)
        x = -0.0002928 + 1 * jax.random.normal(jax.random.fold_in(_rk, 1), (8, 128, 256), jnp.float32)
        _lenS = 128 - jax.random.randint(jax.random.fold_in(_rk, 7), (8,), 0, max(1, 128 // 4) + 1, jnp.int32)
        _lenS2 = 128 - jax.random.randint(jax.random.fold_in(_rk, 8), (8,), 0, max(1, 128 // 4) + 1, jnp.int32)
        fside_S2_0 = -0.00337071 + 1.01897 * jax.random.normal(jax.random.fold_in(_rk, 11), (128,), jnp.float32)
        _ctx_2048P = jax.random.normal(jax.random.fold_in(_rk, 12), (8, 16, 256), jnp.float32)
        _ctx_2048c = jax.random.dirichlet(jax.random.fold_in(_rk, 512), 0.3 * jnp.ones((16,), jnp.float32), (8, 128))
        _ctx_2048t = jnp.einsum('bsk,bkd->bsd', _ctx_2048c, _ctx_2048P)
        _ctx_2048t = _ctx_2048t * jax.lax.rsqrt(jnp.mean(jnp.square(_ctx_2048t)) + 1e-12) * 0.953939
        ctx_2048 = 0.000675642 + 1.00031 * (_ctx_2048t + 0.3 * jax.random.normal(jax.random.fold_in(_rk, 612), (8, 128, 256), jnp.float32))
        _validS = jnp.arange(128)[None, :] < _lenS[:, None]
        _validS2 = jnp.arange(128)[None, :] < _lenS2[:, None]
        _causal = jnp.tril(jnp.ones((128, 128), dtype=bool))
        mask_Bx1xSxS_fk0 = jnp.where(jnp.broadcast_to(_validS[:, None, None, :], (8, 1, 128, 128)), -1000000000.0, 0.0).astype(jnp.float32)
        _g = jax.random.normal(jax.random.fold_in(_rk, 9001), (2, 2), jnp.float32)
        _g = jnp.sign(_g) * jnp.maximum(jnp.abs(_g), 1.0) + (_g == 0) * 1.0
        g_xattn = _g[0]
        g_ffn = _g[1]
        return (x, fside_S2_0, ctx_2048, mask_Bx1xSxS_fk0, g_xattn, g_ffn)
    x, fside_S2_0, ctx_2048, mask_Bx1xSxS_fk0, g_xattn, g_ffn = _rec_inputs()

    def _L0_xattn_setup():
        import jax, jax.numpy as jnp
        import numpy as np
        key = jax.random.key(seed)
        ks = jax.random.split(key, 5)
        B, D, L, NH = (2, 128, 256, 8)
        H = D // NH
        return {'v': jax.random.normal(ks[0], (B, D, L), jnp.float32), 'k': jax.random.normal(ks[1], (H, L), jnp.float32) * 0.1, 'bias': jax.random.normal(ks[2], (D,), jnp.float32), 'x1': jax.random.normal(ks[3], (B, D, L), jnp.float32), 'x2': jax.random.normal(ks[4], (B, D, L), jnp.float32), 'num_heads': NH}
    _L0_xattn_all = _L0_xattn_setup()
    _L0_xattn_in = {k: v for k, v in _L0_xattn_all.items() if k in ('k',)}
    del _L0_xattn_all

    def _L0_ffn_setup():
        import jax, jax.numpy as jnp
        import numpy as np
        HIDDEN = 256
        NUM_EXPERTS = 8
        TOP_K = 2
        MOE_INTER = 176
        SHARED_INTER = 704

        def _silu_and_mul(gu):
            i = gu.shape[-1] // 2
            return jax.nn.silu(gu[:, :i]) * gu[:, i:]
        key = jax.random.key(seed)
        ks = jax.random.split(key, 7)
        s = 0.02
        return {'hidden_states': jax.random.normal(ks[0], (2, 256, HIDDEN), dtype=jnp.float32), 'gate_w': jax.random.normal(ks[1], (NUM_EXPERTS, HIDDEN), dtype=jnp.float32) * s, 'shared_gate_w': jax.random.normal(ks[2], (1, HIDDEN), dtype=jnp.float32) * s, 'shared_gate_up_w': jax.random.normal(ks[3], (2 * SHARED_INTER, HIDDEN), dtype=jnp.float32) * s, 'shared_down_w': jax.random.normal(ks[4], (HIDDEN, SHARED_INTER), dtype=jnp.float32) * s, 'w13': jax.random.normal(ks[5], (NUM_EXPERTS, 2 * MOE_INTER, HIDDEN), dtype=jnp.float32) * s, 'w2': jax.random.normal(ks[6], (NUM_EXPERTS, HIDDEN, MOE_INTER), dtype=jnp.float32) * s}
    _L0_ffn_all = _L0_ffn_setup()
    _L0_ffn_in = {k: v for k, v in _L0_ffn_all.items() if k in ('gate_w', 'shared_gate_w', 'shared_gate_up_w', 'shared_down_w', 'w13', 'w2')}
    del _L0_ffn_all

    def _L1_xattn_setup():
        import jax, jax.numpy as jnp
        import numpy as np
        import math
        B, S, HID, H = (2, 256, 256, 32)
        D = HID // H
        AL = 10

        def _rope_tables(seq_len, dim, dtype):
            inv_freq = 1.0 / 10000.0 ** (np.arange(0, dim, 2, dtype=np.float32) / dim)
            t = np.arange(seq_len, dtype=np.float32)
            freqs = np.outer(t, inv_freq)
            emb = np.concatenate([freqs, freqs], -1)
            return (jnp.asarray(np.cos(emb), dtype), jnp.asarray(np.sin(emb), dtype))

        def _rotate_half(x):
            x1, x2 = jnp.split(x, 2, axis=-1)
            return jnp.concatenate([-x2, x1], axis=-1)
        key = jax.random.key(seed)
        ks = jax.random.split(key, 8)
        hidden_states = jax.random.normal(ks[0], (B, S, HID), dtype=jnp.float32)
        adapter = jax.random.normal(ks[1], (B, AL, HID), dtype=jnp.float32)
        causal = jnp.tril(jnp.ones((S, S), dtype=bool))
        attention_mask = jnp.broadcast_to(jnp.where(causal, 0.0, -1000000000.0).astype(jnp.float32)[None, None], (B, 1, S, S))
        scale = 0.02
        Wq = jax.random.normal(ks[2], (HID, HID), dtype=jnp.float32) * scale
        Wk = jax.random.normal(ks[3], (HID, HID), dtype=jnp.float32) * scale
        Wv = jax.random.normal(ks[4], (HID, HID), dtype=jnp.float32) * scale
        Wo = jax.random.normal(ks[5], (HID, HID), dtype=jnp.float32) * scale
        gate = jax.random.normal(ks[6], (1, H, 1, 1), dtype=jnp.float32) * 0.1
        return {'hidden_states': hidden_states, 'attention_mask': attention_mask, 'adapter': adapter, 'Wq': Wq, 'Wk': Wk, 'Wv': Wv, 'Wo': Wo, 'gate': gate}
    _L1_xattn_all = _L1_xattn_setup()
    _L1_xattn_in = {k: v for k, v in _L1_xattn_all.items() if k in ('Wq', 'Wk', 'Wv', 'Wo', 'gate')}
    del _L1_xattn_all

    def _L1_ffn_setup():
        import jax, jax.numpy as jnp
        import numpy as np
        TOPK = 6
        CAP = 128
        ROUTE_SCALE = 1.0
        key = jax.random.key(seed)
        k = jax.random.split(key, 6)
        B, T, C = (2, 256, 256)
        E, H, HS = (64, 32, 64)
        std = 0.01
        return {'x': jax.random.normal(k[0], (B, T, C), jnp.float32), 'w_gate': jax.random.normal(k[1], (C, E), jnp.float32) * std, 'w_shared_up': jax.random.normal(k[2], (C, 2 * HS), jnp.float32) * std, 'w_shared_down': jax.random.normal(k[3], (HS, C), jnp.float32) * std, 'w_up': jax.random.normal(k[4], (E, C, 2 * H), jnp.float32) * std, 'w_down': jax.random.normal(k[5], (E, H, C), jnp.float32) * std}
    _L1_ffn_all = _L1_ffn_setup()
    _L1_ffn_in = {k: v for k, v in _L1_ffn_all.items() if k in ('w_gate', 'w_shared_up', 'w_shared_down', 'w_up', 'w_down')}
    del _L1_ffn_all
    return {'x': x, 'fside_S2_0': fside_S2_0, 'ctx_2048': ctx_2048, 'mask_Bx1xSxS_fk0': mask_Bx1xSxS_fk0, 'g_xattn': g_xattn, 'g_ffn': g_ffn, 'L0_xattn_k': _L0_xattn_in['k'], 'L0_ffn_gate_w': _L0_ffn_in['gate_w'], 'L0_ffn_shared_gate_w': _L0_ffn_in['shared_gate_w'], 'L0_ffn_shared_gate_up_w': _L0_ffn_in['shared_gate_up_w'], 'L0_ffn_shared_down_w': _L0_ffn_in['shared_down_w'], 'L0_ffn_w13': _L0_ffn_in['w13'], 'L0_ffn_w2': _L0_ffn_in['w2'], 'L1_xattn_Wq': _L1_xattn_in['Wq'], 'L1_xattn_Wk': _L1_xattn_in['Wk'], 'L1_xattn_Wv': _L1_xattn_in['Wv'], 'L1_xattn_Wo': _L1_xattn_in['Wo'], 'L1_xattn_gate': _L1_xattn_in['gate'], 'L1_ffn_w_gate': _L1_ffn_in['w_gate'], 'L1_ffn_w_shared_up': _L1_ffn_in['w_shared_up'], 'L1_ffn_w_shared_down': _L1_ffn_in['w_shared_down'], 'L1_ffn_w_up': _L1_ffn_in['w_up'], 'L1_ffn_w_down': _L1_ffn_in['w_down']}

def reference(x, fside_S2_0, ctx_2048, mask_Bx1xSxS_fk0, g_xattn, g_ffn, L0_xattn_k, L0_ffn_gate_w, L0_ffn_shared_gate_w, L0_ffn_shared_gate_up_w, L0_ffn_shared_down_w, L0_ffn_w13, L0_ffn_w2, L1_xattn_Wq, L1_xattn_Wk, L1_xattn_Wv, L1_xattn_Wo, L1_xattn_gate, L1_ffn_w_gate, L1_ffn_w_shared_up, L1_ffn_w_shared_down, L1_ffn_w_up, L1_ffn_w_down):
    import jax
    import jax.numpy as jnp

    def _L0_xattn_ref(v, k, bias, x1, x2, num_heads):
        import jax, jax.numpy as jnp
        import numpy as np
        B, D, L = v.shape
        H = D // num_heads
        fft_size = 2 * L
        vr = v.reshape(B, H, num_heads, L)
        x1r = x1.reshape(B, H, num_heads, L)
        x2r = x2.reshape(B, H, num_heads, L)
        kv = vr[:, :, :, None, :] * x2r[:, :, None, :, :]
        k_f = jnp.fft.rfft(k.astype(jnp.float32), n=fft_size)
        y = jnp.fft.irfft(jnp.fft.rfft(kv, n=fft_size) * k_f[None, :, None, None, :], n=fft_size)[..., :L]
        skip = bias.astype(jnp.float32).reshape(H, num_heads)[None, :, :, None, None]
        y = y + kv * skip
        out = jnp.einsum('bhijl,bhil->bhjl', y, x1r)
        return out.reshape(B, D, L)

    def _L0_ffn_ref(hidden_states, gate_w, shared_gate_w, shared_gate_up_w, shared_down_w, w13, w2):
        import jax, jax.numpy as jnp
        import numpy as np
        HIDDEN = 256
        NUM_EXPERTS = 8
        TOP_K = 2
        MOE_INTER = 176
        SHARED_INTER = 704

        def _silu_and_mul(gu):
            i = gu.shape[-1] // 2
            return jax.nn.silu(gu[:, :i]) * gu[:, i:]
        orig_shape = hidden_states.shape
        x = hidden_states.reshape(-1, orig_shape[-1])
        shared = _silu_and_mul(x @ shared_gate_up_w.T) @ shared_down_w.T
        shared = shared * jax.nn.sigmoid(x @ shared_gate_w.T)
        router_logits = x @ gate_w.T
        probs = jax.nn.softmax(router_logits.astype(jnp.float32), axis=-1)
        routing_weights, selected_experts = jax.lax.top_k(probs, TOP_K)
        combined = jnp.zeros(x.shape, dtype=jnp.float32)
        E = w13.shape[0]
        for e in range(E):
            w_e = jnp.where(selected_experts == e, routing_weights, 0.0).sum(-1)
            h = _silu_and_mul(x @ w13[e].T) @ w2[e].T
            combined = combined + w_e[:, None] * h.astype(jnp.float32)
        out = shared + combined.astype(x.dtype)
        return out.reshape(orig_shape)

    def _L1_xattn_ref(hidden_states, attention_mask, adapter, Wq, Wk, Wv, Wo, gate):
        import jax, jax.numpy as jnp
        import numpy as np
        import math
        B, S, HID, H = (2, 256, 256, 32)
        D = HID // H
        AL = 10

        def _rope_tables(seq_len, dim, dtype):
            inv_freq = 1.0 / 10000.0 ** (np.arange(0, dim, 2, dtype=np.float32) / dim)
            t = np.arange(seq_len, dtype=np.float32)
            freqs = np.outer(t, inv_freq)
            emb = np.concatenate([freqs, freqs], -1)
            return (jnp.asarray(np.cos(emb), dtype), jnp.asarray(np.sin(emb), dtype))

        def _rotate_half(x):
            x1, x2 = jnp.split(x, 2, axis=-1)
            return jnp.concatenate([-x2, x1], axis=-1)
        bsz, q_len, hid = hidden_states.shape
        n_heads = gate.shape[1]
        head_dim = hid // n_heads
        inv_sqrt_d = 1.0 / math.sqrt(head_dim)

        def split_heads(x, length):
            return x.reshape(bsz, length, n_heads, head_dim).transpose(0, 2, 1, 3)
        q = split_heads(hidden_states @ Wq, q_len)
        k = split_heads(hidden_states @ Wk, q_len)
        v = split_heads(hidden_states @ Wv, q_len)
        cos, sin = _rope_tables(q_len, head_dim, q.dtype)
        q = q * cos + _rotate_half(q) * sin
        k = k * cos + _rotate_half(k) * sin
        scores = jnp.einsum('bhqd,bhkd->bhqk', q, k) * inv_sqrt_d
        scores = scores + attention_mask
        scores = jnp.maximum(scores, jnp.finfo(scores.dtype).min)
        w = jax.nn.softmax(scores.astype(jnp.float32), axis=-1).astype(q.dtype)
        attn_output = jnp.einsum('bhqk,bhkd->bhqd', w, v)
        adapter_len = adapter.shape[1]
        a_k = split_heads(adapter @ Wk, adapter_len)
        a_v = split_heads(adapter @ Wv, adapter_len)
        a_scores = jnp.einsum('bhqd,bhkd->bhqk', q, a_k) * inv_sqrt_d
        a_scores = jnp.tanh(gate) * jax.nn.softmax(a_scores.astype(jnp.float32), axis=-1).astype(q.dtype)
        attn_output = attn_output + jnp.einsum('bhqk,bhkd->bhqd', a_scores, a_v)
        attn_output = attn_output.transpose(0, 2, 1, 3).reshape(bsz, q_len, hid)
        return attn_output @ Wo

    def _L1_ffn_ref(x, w_gate, w_shared_up, w_shared_down, w_up, w_down):
        import jax, jax.numpy as jnp
        import numpy as np
        TOPK = 6
        CAP = 128
        ROUTE_SCALE = 1.0
        B, T, C = x.shape
        E = w_gate.shape[1]
        x_flat = x.reshape(-1, C)
        N = x_flat.shape[0]
        su = x_flat @ w_shared_up
        y_s, g_s = jnp.split(su, 2, axis=-1)
        shared = jax.nn.silu(g_s) * y_s @ w_shared_down
        scores = jax.nn.sigmoid(x_flat @ w_gate)
        _, topk_idx = jax.lax.top_k(scores, TOPK)
        w = jnp.take_along_axis(scores, topk_idx, axis=-1)
        w = w / w.sum(-1, keepdims=True) * ROUTE_SCALE
        flat_e = topk_idx.reshape(-1)
        oh = jax.nn.one_hot(flat_e, E, dtype=jnp.int32)
        pos = jnp.take_along_axis(jnp.cumsum(oh, axis=0), flat_e[:, None], axis=1)[:, 0] - 1
        valid = pos < CAP
        pos_c = jnp.where(valid, pos, CAP - 1)
        token_ids = jnp.repeat(jnp.arange(N), TOPK)
        x_disp = jnp.zeros((E, CAP, C), x.dtype).at[flat_e, pos].set(x_flat[token_ids], mode='drop')
        up = jnp.einsum('ecd,edh->ech', x_disp, w_up)
        g_r, v_r = jnp.split(up, 2, axis=-1)
        h_r = jax.nn.silu(g_r) * v_r
        out_r = jnp.einsum('ech,ehd->ecd', h_r, w_down)
        y_ts = out_r[flat_e, pos_c]
        y_ts = jnp.where(valid[:, None], y_ts, 0.0)
        routed = (y_ts.reshape(N, TOPK, C) * w[:, :, None]).sum(axis=1)
        return (shared + routed).reshape(B, T, C)
    x = x + jnp.tanh(g_xattn[0]) * _L0_xattn_ref(_layernorm(x, axis=-1), L0_xattn_k, fside_S2_0, ctx_2048, ctx_2048, 8)
    x = x + jnp.tanh(g_ffn[0]) * _L0_ffn_ref(_layernorm(x, axis=-1), L0_ffn_gate_w, L0_ffn_shared_gate_w, L0_ffn_shared_gate_up_w, L0_ffn_shared_down_w, L0_ffn_w13, L0_ffn_w2)
    x = x + jnp.tanh(g_xattn[1]) * _L1_xattn_ref(_layernorm(x, axis=-1), mask_Bx1xSxS_fk0, ctx_2048, L1_xattn_Wq, L1_xattn_Wk, L1_xattn_Wv, L1_xattn_Wo, L1_xattn_gate)
    x = x + jnp.tanh(g_ffn[1]) * _L1_ffn_ref(_layernorm(x, axis=-1), L1_ffn_w_gate, L1_ffn_w_shared_up, L1_ffn_w_shared_down, L1_ffn_w_up, L1_ffn_w_down)
    return x

_drawn_inputs = setup_inputs


def setup_inputs(seed=0):
    import zlib

    import numpy as np

    out = dict(_drawn_inputs(seed))
    spreads = {'g_ffn': (-1.0, 0.6)}
    factors = {'L0_ffn_gate_w': 8.0,
     'L0_ffn_shared_gate_w': 8.0,
     'L0_ffn_shared_gate_up_w': 8.0,
     'L0_ffn_shared_down_w': 8.0,
     'L0_ffn_w13': 8.0,
     'L0_ffn_w2': 8.0,
     'L1_xattn_Wq': 8.0,
     'L1_xattn_Wk': 8.0,
     'L1_xattn_Wv': 4.247,
     'L1_xattn_Wo': 4.242,
     'L1_xattn_gate': 8.0,
     'L1_ffn_w_gate': 29.182,
     'L1_ffn_w_shared_up': 8.0,
     'L1_ffn_w_shared_down': 8.0,
     'L1_ffn_w_up': 27.696,
     'L1_ffn_w_down': 27.831}
    for name, (base, spread) in spreads.items():
        noise = np.random.default_rng([zlib.crc32(name.encode()), seed]).standard_normal(out[name].shape)
        drawn = base * np.exp(spread * noise) if base else spread * noise
        out[name] = jnp.asarray(drawn.astype(out[name].dtype))
    for name, factor in factors.items():
        out[name] = (out[name] * factor).astype(out[name].dtype)
    return out
```

```python
from contextlib import ExitStack

import numpy as np

import concourse.bass as bass
from concourse import mybir

ALU = mybir.AluOpType
ACT = mybir.ActivationFunctionType
AX_X = mybir.AxisListType.X
F32 = mybir.dt.float32
F32R = mybir.dt.float32r
BF16 = mybir.dt.bfloat16

P = 128
FIRST = 0
NSEQ = 8
TOK = 128
C = 256
KC = C // P
EPS = 1e-5

GROUPS = 16
GI = TOK // GROUPS

HIDDEN = 2112
UPW = 2 * HIDDEN
KT = -(-HIDDEN // P)
KLAST = HIDDEN - (KT - 1) * P
TGROUPS = [(g, min(4, KT - g)) for g in range(0, KT, 4)]
NTG = len(TGROUPS)
E0, I0, SHARED0 = 8, 176, 704
E1, I1, SHARED1 = 64, 32, 64
TOP0, TOP1, CAP = 2, 6, 128
ROUTE0 = E0 + 2
ROUTE1 = E1
WCOLS = KC * UPW + KT * C + KC * ROUTE1
DOWN_AT = KC * UPW
ROUTE_AT = DOWN_AT + KT * C
WCHUNK = WCOLS // 16

HEADS = 32
HD = C // HEADS
QUADS = HEADS // 4
ATTNW = 4 * C


class Steps:

    def __init__(self, eng, sem, base):
        self.eng, self.sem, self.base, self.n = eng, sem, base, 0

    def mark(self, ins):
        ins.then_inc(self.sem, 1)
        self.n += 1

    def wait(self):
        self.eng.wait_ge(self.sem, self.base + self.n)


def settled(eng, passed):
    eng.sem_inc(passed, 1)


def split3(pe, out, hi, lo, w_hi, w_lo, first, last):
    pe.matmul(out, hi, w_hi, start=first, stop=False)
    pe.matmul(out, hi, w_lo, start=False, stop=False)
    return pe.matmul(out, lo, w_hi, start=False, stop=last)


def program(nc, x, ctx_t, toep, bias, gates, head_gate, mask_q, mask_k, w_ffn0, w_attn, w_ffn1,
            ident_d, before_d, rope_d, out):
    with ExitStack() as ctx:
        def sem(name):
            return ctx.enter_context(nc.semaphore(name))

        def sb_in(scope):
            return lambda name, shape, dt=F32: scope.enter_context(nc.sbuf_tensor(name, shape, dt))

        sb = sb_in(ctx)
        ps = ctx.enter_context(nc.psum_tensor("ps", [P, 8, 512], F32))

        X = sb("residual", [P, NSEQ, C])
        CTXT = sb("ctx_t", [P, KC, NSEQ, TOK])
        ident = sb("ident", [P, P])
        ident_r = sb("ident_r", [P, P], F32R)
        before_f = sb("before_f", [P, P])
        before = sb("before", [P, P], BF16)
        ones_bf = sb("ones_bf", [P, P], BF16)
        rope = sb("rope", [P, 2, 2, HD])
        G = sb("gates", [P, 4])
        TG = sb("tanh_gates", [P, 4])
        HG = sb("head_gate", [P, HEADS])
        THG = sb("tanh_head_gate", [P, HEADS])
        mask_q_sb = sb("mask_q", [P, NSEQ, TOK])
        mask_raw = sb("mask_raw", [P, NSEQ, TOK])
        mask_hi = sb("mask_hi", [P, NSEQ, TOK], F32R)
        mask_lo = sb("mask_lo", [P, NSEQ, TOK], F32R)
        w_hi = sb("w_hi", [P, WCOLS], F32R)
        w_lo = sb("w_lo", [P, WCOLS], F32R)
        wa_hi = sb("wa_hi", [P, KC, ATTNW], F32R)
        wa_lo = sb("wa_lo", [P, KC, ATTNW], F32R)
        raw = sb("raw_weights", [P, 2, ATTNW])
        mhalf = sb("minus_half", [P, NSEQ])
        stats = sb("stats", [P, NSEQ, 6])
        mv = sb("mean_var", [P, NSEQ, 2])
        veps = sb("var_eps", [P, NSEQ])
        rstd = sb("rstd", [P, NSEQ])

        with ExitStack() as scope:
            sa = sb_in(scope)
            xn_u = sa("xn_then_skip", [P, NSEQ * C])
            XN = xn_u[:].rearrange("p (b c) -> p b c", b=NSEQ)
            U = xn_u[:].rearrange("p (k b s) -> p k b s", k=KC, b=NSEQ)
            VT = sa("v_t", [P, KC, NSEQ, TOK])
            R = sa("mixed_t", [P, KC, NSEQ, TOK])
            T = sa("toeplitz", [P, 2, C])
            KV = sa("kv", [P, 2, KC, 512])
            Z = sa("z", [P, 2, KC, 512])
            SK = sa("skip_sum", [P, KC * NSEQ * GROUPS])
            bias_b = sa("bias_b", [P, TOK])

        with ExitStack() as scope:
            sf = sb_in(scope)
            xn_f = sf("xn_f", [P, C])
            xt_hi = sf("xt_hi", [P, KC, TOK], F32R)
            xt_lo = sf("xt_lo", [P, KC, TOK], F32R)
            SG = sf("silu_gate", [P, 4, 256])
            HID = sf("hidden", [P, HIDDEN])
            ht_hi = sf("hidden_t_hi", [P, KT, TOK], F32R)
            ht_lo = sf("hidden_t_lo", [P, KT, TOK], F32R)
            top8 = sf("top8", [P, 8])
            sel8 = sf("select8", [P, 8])
            neg_max = sf("neg_max", [P, 1])
            ex = sf("exps", [P, E1 + 2])
            ex_sum = sf("exp_sum", [P, 1])
            prob = sf("prob", [P, E1 + 8])
            marked = sf("marked", [P, E1 + 8])
            W = sf("route_w", [P, E1])
            WV = sf("route_w_valid", [P, E1])
            tmp1 = sf("tmp1", [P, E1])
            chosen = sf("chosen", [P, E1], BF16)
            earlier = sf("earlier", [P, E1], BF16)

        with ExitStack() as scope:
            sc = sb_in(scope)
            xn_a = sc("xn_a", [P, C])
            xa_hi = sc("xa_hi", [P, KC, TOK], F32R)
            xa_lo = sc("xa_lo", [P, KC, TOK], F32R)
            ca_hi = sc("ca_hi", [P, KC, TOK], F32R)
            ca_lo = sc("ca_lo", [P, KC, TOK], F32R)
            T1 = sc("rope_cos", [P, 2, HEADS, HD])
            T2 = sc("rope_sin", [P, 2, HEADS, HD])
            RQ = sc("roped", [P, 2, HEADS, HD])
            QS = sc("q_stack", [P, HEADS, 32])
            KS = sc("k_stack", [P, HEADS, 32])
            AS = sc("a_stack", [P, HEADS, 32])
            KAT = sc("ka_t", [P, QUADS, 2, TOK], F32R)
            QT1 = sc("q_t", [P, QUADS, TOK], F32R)
            QT2 = sc("q_max_t", [P, QUADS, TOK], F32R)
            V9 = sc("v_ones", [P, 2, HEADS, HD + 1])
            junk = sc("junk", [P, 4, TOK], BF16)
            mask_now = sc("mask_now", [P, TOK])
            MX = sc("row_max", [P, 2, HEADS])
            PR = sc("probs", [P, 4, 4, TOK])
            den = sc("den", [P, 2, HEADS])
            O1 = sc("o1", [P, HEADS, HD])
            O2 = sc("o2", [P, HEADS, HD])
            ON = sc("o_norm", [P, C])
            ot_hi = sc("ot_hi", [P, KC, TOK], F32R)
            ot_lo = sc("ot_lo", [P, KC, TOK], F32R)

        in_x = [sem("in_x0"), sem("in_x1")]
        in_ctx, in_const, in_late = sem("in_ctx"), sem("in_const"), sem("in_late")
        in_toep = [sem("in_toep0"), sem("in_toep1")]
        in_raw = [sem("in_raw0"), sem("in_raw1")]
        chunk_hi, chunk_lo, later_lo = sem("chunk_hi"), sem("chunk_lo"), sem("later_lo")
        consts = sem("consts")
        passed = sem("passed")
        gates_ready = sem("gates_ready")
        out_stored = sem("out_stored")
        a_steps, a_var, a_rstd, a_xn = sem("a_steps"), sem("a_var"), sem("a_rstd"), sem("a_xn")
        a_xt, a_vt = sem("a_xt"), sem("a_vt")
        a_kv, a_y, a_zread, a_red = sem("a_kv"), sem("a_y"), sem("a_zread"), sem("a_red")
        a_skip, a_u, a_rt, a_res = sem("a_skip"), sem("a_u"), sem("a_rt"), sem("a_res")
        a_rsum = sem("a_rsum")

        def split_hi(act, slot, landed, dst, width):
            act.wait_ge(in_raw[slot], 16 * landed)
            act.copy(dst, raw[:, slot, 0:width]).then_inc(chunk_hi, 1)

        def split_lo(eng, slot, n1, dst, hi, width, done):
            eng.wait_ge(chunk_hi, n1)
            eng.tensor_tensor(dst, raw[:, slot, 0:width], hi.bitcast(F32), ALU.subtract).then_inc(done, 1)

        def mixer_sync(sp):
            sp.dma_start(X[:, 0:4, :], x[0:4].rearrange("b s c -> s b c")).then_inc(in_x[0], 16)
            sp.dma_start(X[:, 4:8, :], x[4:8].rearrange("b s c -> s b c")).then_inc(in_x[1], 16)
            sp.dma_start(ident[:], ident_d).then_inc(in_const, 16)
            sp.dma_start(CTXT[:], ctx_t.rearrange("p (k b s) -> p k b s", k=KC, b=NSEQ)).then_inc(in_ctx, 16)
            sp.dma_start(bias_b[:], bias.partition_broadcast(P)).then_inc(in_const, 16)
            sp.dma_start(G[:], gates.partition_broadcast(P)).then_inc(in_const, 16)
            sp.dma_start(HG[:], head_gate.partition_broadcast(P)).then_inc(in_const, 16)
            sp.dma_start(rope[:], rope_d.rearrange("p (a b d) -> p a b d", a=2, b=2)).then_inc(in_const, 16)
            sp.dma_start(before_f[:], before_d).then_inc(in_const, 16)
            with sp.Fori(0, GROUPS // 2) as i:
                for par in range(2):
                    h = 2 * i + par
                    sp.wait_ge(a_y, h + 1)
                    sp.dma_start(T[:, par, :], toep[h]).then_inc(in_toep[par], 16)
                    sp.wait_ge(chunk_lo, h + 1)
                    sp.dma_start(raw[:, par, 0:WCHUNK], w_ffn0[h]).then_inc(in_raw[par], 16)
            sp.dma_start(mask_q_sb[:], mask_q.rearrange("b q k -> q b k")).then_inc(in_late, 16)
            sp.dma_start(mask_raw[:], mask_k.rearrange("b k q -> k b q")).then_inc(in_late, 16)
            for par in range(2):
                sp.wait_ge(chunk_lo, GROUPS + par + 1)
                sp.dma_start(raw[:, par, :], w_attn[par]).then_inc(in_raw[par], 16)

        def mixer_scalar(act):
            act.wait_ge(in_const, 16 * 6)
            act.activation(TG[:], G[:], ACT.Tanh).then_inc(gates_ready, 1)
            act.activation(THG[:], HG[:], ACT.Tanh).then_inc(gates_ready, 1)
            for n in range(4):
                act.wait_ge(a_xt, n + 1)
                act.copy(VT[:, :, 2 * n:2 * n + 2, :],
                         ps[:, n, :].rearrange("p (k b s) -> p k b s", k=KC, b=2)).then_inc(a_vt, 1)
            with act.Fori(0, GROUPS // 2) as i:
                for par in range(2):
                    h = 2 * i + par
                    split_hi(act, par, i + 1, w_hi[:, bass.ds(h * WCHUNK, WCHUNK)], WCHUNK)

        def mixer_gpsimd(pool):
            pool.wait_ge(a_var, 1)
            pool.tensor_tensor(rstd[:], veps[:], mhalf[:], ALU.pow).then_inc(a_rstd, 1)
            pool.wait_ge(a_vt, 4)
            pool.wait_ge(in_ctx, 16)
            with pool.Fori(0, GROUPS // 2) as i:
                for par in range(2):
                    h = 2 * i + par
                    pool.wait_ge(a_y, h + 1)
                    for mb in range(KC):
                        v = VT[:, mb, :, bass.ds(h * GI, GI)].unsqueeze(3).to_broadcast([P, NSEQ, GI, GI])
                        k = CTXT[:, mb, :, bass.ds(h * GI, GI)].unsqueeze(2).to_broadcast([P, NSEQ, GI, GI])
                        pool.tensor_tensor(
                            KV[:, par, mb, :].rearrange("p (b i j) -> p b i j", b=NSEQ, i=GI), v, k, ALU.mult,
                        ).then_inc(a_kv, 1)
            pool.wait_ge(a_skip, 1)
            pool.tensor_tensor(
                U[:].rearrange("p k b (h j) -> p (k b h) j", j=GI),
                CTXT[:].rearrange("p k b (h j) -> p (k b h) j", j=GI),
                SK[:].unsqueeze(2).to_broadcast([P, KC * NSEQ * GROUPS, GI]), ALU.mult).then_inc(a_u, 1)

        def mixer_tensor(pe):
            pe.sem_inc(a_y, 2)
            pe.sem_inc(a_zread, 2)
            pe.wait_ge(in_const, 16 * 6)
            pe.wait_ge(a_xn, 1)
            for n in range(4):
                for kb in range(KC):
                    for b2 in range(2):
                        at = (kb * 2 + b2) * TOK
                        mm = pe.transpose(ps[:, n, at:at + TOK], XN[:, 2 * n + b2, kb * P:(kb + 1) * P], ident[:])
                mm.then_inc(a_xt, 1)
            with pe.Fori(0, GROUPS // 2) as i:
                for par in range(2):
                    h = 2 * i + par
                    y0, y1 = ps[:, 4 + 2 * par, :], ps[:, 5 + 2 * par, :]
                    pe.wait_ge(in_toep[par], 16 * i + 16)
                    pe.wait_ge(a_kv, 2 * h + 2)
                    pe.wait_ge(a_zread, h + 1)
                    pe.matmul(y0, T[:, par, 0:P], KV[:, par, 0, :], start=True, stop=True)
                    pe.matmul(y1, T[:, par, P:C], KV[:, par, 0, :], start=True, stop=False)
                    pe.matmul(y1, T[:, par, 0:P], KV[:, par, 1, :], start=False, stop=True).then_inc(a_y, 1)
            pe.wait_ge(a_rsum, KC)
            for n in range(4):
                for b2 in range(2):
                    for lb in range(KC):
                        at = b2 * C + lb * P
                        mm = pe.transpose(ps[:, n, at:at + P], R[:, lb, 2 * n + b2, :], ident[:])
                mm.then_inc(a_rt, 1)

        def mixer_vector(dve):
            st = Steps(dve, a_steps, 0)
            dve.sem_inc(chunk_lo, 2)
            dve.memset(mhalf[:], -0.5).then_inc(consts, 1)
            dve.memset(ones_bf[:], 1.0).then_inc(consts, 1)
            for b in range(NSEQ):
                dve.wait_ge(in_x[b // 4], 16)
                st.mark(dve.bn_stats(stats[:, b, :], X[:, b, :]))
            for b in range(NSEQ):
                dve.wait_ge(a_steps, b + 1)
                st.mark(dve.bn_aggr(mv[:, b, :], stats[:, b, :]))
            st.wait()
            dve.tensor_scalar(veps[:], mv[:, :, 1], EPS, None, ALU.add).then_inc(a_var, 1)
            dve.wait_ge(a_rstd, 1)
            for b in range(NSEQ):
                ins = dve.tensor_scalar(XN[:, b, :], X[:, b, :], mv[:, b, 0:1], rstd[:, b:b + 1],
                                        ALU.subtract, ALU.mult)
            ins.then_inc(a_xn, 1)
            dve.wait_ge(in_const, 16 * 6)
            dve.tensor_copy(ident_r[:], ident[:]).then_inc(consts, 1)
            dve.tensor_copy(before[:], before_f[:]).then_inc(consts, 1)
            dve.wait_ge(a_vt, 4)
            dve.wait_ge(in_ctx, 16)
            st.mark(dve.tensor_tensor(U[:], VT[:], CTXT[:], ALU.mult))
            st.wait()
            flat = "p k b s -> p (k b) s"
            st.mark(dve.tensor_tensor(U[:].rearrange(flat), U[:].rearrange(flat),
                                      bias_b[:].unsqueeze(1).to_broadcast([P, KC * NSEQ, TOK]), ALU.mult))
            st.wait()
            dve.tensor_reduce(SK[:], U[:].rearrange("p k b (h j) -> p (k b h) j", j=GI), AX_X, ALU.add
                              ).then_inc(a_skip, 1)
            with dve.Fori(0, GROUPS // 2) as i:
                for par in range(2):
                    h = 2 * i + par
                    dve.wait_ge(a_y, 2 + h + 1)
                    for lb in range(KC):
                        x1 = CTXT[:, lb, :, bass.ds(h * GI, GI)].unsqueeze(3).to_broadcast([P, NSEQ, GI, GI])
                        four = "p (b i j) -> p b i j"
                        ins = dve.tensor_tensor(
                            Z[:, par, lb, :].rearrange(four, b=NSEQ, i=GI),
                            ps[:, 4 + 2 * par + lb, :].rearrange(four, b=NSEQ, i=GI), x1, ALU.mult)
                    ins.then_inc(a_zread, 1)
                    split_lo(dve, par, h + 1, w_lo[:, bass.ds(h * WCHUNK, WCHUNK)],
                             w_hi[:, bass.ds(h * WCHUNK, WCHUNK)], WCHUNK, chunk_lo)
                    dve.wait_ge(a_zread, 2 + h + 1)
                    for lb in range(KC):
                        dve.tensor_reduce(R[:, lb, :, bass.ds(h * GI, GI)],
                                          Z[:, par, lb, :].rearrange("p (b i j) -> p b j i", b=NSEQ, i=GI),
                                          AX_X, ALU.add).then_inc(a_red, 1)
            dve.wait_ge(a_u, 1)
            dve.wait_ge(a_red, 2 * GROUPS)
            for lb in range(KC):
                dve.tensor_tensor(R[:, lb], R[:, lb], U[:, lb], ALU.add).then_inc(a_rsum, 1)
            dve.wait_ge(gates_ready, 2)
            for n in range(4):
                dve.wait_ge(a_rt, n + 1)
                xs = X[:, 2 * n:2 * n + 2, :].rearrange("p b c -> p (b c)")
                dve.scalar_tensor_tensor(xs, ps[:, n, :], TG[:, 0:1], xs, ALU.mult, ALU.add).then_inc(a_res, 1)

        class Norm:
            STEPS = 2

            def __init__(self, tag, xn):
                self.steps, self.var, self.rstd, self.xn_ready = (
                    sem(f"{tag}_norm_steps"), sem(f"{tag}_var"), sem(f"{tag}_rstd"), sem(f"{tag}_xn"))
                self.xn = xn

            def vector(self, dve, b, xn_free):
                st = Steps(dve, self.steps, b * self.STEPS)
                st.mark(dve.bn_stats(stats[:, 0, :], X[:, b, :]))
                st.wait()
                settled(dve, passed)
                st.mark(dve.bn_aggr(mv[:, 0, :], stats[:, 0, :]))
                st.wait()
                dve.tensor_scalar(veps[:, 0:1], mv[:, 0, 1:2], EPS, None, ALU.add).then_inc(self.var, 1)
                dve.wait_ge(self.rstd, b + 1)
                xn_free()
                dve.tensor_scalar(self.xn[:], X[:, b, :], mv[:, 0, 0:1], rstd[:, 0:1],
                                  ALU.subtract, ALU.mult).then_inc(self.xn_ready, 1)

            def gpsimd(self, pool, b):
                pool.wait_ge(self.var, b + 1)
                pool.tensor_tensor(rstd[:, 0:1], veps[:, 0:1], mhalf[:, 0:1], ALU.pow).then_inc(self.rstd, 1)

        class Ffn:
            def __init__(self, layer):
                tag = f"f{layer}"
                self.layer = layer
                self.norm = Norm(tag, xn_f)
                self.xt, self.xh, self.xl = sem(f"{tag}_xt"), sem(f"{tag}_xh"), sem(f"{tag}_xl")
                self.logit, self.neg, self.exps = sem(f"{tag}_logit"), sem(f"{tag}_neg"), sem(f"{tag}_exps")
                self.w_ready, self.chosen, self.pos = sem(f"{tag}_w_ready"), sem(f"{tag}_chosen"), sem(f"{tag}_pos")
                self.valid, self.up, self.used = sem(f"{tag}_valid"), sem(f"{tag}_up"), sem(f"{tag}_used")
                self.silu, self.weighted, self.ht = sem(f"{tag}_silu"), sem(f"{tag}_weighted"), sem(f"{tag}_ht")
                self.hh, self.hl, self.down = sem(f"{tag}_hh"), sem(f"{tag}_hl"), sem(f"{tag}_down")
                self.res, self.rsteps, self.pread = sem(f"{tag}_res"), sem(f"{tag}_rsteps"), sem(f"{tag}_pread")
                if layer == 0:
                    self.units = [(2 * I0 * n, 2 * I0, I0 * n, I0) for n in range(12)]
                    self.need = [3, 6, 9, 12, 12]
                    self.order = ["u0", "u1", "u2", "u3", "u4", "T0", "u5", "u6", "u7", "T1", "u8", "D0", "u9",
                                  "u10", "T2", "u11", "D1", "X", "D2", "T3", "T4", "R", "D3", "D4"]
                    self.tg = 1
                    self.nroute = ROUTE0
                else:
                    self.units = [(512 * n, 512, 256 * n, 256) for n in range(8)] + [(4096, 128, 2048, 64)]
                    self.need = [2, 4, 6, 8, 9]
                    self.order = ["u0", "u1", "P", "u2", "u3", "T0", "u4", "u5", "T1", "D0", "u6", "u7", "T2", "D1",
                                  "u8", "X", "D2", "T3", "T4", "R", "D3", "D4"]
                    self.tg = 3
                    self.nroute = ROUTE1
                self.nu = len(self.units)

            def x_tensor(self, pe, b):
                pe.wait_ge(self.norm.xn_ready, b + 1)
                if b is not FIRST:
                    pe.wait_ge(self.w_ready, b)
                    if self.layer == 1:
                        pe.wait_ge(self.valid, b)
                for kb in range(KC):
                    mm = pe.transpose(ps[:, 7, kb * P:(kb + 1) * P], xn_f[:, kb * P:(kb + 1) * P], ident[:])
                mm.then_inc(self.xt, 1)

            def x_scalar(self, act, b):
                act.wait_ge(self.xt, b + 1)
                act.copy(xt_hi[:].rearrange("p k s -> p (k s)"), ps[:, 7, 0:C]).then_inc(self.xh, 1)

            def x_vector(self, dve, b):
                dve.wait_ge(self.xh, b + 1)
                dve.tensor_tensor(xt_lo[:].rearrange("p k s -> p (k s)"), ps[:, 7, 0:C],
                                  xt_hi[:].rearrange("p k s -> p (k s)").bitcast(F32), ALU.subtract
                                  ).then_inc(self.xl, 1)

            def r_tensor(self, pe, b):
                pe.wait_ge(self.xl, b + 1)
                for kc in range(KC):
                    at = ROUTE_AT + kc * self.nroute
                    mm = split3(pe, ps[:, 7, C:C + self.nroute], xt_hi[:, kc, :], xt_lo[:, kc, :],
                                w_hi[:, at:at + self.nroute], w_lo[:, at:at + self.nroute], kc == 0, kc == KC - 1)
                mm.then_inc(self.logit, 1)

            def r_scalar(self, act, b):
                if self.layer == 0:
                    act.wait_ge(self.neg, b + 1)
                    act.activation(ex[:, 0:E0], ps[:, 7, C:C + E0], ACT.Exp, bias=neg_max[:, 0:1],
                                   accum_out=ex_sum[:]).then_inc(self.exps, 1)
                    act.activation(ex[:, E0:E0 + 1], ps[:, 7, C + E0:C + E0 + 1], ACT.Exp, scale=-1.0
                                   ).then_inc(self.exps, 1)
                else:
                    act.wait_ge(self.logit, b + 1)
                    act.activation(ex[:, 0:E1], ps[:, 7, C:C + E1], ACT.Exp, scale=-1.0).then_inc(self.exps, 1)

            RSTEPS = (7, 8)

            def r_vector(self, dve, b):
                n, top = ((E0, TOP0), (E1, TOP1))[self.layer]
                width = n + 8 - top
                st = Steps(dve, self.rsteps, b * self.RSTEPS[self.layer])
                if self.layer == 0:
                    dve.wait_ge(self.logit, b + 1)
                    settled(dve, passed)
                    st.mark(dve.max(top8[:], ps[:, 7, C:C + E0]))
                    st.wait()
                    dve.tensor_scalar(neg_max[:], top8[:, 0:1], -1.0, None, ALU.mult).then_inc(self.neg, 1)
                    dve.wait_ge(self.exps, 2 * b + 2)
                    st.mark(dve.reciprocal(tmp1[:, 0:1], ex_sum[:]))
                    st.mark(dve.tensor_scalar(tmp1[:, 1:2], ex[:, E0:E0 + 1], 1.0, None, ALU.add))
                    st.wait()
                    st.mark(dve.tensor_scalar(prob[:, 0:n], ex[:, 0:n], tmp1[:, 0:1], None, ALU.mult))
                else:
                    dve.wait_ge(self.exps, b + 1)
                    st.mark(dve.tensor_scalar(tmp1[:], ex[:, 0:n], 1.0, None, ALU.add))
                    st.wait()
                    st.mark(dve.reciprocal(prob[:, 0:n], tmp1[:]))
                st.wait()
                settled(dve, passed)
                st.mark(dve.max(top8[:], prob[:, 0:n]))
                st.wait()
                st.mark(dve.tensor_copy(sel8[:, 0:top], top8[:, 0:top]))
                st.wait()
                settled(dve, passed)
                st.mark(dve.match_replace(marked[:, 0:width], sel8[:], prob[:, 0:width], -3.0))
                st.wait()
                if self.layer == 0:
                    dve.reciprocal(W[:, n:n + 1], tmp1[:, 1:2]).then_inc(self.pread, 1)
                    dve.scalar_tensor_tensor(W[:, 0:n], marked[:, 0:n], -2.0, prob[:, 0:n],
                                             ALU.is_lt, ALU.mult).then_inc(self.w_ready, 1)
                else:
                    st.mark(dve.scalar_tensor_tensor(W[:], marked[:, 0:n], -2.0, prob[:, 0:n],
                                                     ALU.is_lt, ALU.mult))
                    st.wait()
                    st.mark(dve.reduce_sum(ex_sum[:], W[:], axis=AX_X))
                    st.wait()
                    st.mark(dve.reciprocal(tmp1[:, 0:1], ex_sum[:]))
                    st.wait()
                    dve.tensor_scalar(W[:], W[:], tmp1[:, 0:1], None, ALU.mult).then_inc(self.w_ready, 1)
                    dve.tensor_scalar(chosen[:], marked[:, 0:n], -2.0, None, ALU.is_lt).then_inc(self.chosen, 1)
                assert st.n == self.RSTEPS[self.layer], st.n

            def p_tensor(self, pe, b):
                pe.wait_ge(self.chosen, b + 1)
                pe.wait_ge(self.pread, b + 1)
                pe.matmul(ps[:, 7, 384:384 + E1], before[:], chosen[:], start=True, stop=False)
                pe.matmul(ps[:, 7, 384:384 + E1], ones_bf[:], earlier[:], start=False, stop=True
                          ).then_inc(self.pos, 1)

            def p_vector(self, dve, b):
                dve.wait_ge(self.pos, b + 1)
                dve.wait_ge(self.w_ready, b + 1)
                dve.wait_ge(self.weighted, 1 + 8 * b)
                dve.scalar_tensor_tensor(WV[:], ps[:, 7, 384:384 + E1], float(CAP), W[:],
                                         ALU.is_lt, ALU.mult).then_inc(self.valid, 1)
                dve.tensor_tensor(earlier[:], earlier[:], chosen[:], ALU.add).then_inc(self.pread, 1)

            def bank_turn(self, u):
                if u >= 4:
                    return self.nu + u - 4 + 1
                last = max(v for v in range(self.nu) if v % 4 == u)
                return last + 1

            def u_tensor(self, pe, b, u):
                c0, width, _, _ = self.units[u]
                pe.wait_ge(self.used, b * self.nu + self.bank_turn(u))
                for kc in range(KC):
                    at = kc * UPW + c0
                    mm = split3(pe, ps[:, u % 4, 0:width], xt_hi[:, kc, :], xt_lo[:, kc, :],
                                w_hi[:, at:at + width], w_lo[:, at:at + width], kc == 0, kc == KC - 1)
                mm.then_inc(self.up, 1)

            def parts(self, u):
                bank = ps[:, u % 4, :]
                if self.layer == 0:
                    return bank[:, 0:I0], bank[:, I0:2 * I0]
                if u == 8:
                    return bank[:, SHARED1:2 * SHARED1], bank[:, 0:SHARED1]
                both = bank.rearrange("p (e t d) -> p e t d", e=8, t=2)
                return both[:, :, 0, :], both[:, :, 1, :]

            def silu_of(self, u):
                hw = self.units[u][3]
                s = SG[:, u % 4, 0:hw]
                return s.rearrange("p (e d) -> p e d", e=8) if self.layer == 1 and u < 8 else s

            def hid_of(self, u):
                _, _, h0, hw = self.units[u]
                s = HID[:, h0:h0 + hw]
                return s.rearrange("p (e d) -> p e d", e=8) if self.layer == 1 and u < 8 else s

            def u_scalar(self, act, b, u):
                act.wait_ge(self.up, b * self.nu + u + 1)
                act.activation(self.silu_of(u), self.parts(u)[0], ACT.Silu).then_inc(self.silu, 1)

            def u_vector(self, dve, b, u):
                if u == 0:
                    dve.wait_ge(self.ht, 1 + NTG * b)
                    if self.layer == 0:
                        dve.wait_ge(self.w_ready, b + 1)
                        dve.wait_ge(self.pread, b + 1)
                dve.wait_ge(self.silu, b * self.nu + u + 1)
                if self.layer == 0:
                    e = E0 if u < 4 else u - 4
                    dve.scalar_tensor_tensor(self.hid_of(u), self.silu_of(u), W[:, e:e + 1], self.parts(u)[1],
                                             ALU.mult, ALU.mult).then_inc(self.used, 1)
                else:
                    dve.tensor_tensor(self.hid_of(u), self.silu_of(u), self.parts(u)[1], ALU.mult
                                      ).then_inc(self.used, 1)

            def u_gpsimd(self, pool, b, u):
                if u == 0:
                    pool.wait_ge(self.valid, b + 1)
                pool.wait_ge(self.used, self.nu * (b + 1) + u + 1)
                h = self.hid_of(u)
                pool.tensor_tensor(h, h, WV[:, 8 * u:8 * u + 8].unsqueeze(2).to_broadcast([P, 8, I1]), ALU.mult
                                   ).then_inc(self.weighted, 1)

            def ht_turn(self, g):
                if g >= 2:
                    return NTG + g - 2 + 1
                return max(v for v in range(NTG) if v % 2 == g) + 1

            def t_tensor(self, pe, b, g):
                if self.layer == 1 and g < 4:
                    pe.wait_ge(self.weighted, 1 + 8 * b + self.need[g])
                else:
                    pe.wait_ge(self.used, self.nu * (b + 1) + self.need[g])
                pe.wait_ge(self.hl, NTG * b + self.ht_turn(g))
                k0, nk = TGROUPS[g]
                settled(pe, passed)
                for j in range(nk):
                    w = P if k0 + j < KT - 1 else KLAST
                    mm = pe.transpose(ps[0:w, 4 + g % 2, j * P:(j + 1) * P],
                                      HID[:, (k0 + j) * P:(k0 + j) * P + w], ident[:])
                mm.then_inc(self.ht, 1)

            def ht_parts(self, g):
                k0, nk = TGROUPS[g]
                w = P if k0 + nk < KT else KLAST
                flat = "p k s -> p (k s)"
                return (ps[0:w, 4 + g % 2, 0:nk * P], ht_hi[0:w, k0:k0 + nk, :].rearrange(flat),
                        ht_lo[0:w, k0:k0 + nk, :].rearrange(flat))

            def t_scalar(self, act, b, g):
                act.wait_ge(self.ht, 1 + NTG * b + g + 1)
                act.wait_ge(self.down, 1 + b)
                src, hi, _ = self.ht_parts(g)
                act.copy(hi, src).then_inc(self.hh, 1)

            def t_vector(self, dve, b, g):
                dve.wait_ge(self.hh, NTG * b + g + 1)
                src, hi, lo = self.ht_parts(g)
                dve.tensor_tensor(lo, src, hi.bitcast(F32), ALU.subtract).then_inc(self.hl, 1)

            def d_tensor(self, pe, b, g):
                pe.wait_ge(self.hl, NTG * (b + 1) + g + 1)
                if g == 0:
                    pe.wait_ge(self.res, 1 + b)
                k0, nk = TGROUPS[g]
                for k in range(k0, k0 + nk):
                    w = P if k < KT - 1 else KLAST
                    at = DOWN_AT + k * C
                    mm = split3(pe, ps[:, 6, 0:C], ht_hi[0:w, k, :], ht_lo[0:w, k, :],
                                w_hi[0:w, at:at + C], w_lo[0:w, at:at + C], k == 0, k == KT - 1)
                if g == NTG - 1:
                    mm.then_inc(self.down, 1)

            def res_vector(self, dve, b):
                dve.wait_ge(self.down, 1 + b + 1)
                dve.scalar_tensor_tensor(X[:, b, :], ps[:, 6, 0:C], TG[:, self.tg:self.tg + 1], X[:, b, :],
                                         ALU.mult, ALU.add).then_inc(self.res, 1)

            def tensor(self, pe):
                pe.sem_inc(self.used, self.nu)
                pe.sem_inc(self.hl, NTG)
                for s in (self.ht, self.down, self.res, self.weighted):
                    pe.sem_inc(s, 1)
                if self.layer == 0:
                    pe.wait_ge(chunk_lo, 2 + GROUPS)
                else:
                    pe.wait_ge(later_lo, 2 + GROUPS)
                self.x_tensor(pe, FIRST)
                self.r_tensor(pe, 0)

                def body(b, last):
                    for what in self.order:
                        kind, n = what[0], int(what[1:] or 0)
                        if kind == "u":
                            self.u_tensor(pe, b, n)
                        elif kind == "T":
                            self.t_tensor(pe, b, n)
                        elif kind == "D":
                            self.d_tensor(pe, b, n)
                        elif kind == "P":
                            self.p_tensor(pe, b)
                        elif kind == "X" and not last:
                            self.x_tensor(pe, b + 1)
                        elif kind == "R" and not last:
                            self.r_tensor(pe, b + 1)

                with pe.Fori(0, NSEQ - 1) as b:
                    body(b, False)
                body(NSEQ - 1, True)

            def scalar(self, act):
                self.x_scalar(act, 0)
                self.r_scalar(act, 0)

                def body(b, last):
                    for what in self.order:
                        kind, n = what[0], int(what[1:] or 0)
                        if kind == "u":
                            self.u_scalar(act, b, n)
                        elif kind == "T":
                            self.t_scalar(act, b, n)
                        elif kind == "X" and not last:
                            self.x_scalar(act, b + 1)
                        elif kind == "R" and not last:
                            self.r_scalar(act, b + 1)

                with act.Fori(0, NSEQ - 1) as b:
                    body(b, False)
                body(NSEQ - 1, True)

            def vector(self, dve):
                n, top = ((E0, TOP0), (E1, TOP1))[self.layer]
                dve.memset(prob[:, n:n + 8], -1.0).then_inc(consts, 1)
                dve.memset(sel8[:], -1.0).then_inc(consts, 1)
                if self.layer == 1:
                    dve.memset(earlier[:], 0.0).then_inc(self.pread, 1)
                dve.wait_ge(consts, 6 if self.layer == 0 else 8)
                self.norm.vector(dve, 0, lambda: None)
                self.x_vector(dve, 0)
                self.r_vector(dve, 0)

                def body(b, last):
                    for what in self.order:
                        kind, n = what[0], int(what[1:] or 0)
                        if kind == "u":
                            self.u_vector(dve, b, n)
                            if n == 2 and not last:
                                self.norm.vector(dve, b + 1, lambda: dve.wait_ge(self.xt, b + 1))
                        elif kind == "T":
                            self.t_vector(dve, b, n)
                        elif kind == "P":
                            self.p_vector(dve, b)
                        elif kind == "X" and not last:
                            self.x_vector(dve, b + 1)
                        elif kind == "R" and not last:
                            self.r_vector(dve, b + 1)
                    self.res_vector(dve, b)

                with dve.Fori(0, NSEQ - 1) as b:
                    body(b, False)
                body(NSEQ - 1, True)

            def gpsimd(self, pool):
                self.norm.gpsimd(pool, 0)

                def body(b, last):
                    if self.layer == 1:
                        for u in range(8):
                            self.u_gpsimd(pool, b, u)
                            if u == 2 and not last:
                                self.norm.gpsimd(pool, b + 1)
                    elif not last:
                        self.norm.gpsimd(pool, b + 1)

                with pool.Fori(0, NSEQ - 1) as b:
                    body(b, False)
                body(NSEQ - 1, True)

        class Attention:
            FX, FQK, FV, FA, FAT, FKT, FQT, FQM, FO, FWO = 0, 1, 2, 3, 4, 6, 8, 10, 12, 13
            FILLS = 14

            def __init__(self):
                self.norm = Norm("at", xn_a)
                self.mdone = sem("at_fill")
                self.mread = [sem("at_read6"), sem("at_read7")]
                self.xh, self.ch, self.cl = sem("at_xh"), sem("at_ch"), sem("at_cl")
                self.roped, self.rsteps = sem("at_roped"), sem("at_rope_steps")
                self.akh, self.qkh, self.qkl = sem("at_akh"), sem("at_qkh"), sem("at_qkl")
                self.sq, self.sqread = sem("at_sq"), sem("at_sqread")
                self.maxed, self.msteps = sem("at_maxed"), sem("at_max_steps")
                self.sk, self.skread, self.pv = sem("at_sk"), sem("at_exp"), sem("at_pv")
                self.onorm, self.osteps, self.oh = sem("at_onorm"), sem("at_o_steps"), sem("at_oh")
                self.setup, self.mask_ready = sem("at_setup"), sem("at_mask")

            def fill_ready(self, pe, b, f):
                pe.wait_ge(self.mread[f % 2], 1 + b * (self.FILLS // 2) + f // 2)
                return ps[:, 6 + f % 2, :]

            def filled(self, eng, b, f):
                eng.wait_ge(self.mdone, b * self.FILLS + f + 1)
                return ps[:, 6 + f % 2, :]

            def used_up(self, eng, b, f):
                eng.wait_ge(self.mread[f % 2], 1 + b * (self.FILLS // 2) + f // 2 + 1)

            @staticmethod
            def heads_of(k):
                return k % 4, 2 * (k // 4)

            def sync(self, sp):
                with sp.Fori(0, NSEQ) as b:
                    for par in range(2):
                        sp.wait_ge(later_lo, 2 * b + par + 1)
                        sp.dma_start(raw[:, par, 0:WCHUNK], w_ffn1[2 * b + par]).then_inc(in_raw[par], 16)

            def weights_scalar(self, act):
                for par in range(2):
                    split_hi(act, par, GROUPS // 2 + 1, wa_hi[:, par, :], ATTNW)

            def weights_gpsimd(self, pool):
                for par in range(2):
                    split_lo(pool, par, GROUPS + par + 1, wa_lo[:, par, :], wa_hi[:, par, :], ATTNW, later_lo)

            def next_weights(self, b, par):
                return bass.ds((2 * b + par) * WCHUNK, WCHUNK)

            def front_tensor(self, pe, b):
                bank = self.fill_ready(pe, b, self.FX)
                pe.wait_ge(self.norm.xn_ready, b + 1)
                for kb in range(KC):
                    mm = pe.transpose(bank[:, kb * P:(kb + 1) * P], xn_a[:, kb * P:(kb + 1) * P], ident[:])
                mm.then_inc(self.mdone, 1)
                self.used_up(pe, b, self.FX)
                for f, lo, width in ((self.FQK, 0, 2 * C), (self.FV, 2 * C, C)):
                    bank = self.fill_ready(pe, b, f)
                    for kc in range(KC):
                        mm = split3(pe, bank[:, 0:width], xa_hi[:, kc, :], xa_lo[:, kc, :],
                                    wa_hi[:, kc, lo:lo + width], wa_lo[:, kc, lo:lo + width], kc == 0, kc == KC - 1)
                    mm.then_inc(self.mdone, 1)
                pe.wait_ge(self.cl, b + 1)
                bank = self.fill_ready(pe, b, self.FA)
                for kc in range(KC):
                    mm = split3(pe, bank, ca_hi[:, kc, :], ca_lo[:, kc, :],
                                wa_hi[:, kc, C:3 * C], wa_lo[:, kc, C:3 * C], kc == 0, kc == KC - 1)
                mm.then_inc(self.mdone, 1)
                self.used_up(pe, b, self.FA)
                self.stack_transposes(pe, b, self.FAT, AS)
                pe.wait_ge(self.qkl, 2 * b + 1)
                self.stack_transposes(pe, b, self.FKT, KS)
                pe.wait_ge(self.qkl, 2 * b + 2)
                self.stack_transposes(pe, b, self.FQT, QS)

            def stack_transposes(self, pe, b, f0, stack):
                for f in range(2):
                    bank = self.fill_ready(pe, b, f0 + f)
                    for q in range(4):
                        mm = pe.transpose(bank[:, q * P:(q + 1) * P],
                                          stack[:, 4 * (4 * f + q):4 * (4 * f + q + 1), :].rearrange("p h d -> p (h d)"),
                                          ident[:])
                    mm.then_inc(self.mdone, 1)

            def sq_tensor(self, pe, b, k):
                if k == 0:
                    self.used_up(pe, b, self.FQT)
                    self.used_up(pe, b, self.FQT + 1)
                r, q0 = self.heads_of(k)
                rows = slice(32 * r, 32 * r + 32)
                pe.wait_ge(self.sqread, 16 * b + k + 1)
                for j in range(2):
                    mm = pe.matmul(ps[:, k % 2, 256 * j:256 * j + 256], QT1[rows, q0 + j, :],
                                   KAT[rows, q0 + j, :, :], start=True, stop=True)
                mm.then_inc(self.sq, 1)

            def sk_tensor(self, pe, b, k):
                a, kk = k // 8, k % 8
                r, q0 = kk % 4, 4 * (kk // 4)
                rows = slice(32 * r, 32 * r + 32)
                if k == 0:
                    self.used_up(pe, b, self.FQM)
                    self.used_up(pe, b, self.FQM + 1)
                pe.wait_ge(self.skread, 16 * b + k + 1)
                bank = ps[:, 2 + k % 2, :]
                if a == 0:
                    four = bank.rearrange("p (t q) -> p t q", t=4)
                    for n, m in enumerate((mask_hi, mask_lo)):
                        pe.matmul(four, ident_r[:], m[:, b, :].unsqueeze(1).to_broadcast([P, 4, TOK]),
                                  start=(n == 0), stop=False, skip_group_check=True)
                for t in range(4):
                    mm = pe.matmul(bank[:, t * P:(t + 1) * P], KAT[rows, q0 + t, a, :], QT2[rows, q0 + t, :],
                                   start=(a == 1), stop=True, skip_group_check=True)
                mm.then_inc(self.sk, 1)

            def pv_tensor(self, pe, b, k):
                a, kk = k // 8, k % 8
                r, q0 = kk % 4, 4 * (kk // 4)
                pe.wait_ge(self.skread, 2 + 16 * b + k + 1)
                if k == 0:
                    pe.wait_ge(self.onorm, 1 + b)
                for t in range(4):
                    h = 4 * (q0 + t) + r
                    mm = pe.matmul(ps[:, 4 + a, 9 * h:9 * h + 9], PR[:, k % 4, t, :], V9[:, a, h, :],
                                   start=True, stop=True, skip_group_check=True)
                mm.then_inc(self.pv, 1)

            def out_tensor(self, pe, b):
                pe.wait_ge(self.onorm, 1 + b + 1)
                bank = self.fill_ready(pe, b, self.FO)
                for kb in range(KC):
                    mm = pe.transpose(bank[:, kb * P:(kb + 1) * P], ON[:, kb * P:(kb + 1) * P], ident[:])
                mm.then_inc(self.mdone, 1)
                self.used_up(pe, b, self.FO)
                bank = self.fill_ready(pe, b, self.FWO)
                for kc in range(KC):
                    mm = split3(pe, bank[:, 0:C], ot_hi[:, kc, :], ot_lo[:, kc, :],
                                wa_hi[:, kc, 3 * C:], wa_lo[:, kc, 3 * C:], kc == 0, kc == KC - 1)
                mm.then_inc(self.mdone, 1)

            def tensor(self, pe):
                pe.sem_inc(self.sqread, 2)
                pe.sem_inc(self.skread, 2)
                pe.sem_inc(self.pv, 4)
                for s in (*self.mread, self.onorm):
                    pe.sem_inc(s, 1)
                pe.wait_ge(later_lo, 2)
                pe.wait_ge(self.mask_ready, 2)
                with pe.Fori(0, NSEQ) as b:
                    self.front_tensor(pe, b)
                    for k in range(16):
                        self.sq_tensor(pe, b, k)
                    pe.wait_ge(self.maxed, b + 1)
                    self.stack_transposes(pe, b, self.FQM, QS)
                    for k in range(16):
                        self.sk_tensor(pe, b, k)
                        if k >= 1:
                            self.pv_tensor(pe, b, k - 1)
                    self.pv_tensor(pe, b, 15)
                    self.out_tensor(pe, b)

            def scalar(self, act):
                act.wait_ge(self.setup, 5)
                with act.Fori(0, NSEQ) as b:
                    flat = "p k s -> p (k s)"
                    bank = self.filled(act, b, self.FX)
                    act.copy(xa_hi[:].rearrange(flat), bank[:, 0:C]).then_inc(self.xh, 1)
                    act.copy(ca_hi[:], CTXT[:, :, b, :]).then_inc(self.ch, 1)
                    bank = self.filled(act, b, self.FV)
                    act.copy(V9[:, 0, :, 0:HD], bank[:, 0:C].rearrange("p (h d) -> p h d", d=HD)
                             ).then_inc(self.mread[self.FV % 2], 1)
                    bank = self.filled(act, b, self.FA)
                    act.copy(V9[:, 1, :, 0:HD], bank[:, C:2 * C].rearrange("p (h d) -> p h d", d=HD)
                             ).then_inc(self.akh, 1)
                    for at in (0, 16):
                        act.copy(AS[:, :, at:at + HD].bitcast(F32R), bank[:, 0:C].rearrange("p (h d) -> p h d", d=HD)
                                 ).then_inc(self.akh, 1)
                    act.wait_ge(self.roped, b + 1)
                    for at in (0, 16):
                        act.copy(KS[:, :, at:at + HD].bitcast(F32R), RQ[:, 1]).then_inc(self.qkh, 1)
                    for at in (0, 8):
                        act.copy(QS[:, :, at:at + HD].bitcast(F32R), RQ[:, 0]).then_inc(self.qkh, 1)
                    for f0, which in ((self.FAT, 1), (self.FKT, 0)):
                        for f in range(2):
                            bank = self.filled(act, b, f0 + f)
                            act.copy(KAT[:, 4 * f:4 * f + 4, which, :], bank.rearrange("p (q s) -> p q s", q=4)
                                     ).then_inc(self.mread[(f0 + f) % 2], 1)
                    for f in range(2):
                        bank = self.filled(act, b, self.FQT + f)
                        act.copy(QT1[:, 4 * f:4 * f + 4, :].rearrange("p q s -> p (q s)"), bank
                                 ).then_inc(self.mread[f % 2], 1)
                    for par in range(2):
                        split_hi(act, par, GROUPS // 2 + 2 + b, w_hi[:, self.next_weights(b, par)], WCHUNK)
                    for f in range(2):
                        bank = self.filled(act, b, self.FQM + f)
                        act.copy(QT2[:, 4 * f:4 * f + 4, :].rearrange("p q s -> p (q s)"), bank
                                 ).then_inc(self.mread[f % 2], 1)
                    for k in range(16):
                        act.wait_ge(self.sk, 16 * b + k + 1)
                        act.wait_ge(self.pv, 16 * b + k + 1)
                        act.activation(PR[:, k % 4, :, :].rearrange("p t q -> p (t q)"), ps[:, 2 + k % 2, :],
                                       ACT.Exp).then_inc(self.skread, 1)
                    bank = self.filled(act, b, self.FO)
                    act.copy(ot_hi[:].rearrange(flat), bank[:, 0:C]).then_inc(self.oh, 1)

            RSTEPS, OSTEPS = 4, 5

            def front_vector(self, dve, b):
                flat = "p k s -> p (k s)"
                self.norm.vector(dve, b, lambda: None)
                dve.wait_ge(self.xh, b + 1)
                bank = self.filled(dve, b, self.FX)
                dve.tensor_tensor(xa_lo[:].rearrange(flat), bank[:, 0:C], xa_hi[:].rearrange(flat).bitcast(F32),
                                  ALU.subtract).then_inc(self.mread[0], 1)
                dve.wait_ge(self.ch, b + 1)
                dve.tensor_tensor(ca_lo[:], CTXT[:, :, b, :], ca_hi[:].bitcast(F32), ALU.subtract
                                  ).then_inc(self.cl, 1)
                st = Steps(dve, self.rsteps, b * self.RSTEPS)
                qk = self.filled(dve, b, self.FQK).rearrange("p (w h d) -> p w h d", w=2, d=HD)
                half = HD // 2
                st.mark(dve.tensor_tensor(T1[:], qk, rope[:, 0].unsqueeze(2).to_broadcast([P, 2, HEADS, HD]), ALU.mult))
                sin = rope[:, 1].unsqueeze(2).to_broadcast([P, 2, HEADS, HD])
                st.mark(dve.tensor_tensor(T2[:, :, :, 0:half], qk[:, :, :, half:HD], sin[:, :, :, 0:half], ALU.mult))
                dve.tensor_tensor(T2[:, :, :, half:HD], qk[:, :, :, 0:half], sin[:, :, :, half:HD], ALU.mult
                                  ).then_inc(self.mread[self.FQK % 2], 1)
                dve.wait_ge(self.akh, 3 * b + 3)
                bank = self.filled(dve, b, self.FA)
                dve.tensor_tensor(AS[:, :, 8:16], bank[:, 0:C].rearrange("p (h d) -> p h d", d=HD), AS[:, :, 0:8],
                                  ALU.subtract).then_inc(self.mread[self.FA % 2], 1)
                st.mark(dve.memset(QS[:, :, 24:28], 0.0))
                st.mark(dve.tensor_copy(mask_now[:], mask_q_sb[:, b, :]))
                dve.wait_ge(self.qkh, 4 * b + 2)
                dve.tensor_tensor(KS[:, :, 8:16], RQ[:, 1], KS[:, :, 0:8], ALU.subtract).then_inc(self.qkl, 1)
                dve.wait_ge(self.qkh, 4 * b + 4)
                st.wait()
                dve.tensor_tensor(QS[:, :, 16:24], RQ[:, 0], QS[:, :, 0:8], ALU.subtract).then_inc(self.qkl, 1)
                assert st.n == self.RSTEPS, st.n

            def sq_vector(self, dve, b, k):
                r, q0 = self.heads_of(k)
                dve.wait_ge(self.sq, 16 * b + k + 1)
                bank = ps[:, k % 2, :]
                h = 4 * q0 + r
                dve.tensor_reduce(MX[:, 1, h:h + 5:4], bank.rearrange("p (j w s) -> p j w s", j=2, w=2)[:, :, 1, :],
                                  AX_X, ALU.max)
                for j in range(2):
                    h = 4 * (q0 + j) + r
                    ins = dve.tensor_tensor_reduce(junk[:, 2 * (k % 2) + j, :], bank[:, 256 * j:256 * j + P],
                                                   mask_now[:], 1.0, -3.4e38, ALU.add, ALU.max, MX[:, 0, h:h + 1])
                ins.then_inc(self.sqread, 1)

            def max_vector(self, dve, b):
                dve.wait_ge(self.sqread, 2 + 16 * (b + 1))
                rows = QS[:, :, 24:28].rearrange("p h (a w) -> p w a h", w=2)
                dve.tensor_scalar(rows[:, 0].bitcast(F32R), MX[:], -1.0, None, ALU.mult).then_inc(self.msteps, 1)
                dve.wait_ge(self.msteps, b + 2)
                dve.scalar_tensor_tensor(rows[:, 1], MX[:], -1.0, rows[:, 0], ALU.mult, ALU.subtract
                                         ).then_inc(self.maxed, 1)

            def out_vector(self, dve, b):
                dve.wait_ge(self.pv, 4 + 16 * (b + 1))
                st = Steps(dve, self.osteps, b * self.OSTEPS)
                outs = [ps[:, 4 + a, 0:9 * HEADS].rearrange("p (h d) -> p h d", d=9) for a in range(2)]
                for a in range(2):
                    st.mark(dve.reciprocal(den[:, a, :], outs[a][:, :, HD]))
                st.wait()
                st.mark(dve.tensor_tensor(den[:, 1, :], den[:, 1, :], THG[:], ALU.mult))
                st.wait()
                st.mark(dve.tensor_tensor(O1[:], outs[0][:, :, 0:HD], den[:, 0, :].unsqueeze(2).to_broadcast([P, HEADS, HD]), ALU.mult))
                st.mark(dve.tensor_tensor(O2[:], outs[1][:, :, 0:HD], den[:, 1, :].unsqueeze(2).to_broadcast([P, HEADS, HD]), ALU.mult))
                st.wait()
                dve.tensor_tensor(ON[:].rearrange("p (h d) -> p h d", d=HD), O1[:], O2[:], ALU.add).then_inc(self.onorm, 1)
                assert st.n == self.OSTEPS, st.n
                flat = "p k s -> p (k s)"
                dve.wait_ge(self.oh, b + 1)
                bank = ps[:, 6, :]
                dve.tensor_tensor(ot_lo[:].rearrange(flat), bank[:, 0:C], ot_hi[:].rearrange(flat).bitcast(F32),
                                  ALU.subtract).then_inc(self.mread[0], 1)
                bank = self.filled(dve, b, self.FWO)
                dve.scalar_tensor_tensor(X[:, b, :], bank[:, 0:C], TG[:, 2:3], X[:, b, :], ALU.mult, ALU.add
                                         ).then_inc(self.mread[1], 1)

            def vector(self, dve):
                dve.wait_ge(ffn0.res, 1 + NSEQ)
                dve.memset(QS[:], 0.0).then_inc(self.setup, 1)
                dve.memset(KS[:], 0.0).then_inc(self.setup, 1)
                dve.memset(AS[:], 0.0).then_inc(self.setup, 1)
                dve.memset(V9[:], 1.0).then_inc(self.setup, 1)
                dve.wait_ge(self.setup, 3)
                dve.memset(KS[:, :, 24:26], 1.0).then_inc(self.mask_ready, 1)
                dve.memset(AS[:, :, 26:28], 1.0).then_inc(self.setup, 1)
                dve.wait_ge(in_late, 32)
                dve.tensor_copy(mask_hi[:], mask_raw[:]).then_inc(self.msteps, 1)
                dve.wait_ge(self.msteps, 1)
                dve.tensor_tensor(mask_lo[:], mask_raw[:], mask_hi[:].bitcast(F32), ALU.subtract
                                  ).then_inc(self.mask_ready, 1)
                dve.wait_ge(self.setup, 5)
                dve.wait_ge(self.mask_ready, 2)
                with dve.Fori(0, NSEQ) as b:
                    self.front_vector(dve, b)
                    for k in range(16):
                        self.sq_vector(dve, b, k)
                    self.max_vector(dve, b)
                    self.out_vector(dve, b)

            def gpsimd(self, pool):
                with pool.Fori(0, NSEQ) as b:
                    self.norm.gpsimd(pool, b)
                    self.used_up(pool, b, self.FQK)
                    pool.tensor_tensor(RQ[:], T1[:], T2[:], ALU.add).then_inc(self.roped, 1)
                    for par in range(2):
                        n = GROUPS + 2 + 2 * b + par + 1
                        split_lo(pool, par, n, w_lo[:, self.next_weights(b, par)],
                                 w_hi[:, self.next_weights(b, par)], WCHUNK, later_lo)


        ffn0 = Ffn(0)
        attn = Attention()
        ffn1 = Ffn(1)

        block = ctx.enter_context(nc.Block())

        @block.sync
        def _(sp):
            mixer_sync(sp)
            attn.sync(sp)
            with sp.Fori(0, NSEQ) as b:
                sp.wait_ge(ffn1.res, 1 + b + 1)
                sp.dma_start(out[b], X[:, b, :]).then_inc(out_stored, 16)
            sp.wait_ge(out_stored, 16 * NSEQ)

        @block.scalar
        def _(act):
            mixer_scalar(act)
            attn.weights_scalar(act)
            ffn0.scalar(act)
            attn.scalar(act)
            ffn1.scalar(act)

        @block.gpsimd
        def _(pool):
            mixer_gpsimd(pool)
            attn.weights_gpsimd(pool)
            ffn0.gpsimd(pool)
            attn.gpsimd(pool)
            ffn1.gpsimd(pool)

        @block.tensor
        def _(pe):
            mixer_tensor(pe)
            ffn0.tensor(pe)
            attn.tensor(pe)
            ffn1.tensor(pe)

        @block.vector
        def _(dve):
            mixer_vector(dve)
            dve.wait_ge(a_res, 4)
            ffn0.vector(dve)
            attn.vector(dve)
            ffn1.vector(dve)


def layouts(inp):
    f = {k: np.asarray(v) for k, v in inp.items()}

    def rows(a):
        k = a.shape[0] // P
        return a.reshape(k, P, a.shape[1]).transpose(1, 0, 2).reshape(P, k * a.shape[1])

    def pad_rows(a, n):
        return np.concatenate([a, np.zeros((n - a.shape[0], a.shape[1]), a.dtype)], 0)

    def chunks(a, n):
        a = np.concatenate([a, np.zeros((P, n * (-(-a.shape[1] // n)) - a.shape[1]), a.dtype)], 1)
        return np.ascontiguousarray(a.reshape(P, n, -1).transpose(1, 0, 2))

    ctx = f["ctx_2048"]
    ctx_t = ctx.transpose(2, 0, 1).reshape(KC, P, NSEQ, TOK).transpose(1, 0, 2, 3).reshape(P, -1)
    k = f["L0_xattn_k"]
    k_pad = np.concatenate([np.zeros((GROUPS, C - 1), k.dtype), k], 1)
    toep = k_pad[:, C - 1 - np.arange(P)[:, None] + np.arange(C)[None, :]]

    gu = f["L0_ffn_shared_gate_up_w"]
    up = [gu[SHARED0 * t + I0 * n:SHARED0 * t + I0 * (n + 1)] for n in range(4) for t in range(2)]
    up0 = np.concatenate(up + [f["L0_ffn_w13"].reshape(-1, C)], 0).T
    down0 = np.concatenate([f["L0_ffn_shared_down_w"].T, f["L0_ffn_w2"].transpose(0, 2, 1).reshape(-1, C)], 0)
    route0 = np.concatenate([f["L0_ffn_gate_w"].T, f["L0_ffn_shared_gate_w"].T, np.zeros((C, 1), np.float32)], 1)
    up1 = np.concatenate([f["L1_ffn_w_up"].transpose(1, 0, 2).reshape(C, -1), f["L1_ffn_w_shared_up"]], 1)
    down1 = np.concatenate([f["L1_ffn_w_down"].reshape(-1, C), f["L1_ffn_w_shared_down"]], 0)

    def stream(up, down, route):
        a = np.concatenate([rows(up), rows(pad_rows(down, KT * P)), rows(route)], 1)
        a = np.concatenate([a, np.zeros((P, WCOLS - a.shape[1]), a.dtype)], 1)
        return chunks(a, 16)

    qkvo = np.concatenate([f["L1_xattn_Wq"], f["L1_xattn_Wk"], f["L1_xattn_Wv"], f["L1_xattn_Wo"]], 1)
    inv_freq = 1.0 / 10000.0 ** (np.arange(0, HD, 2, dtype=np.float32) / HD)
    emb = np.outer(np.arange(TOK, dtype=np.float32), inv_freq)
    emb = np.concatenate([emb, emb], -1)
    sign = np.where(np.arange(HD) < HD // 2, -1.0, 1.0)
    cos, sin = np.cos(emb), np.sin(emb) * sign
    scale = 1.0 / np.sqrt(np.float32(HD))
    rope = np.stack([np.stack([cos * scale, cos], 1), np.stack([sin * scale, sin], 1)], 1)
    mask = f["mask_Bx1xSxS_fk0"][:, 0]
    arrays = {
        "x": f["x"], "ctx_t": ctx_t, "toep": toep, "bias": f["fside_S2_0"],
        "gates": np.stack([f["g_xattn"][0], f["g_ffn"][0], f["g_xattn"][1], f["g_ffn"][1]]),
        "head_gate": f["L1_xattn_gate"].reshape(-1),
        "mask_q": mask, "mask_k": mask.transpose(0, 2, 1),
        "w_ffn0": stream(up0, down0, route0), "w_attn": chunks(rows(qkvo), 2),
        "w_ffn1": stream(up1, down1, f["L1_ffn_w_gate"]),
        "ident_d": np.eye(P, dtype=np.float32),
        "before_d": np.triu(np.ones((P, P), np.float32), 1),
        "rope_d": rope.reshape(P, -1).astype(np.float32),
    }
    return {n: np.ascontiguousarray(a) for n, a in arrays.items()}


def kernel(**inputs):
    import concourse.bacc as bacc
    from concourse.bass_utils import run_bass_kernel_spmd

    nc = bacc.Bacc("TRN2", target_bir_lowering=False, num_devices=1, dynamic_dma_scratch_size=2048)
    arrays = layouts(inputs)
    args = {n: nc.dram_tensor(f"in_{n}", a.shape, mybir.dt.from_np(a.dtype), kind="ExternalInput").ap()
            for n, a in arrays.items()}
    out = nc.dram_tensor("out_0", (NSEQ, TOK, C), F32, kind="ExternalOutput").ap()
    program(nc, out=out, **args)
    r = run_bass_kernel_spmd(nc, [{f"in_{n}": a for n, a in arrays.items()}], core_ids=[0])
    return r.results[0]["out_0"]
```

```python
from contextlib import ExitStack

import numpy as np

import concourse.bass as bass
from concourse import mybir

ALU = mybir.AluOpType
ACT = mybir.ActivationFunctionType
AX_X = mybir.AxisListType.X
F32 = mybir.dt.float32
F32R = mybir.dt.float32r
BF16 = mybir.dt.bfloat16

P = 128
FIRST = 0
SETUP = 7
NSEQ = 8
TOK = 128
C = 256
KC = C // P
EPS = 1e-5

GROUPS = 16
GI = TOK // GROUPS

HIDDEN = 2112
UPW = 2 * HIDDEN
KT = -(-HIDDEN // P)
KLAST = HIDDEN - (KT - 1) * P
TGROUPS = [(g, min(4, KT - g)) for g in range(0, KT, 4)]
NTG = len(TGROUPS)
E0, I0, SHARED0 = 8, 176, 704
E1, I1, SHARED1 = 64, 32, 64
TOP0, TOP1, CAP = 2, 6, 128
ROUTE0 = E0 + 2
ROUTE1 = E1
WCOLS = KC * UPW + KT * C + KC * ROUTE1
DOWN_AT = KC * UPW
ROUTE_AT = DOWN_AT + KT * C
WCHUNK = WCOLS // 16

HEADS = 32
HD = C // HEADS
QUADS = HEADS // 4
ATTNW = 4 * C


class Steps:

    def __init__(self, eng, sem, base):
        self.eng, self.sem, self.base, self.n = eng, sem, base, 0

    def mark(self, ins):
        ins.then_inc(self.sem, 1)
        self.n += 1

    def wait(self):
        self.eng.wait_ge(self.sem, self.base + self.n)


def settled(eng, passed):
    eng.sem_inc(passed, 1)


def split3(pe, out, hi, lo, w_hi, w_lo, first, last):
    pe.matmul(out, hi, w_hi, start=first, stop=False)
    pe.matmul(out, hi, w_lo, start=False, stop=False)
    return pe.matmul(out, lo, w_hi, start=False, stop=last)


def program(nc, x, ctx_t, toep, bias, gates, head_gate, mask_q, mask_k, w_ffn0, w_attn, w_ffn1,
            ident_d, before_d, rope_d, out):
    with ExitStack() as ctx:
        def sem(name):
            return ctx.enter_context(nc.semaphore(name))

        def sb_in(scope):
            return lambda name, shape, dt=F32: scope.enter_context(nc.sbuf_tensor(name, shape, dt))

        sb = sb_in(ctx)
        ps = ctx.enter_context(nc.psum_tensor("ps", [P, 8, 512], F32))

        X = sb("residual", [P, NSEQ, C])
        CTXT = sb("ctx_t", [P, KC, NSEQ, TOK])
        ident = sb("ident", [P, P])
        ident_r = sb("ident_r", [P, P], F32R)
        before_f = sb("before_f", [P, P])
        before = sb("before", [P, P], BF16)
        ones_bf = sb("ones_bf", [P, P], BF16)
        rope = sb("rope", [P, 2, 2, HD])
        G = sb("gates", [P, 4])
        TG = sb("tanh_gates", [P, 4])
        HG = sb("head_gate", [P, HEADS])
        THG = sb("tanh_head_gate", [P, HEADS])
        w_hi = sb("w_hi", [P, WCOLS], F32R)
        w_lo = sb("w_lo", [P, WCOLS], F32R)
        wa_hi = sb("wa_hi", [P, KC, ATTNW], F32R)
        wa_lo = sb("wa_lo", [P, KC, ATTNW], F32R)
        raw = sb("raw_weights", [P, 2, WCHUNK])
        mhalf = sb("minus_half", [P, NSEQ])
        stats = sb("stats", [P, NSEQ, 6])
        mv = sb("mean_var", [P, NSEQ, 2])
        veps = sb("var_eps", [P, NSEQ])
        rstd = sb("rstd", [P, NSEQ])

        with ExitStack() as scope:
            sa = sb_in(scope)
            xn_u = sa("xn_then_skip", [P, NSEQ * C])
            XN = xn_u[:].rearrange("p (b c) -> p b c", b=NSEQ)
            U = xn_u[:].rearrange("p (k b s) -> p k b s", k=KC, b=NSEQ)
            VT = sa("v_t", [P, KC, NSEQ, TOK])
            R = sa("mixed_t", [P, KC, NSEQ, TOK])
            T = sa("toeplitz", [P, 2, C])
            KV = sa("kv", [P, 2, KC, 512])
            Z = sa("z", [P, 2, KC, 512])
            SK = sa("skip_sum", [P, KC * NSEQ * GROUPS])
            bias_b = sa("bias_b", [P, TOK])

        with ExitStack() as scope:
            sf = sb_in(scope)
            xn_f = sf("xn_f", [P, C])
            wa_raw = sf("wa_raw", [P, KC, ATTNW])
            xt_hi = sf("xt_hi", [P, KC, TOK], F32R)
            xt_lo = sf("xt_lo", [P, KC, TOK], F32R)
            SG = sf("silu_gate", [P, 4, 256])
            HID = sf("hidden", [P, HIDDEN])
            ht_hi = sf("hidden_t_hi", [P, KT, TOK], F32R)
            ht_lo = sf("hidden_t_lo", [P, KT, TOK], F32R)
            top8 = sf("top8", [P, 8])
            sel8 = sf("select8", [P, 8])
            neg_max = sf("neg_max", [P, 1])
            ex = sf("exps", [P, E1 + 2])
            ex_sum = sf("exp_sum", [P, 1])
            prob = sf("prob", [P, E1 + 8])
            marked = sf("marked", [P, E1 + 8])
            W = sf("route_w", [P, E1])
            WV = sf("route_w_valid", [P, E1])
            tmp1 = sf("tmp1", [P, E1])
            chosen = sf("chosen", [P, E1], BF16)
            earlier = sf("earlier", [P, E1], BF16)

        with ExitStack() as scope:
            sc = sb_in(scope)
            xn_a = sc("xn_a", [P, C])
            xa_hi = sc("xa_hi", [P, KC, TOK], F32R)
            xa_lo = sc("xa_lo", [P, KC, TOK], F32R)
            ca_hi = sc("ca_hi", [P, KC, TOK], F32R)
            ca_lo = sc("ca_lo", [P, KC, TOK], F32R)
            T1 = sc("rope_cos", [P, 2, HEADS, HD])
            T2 = sc("rope_sin", [P, 2, HEADS, HD])
            QS = sc("q_stack", [P, HEADS, 32])
            KS = sc("k_stack", [P, HEADS, 32])
            AS = sc("a_stack", [P, HEADS, 32])
            KAT = sc("ka_t", [P, 2, QUADS, 2, TOK], F32R)
            QT = sc("q_t", [P, QUADS, TOK], F32R)
            QB = sc("q_blocks", [P, QUADS, 4, TOK], F32R)
            V9 = sc("v_ones", [P, 2, 2, HEADS, HD + 1])
            junk = sc("junk", [P, 4, TOK], BF16)
            MX = sc("row_max", [P, 4, 2, QUADS])
            MXS = sc("max_split", [P, 4, 4, QUADS])
            MXT = sc("max_t", [P, TOK], F32R)
            mask_q_sb = sc("mask_q", [P, 2, TOK])
            mask_raw = sc("mask_raw", [P, 2, TOK])
            mask_hi = sc("mask_hi", [P, 2, TOK], F32R)
            mask_lo = sc("mask_lo", [P, 2, TOK], F32R)
            PR = sc("probs", [P, 4, 4, TOK])
            den = sc("den", [P, 2, HEADS])
            ON = sc("o_norm", [P, C])
            ot_hi = sc("ot_hi", [P, KC, TOK], F32R)
            ot_lo = sc("ot_lo", [P, KC, TOK], F32R)

        in_x = [sem("in_x0"), sem("in_x1")]
        in_ctx, in_const, in_late = sem("in_ctx"), sem("in_const"), sem("in_late")
        in_toep = [sem("in_toep0"), sem("in_toep1")]
        in_raw = [sem("in_raw0"), sem("in_raw1")]
        chunk_hi, chunk_lo, later_lo = sem("chunk_hi"), sem("chunk_lo"), sem("later_lo")
        consts = sem("consts")
        passed = sem("passed")
        gates_ready = sem("gates_ready")
        out_stored = sem("out_stored")
        a_steps, a_var, a_rstd, a_xn = sem("a_steps"), sem("a_var"), sem("a_rstd"), sem("a_xn")
        a_xt, a_vt = sem("a_xt"), sem("a_vt")
        a_kv, a_y, a_zread, a_red = sem("a_kv"), sem("a_y"), sem("a_zread"), sem("a_red")
        a_skip, a_u, a_rt, a_res = sem("a_skip"), sem("a_u"), sem("a_rt"), sem("a_res")
        a_rsum = sem("a_rsum")

        def split_hi(act, slot, landed, dst, width):
            act.wait_ge(in_raw[slot], 16 * landed)
            act.copy(dst, raw[:, slot, 0:width]).then_inc(chunk_hi, 1)

        def split_lo(eng, slot, n1, dst, hi, width, done):
            eng.wait_ge(chunk_hi, n1)
            eng.tensor_tensor(dst, raw[:, slot, 0:width], hi.bitcast(F32), ALU.subtract).then_inc(done, 1)

        def mixer_sync(sp):
            sp.dma_start(X[:, 0:4, :], x[0:4].rearrange("b s c -> s b c")).then_inc(in_x[0], 16)
            sp.dma_start(X[:, 4:8, :], x[4:8].rearrange("b s c -> s b c")).then_inc(in_x[1], 16)
            sp.dma_start(ident[:], ident_d).then_inc(in_const, 16)
            sp.dma_start(CTXT[:], ctx_t.rearrange("p (k b s) -> p k b s", k=KC, b=NSEQ)).then_inc(in_ctx, 16)
            sp.dma_start(bias_b[:], bias.partition_broadcast(P)).then_inc(in_const, 16)
            sp.dma_start(G[:], gates.partition_broadcast(P)).then_inc(in_const, 16)
            sp.dma_start(HG[:], head_gate.partition_broadcast(P)).then_inc(in_const, 16)
            sp.dma_start(rope[:], rope_d.rearrange("p (a b d) -> p a b d", a=2, b=2)).then_inc(in_const, 16)
            sp.dma_start(before_f[:], before_d).then_inc(in_const, 16)
            with sp.Fori(0, GROUPS // 2) as i:
                for par in range(2):
                    h = 2 * i + par
                    sp.wait_ge(a_y, h + 1)
                    sp.dma_start(T[:, par, :], toep[h]).then_inc(in_toep[par], 16)
                    sp.wait_ge(chunk_lo, h + 1)
                    sp.dma_start(raw[:, par, 0:WCHUNK], w_ffn0[h]).then_inc(in_raw[par], 16)
            sp.wait_ge(a_res, 4)
            sp.dma_start(wa_raw[:], w_attn.rearrange("p (k n) -> p k n", k=KC)).then_inc(in_late, 16)

        def mixer_scalar(act):
            act.wait_ge(in_const, 16 * 6)
            act.activation(TG[:], G[:], ACT.Tanh).then_inc(gates_ready, 1)
            act.activation(THG[:], HG[:], ACT.Tanh).then_inc(gates_ready, 1)
            for n in range(4):
                act.wait_ge(a_xt, n + 1)
                act.copy(VT[:, :, 2 * n:2 * n + 2, :],
                         ps[:, n, :].rearrange("p (k b s) -> p k b s", k=KC, b=2)).then_inc(a_vt, 1)
            with act.Fori(0, GROUPS // 2) as i:
                for par in range(2):
                    h = 2 * i + par
                    split_hi(act, par, i + 1, w_hi[:, bass.ds(h * WCHUNK, WCHUNK)], WCHUNK)

        def mixer_gpsimd(pool):
            pool.wait_ge(a_var, 1)
            pool.tensor_tensor(rstd[:], veps[:], mhalf[:], ALU.pow).then_inc(a_rstd, 1)
            pool.wait_ge(a_vt, 4)
            pool.wait_ge(in_ctx, 16)
            with pool.Fori(0, GROUPS // 2) as i:
                for par in range(2):
                    h = 2 * i + par
                    pool.wait_ge(a_y, h + 1)
                    for mb in range(KC):
                        v = VT[:, mb, :, bass.ds(h * GI, GI)].unsqueeze(3).to_broadcast([P, NSEQ, GI, GI])
                        k = CTXT[:, mb, :, bass.ds(h * GI, GI)].unsqueeze(2).to_broadcast([P, NSEQ, GI, GI])
                        pool.tensor_tensor(
                            KV[:, par, mb, :].rearrange("p (b i j) -> p b i j", b=NSEQ, i=GI), v, k, ALU.mult,
                        ).then_inc(a_kv, 1)
            pool.wait_ge(a_skip, 1)
            pool.tensor_tensor(
                U[:].rearrange("p k b (h j) -> p (k b h) j", j=GI),
                CTXT[:].rearrange("p k b (h j) -> p (k b h) j", j=GI),
                SK[:].unsqueeze(2).to_broadcast([P, KC * NSEQ * GROUPS, GI]), ALU.mult).then_inc(a_u, 1)

        def mixer_tensor(pe):
            pe.sem_inc(a_y, 2)
            pe.sem_inc(a_zread, 2)
            pe.wait_ge(in_const, 16 * 6)
            pe.wait_ge(a_xn, 1)
            for n in range(4):
                for kb in range(KC):
                    for b2 in range(2):
                        at = (kb * 2 + b2) * TOK
                        mm = pe.transpose(ps[:, n, at:at + TOK], XN[:, 2 * n + b2, kb * P:(kb + 1) * P], ident[:])
                mm.then_inc(a_xt, 1)
            with pe.Fori(0, GROUPS // 2) as i:
                for par in range(2):
                    h = 2 * i + par
                    y0, y1 = ps[:, 4 + 2 * par, :], ps[:, 5 + 2 * par, :]
                    pe.wait_ge(in_toep[par], 16 * i + 16)
                    pe.wait_ge(a_kv, 2 * h + 2)
                    pe.wait_ge(a_zread, h + 1)
                    pe.matmul(y0, T[:, par, 0:P], KV[:, par, 0, :], start=True, stop=True)
                    pe.matmul(y1, T[:, par, P:C], KV[:, par, 0, :], start=True, stop=False)
                    pe.matmul(y1, T[:, par, 0:P], KV[:, par, 1, :], start=False, stop=True).then_inc(a_y, 1)
            pe.wait_ge(a_rsum, KC)
            for n in range(4):
                for b2 in range(2):
                    for lb in range(KC):
                        at = b2 * C + lb * P
                        mm = pe.transpose(ps[:, n, at:at + P], R[:, lb, 2 * n + b2, :], ident[:])
                mm.then_inc(a_rt, 1)

        def mixer_vector(dve):
            st = Steps(dve, a_steps, 0)
            dve.sem_inc(chunk_lo, 2)
            dve.memset(mhalf[:], -0.5).then_inc(consts, 1)
            dve.memset(ones_bf[:], 1.0).then_inc(consts, 1)
            for b in range(NSEQ):
                dve.wait_ge(in_x[b // 4], 16)
                st.mark(dve.bn_stats(stats[:, b, :], X[:, b, :]))
            for b in range(NSEQ):
                dve.wait_ge(a_steps, b + 1)
                st.mark(dve.bn_aggr(mv[:, b, :], stats[:, b, :]))
            st.wait()
            dve.tensor_scalar(veps[:], mv[:, :, 1], EPS, None, ALU.add).then_inc(a_var, 1)
            dve.wait_ge(a_rstd, 1)
            for b in range(NSEQ):
                ins = dve.tensor_scalar(XN[:, b, :], X[:, b, :], mv[:, b, 0:1], rstd[:, b:b + 1],
                                        ALU.subtract, ALU.mult)
            ins.then_inc(a_xn, 1)
            dve.wait_ge(in_const, 16 * 6)
            dve.tensor_copy(ident_r[:], ident[:]).then_inc(consts, 1)
            dve.tensor_copy(before[:], before_f[:]).then_inc(consts, 1)
            dve.wait_ge(a_vt, 4)
            dve.wait_ge(in_ctx, 16)
            st.mark(dve.tensor_tensor(U[:], VT[:], CTXT[:], ALU.mult))
            st.wait()
            flat = "p k b s -> p (k b) s"
            st.mark(dve.tensor_tensor(U[:].rearrange(flat), U[:].rearrange(flat),
                                      bias_b[:].unsqueeze(1).to_broadcast([P, KC * NSEQ, TOK]), ALU.mult))
            st.wait()
            dve.tensor_reduce(SK[:], U[:].rearrange("p k b (h j) -> p (k b h) j", j=GI), AX_X, ALU.add
                              ).then_inc(a_skip, 1)
            with dve.Fori(0, GROUPS // 2) as i:
                for par in range(2):
                    h = 2 * i + par
                    dve.wait_ge(a_y, 2 + h + 1)
                    for lb in range(KC):
                        x1 = CTXT[:, lb, :, bass.ds(h * GI, GI)].unsqueeze(3).to_broadcast([P, NSEQ, GI, GI])
                        four = "p (b i j) -> p b i j"
                        ins = dve.tensor_tensor(
                            Z[:, par, lb, :].rearrange(four, b=NSEQ, i=GI),
                            ps[:, 4 + 2 * par + lb, :].rearrange(four, b=NSEQ, i=GI), x1, ALU.mult)
                    ins.then_inc(a_zread, 1)
                    split_lo(dve, par, h + 1, w_lo[:, bass.ds(h * WCHUNK, WCHUNK)],
                             w_hi[:, bass.ds(h * WCHUNK, WCHUNK)], WCHUNK, chunk_lo)
                    dve.wait_ge(a_zread, 2 + h + 1)
                    for lb in range(KC):
                        dve.tensor_reduce(R[:, lb, :, bass.ds(h * GI, GI)],
                                          Z[:, par, lb, :].rearrange("p (b i j) -> p b j i", b=NSEQ, i=GI),
                                          AX_X, ALU.add).then_inc(a_red, 1)
            dve.wait_ge(a_u, 1)
            dve.wait_ge(a_red, 2 * GROUPS)
            for lb in range(KC):
                dve.tensor_tensor(R[:, lb], R[:, lb], U[:, lb], ALU.add).then_inc(a_rsum, 1)
            dve.wait_ge(gates_ready, 2)
            for n in range(4):
                dve.wait_ge(a_rt, n + 1)
                xs = X[:, 2 * n:2 * n + 2, :].rearrange("p b c -> p (b c)")
                dve.scalar_tensor_tensor(xs, ps[:, n, :], TG[:, 0:1], xs, ALU.mult, ALU.add).then_inc(a_res, 1)

        class Norm:
            STEPS = 2

            def __init__(self, tag, xn):
                self.steps, self.var, self.rstd, self.xn_ready = (
                    sem(f"{tag}_norm_steps"), sem(f"{tag}_var"), sem(f"{tag}_rstd"), sem(f"{tag}_xn"))
                self.xn = xn

            def vector(self, dve, b, xn_free):
                st = Steps(dve, self.steps, b * self.STEPS)
                st.mark(dve.bn_stats(stats[:, 0, :], X[:, b, :]))
                st.wait()
                settled(dve, passed)
                st.mark(dve.bn_aggr(mv[:, 0, :], stats[:, 0, :]))
                st.wait()
                dve.tensor_scalar(veps[:, 0:1], mv[:, 0, 1:2], EPS, None, ALU.add).then_inc(self.var, 1)
                dve.wait_ge(self.rstd, b + 1)
                xn_free()
                dve.tensor_scalar(self.xn[:], X[:, b, :], mv[:, 0, 0:1], rstd[:, 0:1],
                                  ALU.subtract, ALU.mult).then_inc(self.xn_ready, 1)

            def gpsimd(self, pool, b):
                pool.wait_ge(self.var, b + 1)
                pool.tensor_tensor(rstd[:, 0:1], veps[:, 0:1], mhalf[:, 0:1], ALU.pow).then_inc(self.rstd, 1)

        class Ffn:
            def __init__(self, layer):
                tag = f"f{layer}"
                self.layer = layer
                self.norm = Norm(tag, xn_f)
                self.xt, self.xh, self.xl = sem(f"{tag}_xt"), sem(f"{tag}_xh"), sem(f"{tag}_xl")
                self.logit, self.neg, self.exps = sem(f"{tag}_logit"), sem(f"{tag}_neg"), sem(f"{tag}_exps")
                self.w_ready, self.chosen, self.pos = sem(f"{tag}_w_ready"), sem(f"{tag}_chosen"), sem(f"{tag}_pos")
                self.valid, self.up, self.used = sem(f"{tag}_valid"), sem(f"{tag}_up"), sem(f"{tag}_used")
                self.silu, self.weighted, self.ht = sem(f"{tag}_silu"), sem(f"{tag}_weighted"), sem(f"{tag}_ht")
                self.hh, self.hl, self.down = sem(f"{tag}_hh"), sem(f"{tag}_hl"), sem(f"{tag}_down")
                self.res, self.rsteps, self.pread = sem(f"{tag}_res"), sem(f"{tag}_rsteps"), sem(f"{tag}_pread")
                if layer == 0:
                    self.units = [(2 * I0 * n, 2 * I0, I0 * n, I0) for n in range(12)]
                    self.need = [3, 6, 9, 12, 12]
                    self.order = ["u0", "u1", "u2", "u3", "u4", "T0", "u5", "u6", "u7", "T1", "u8", "D0", "u9",
                                  "u10", "T2", "u11", "D1", "X", "D2", "T3", "T4", "R", "D3", "D4"]
                    self.tg = 1
                    self.nroute = ROUTE0
                else:
                    self.units = [(512 * n, 512, 256 * n, 256) for n in range(8)] + [(4096, 128, 2048, 64)]
                    self.need = [2, 4, 6, 8, 9]
                    self.order = ["u0", "u1", "P", "u2", "u3", "T0", "u4", "u5", "T1", "D0", "u6", "u7", "T2", "D1",
                                  "u8", "X", "D2", "T3", "T4", "R", "D3", "D4"]
                    self.tg = 3
                    self.nroute = ROUTE1
                self.nu = len(self.units)

            def x_tensor(self, pe, b):
                pe.wait_ge(self.norm.xn_ready, b + 1)
                if b is not FIRST:
                    pe.wait_ge(self.w_ready, b)
                    if self.layer == 1:
                        pe.wait_ge(self.valid, b)
                for kb in range(KC):
                    mm = pe.transpose(ps[:, 7, kb * P:(kb + 1) * P], xn_f[:, kb * P:(kb + 1) * P], ident[:])
                mm.then_inc(self.xt, 1)

            def x_scalar(self, act, b):
                act.wait_ge(self.xt, b + 1)
                act.copy(xt_hi[:].rearrange("p k s -> p (k s)"), ps[:, 7, 0:C]).then_inc(self.xh, 1)

            def x_vector(self, dve, b):
                dve.wait_ge(self.xh, b + 1)
                dve.tensor_tensor(xt_lo[:].rearrange("p k s -> p (k s)"), ps[:, 7, 0:C],
                                  xt_hi[:].rearrange("p k s -> p (k s)").bitcast(F32), ALU.subtract
                                  ).then_inc(self.xl, 1)

            def r_tensor(self, pe, b):
                pe.wait_ge(self.xl, b + 1)
                for kc in range(KC):
                    at = ROUTE_AT + kc * self.nroute
                    mm = split3(pe, ps[:, 7, C:C + self.nroute], xt_hi[:, kc, :], xt_lo[:, kc, :],
                                w_hi[:, at:at + self.nroute], w_lo[:, at:at + self.nroute], kc == 0, kc == KC - 1)
                mm.then_inc(self.logit, 1)

            def r_scalar(self, act, b):
                if self.layer == 0:
                    act.wait_ge(self.neg, b + 1)
                    act.activation(ex[:, 0:E0], ps[:, 7, C:C + E0], ACT.Exp, bias=neg_max[:, 0:1],
                                   accum_out=ex_sum[:]).then_inc(self.exps, 1)
                    act.activation(ex[:, E0:E0 + 1], ps[:, 7, C + E0:C + E0 + 1], ACT.Exp, scale=-1.0
                                   ).then_inc(self.exps, 1)
                else:
                    act.wait_ge(self.logit, b + 1)
                    act.activation(ex[:, 0:E1], ps[:, 7, C:C + E1], ACT.Exp, scale=-1.0).then_inc(self.exps, 1)

            RSTEPS = (7, 8)

            def r_vector(self, dve, b):
                n, top = ((E0, TOP0), (E1, TOP1))[self.layer]
                width = n + 8 - top
                st = Steps(dve, self.rsteps, b * self.RSTEPS[self.layer])
                if self.layer == 0:
                    dve.wait_ge(self.logit, b + 1)
                    settled(dve, passed)
                    st.mark(dve.max(top8[:], ps[:, 7, C:C + E0]))
                    st.wait()
                    dve.tensor_scalar(neg_max[:], top8[:, 0:1], -1.0, None, ALU.mult).then_inc(self.neg, 1)
                    dve.wait_ge(self.exps, 2 * b + 2)
                    st.mark(dve.reciprocal(tmp1[:, 0:1], ex_sum[:]))
                    st.mark(dve.tensor_scalar(tmp1[:, 1:2], ex[:, E0:E0 + 1], 1.0, None, ALU.add))
                    st.wait()
                    st.mark(dve.tensor_scalar(prob[:, 0:n], ex[:, 0:n], tmp1[:, 0:1], None, ALU.mult))
                else:
                    dve.wait_ge(self.exps, b + 1)
                    st.mark(dve.tensor_scalar(tmp1[:], ex[:, 0:n], 1.0, None, ALU.add))
                    st.wait()
                    st.mark(dve.reciprocal(prob[:, 0:n], tmp1[:]))
                st.wait()
                settled(dve, passed)
                st.mark(dve.max(top8[:], prob[:, 0:n]))
                st.wait()
                st.mark(dve.tensor_copy(sel8[:, 0:top], top8[:, 0:top]))
                st.wait()
                settled(dve, passed)
                st.mark(dve.match_replace(marked[:, 0:width], sel8[:], prob[:, 0:width], -3.0))
                st.wait()
                if self.layer == 0:
                    dve.reciprocal(W[:, n:n + 1], tmp1[:, 1:2]).then_inc(self.pread, 1)
                    dve.scalar_tensor_tensor(W[:, 0:n], marked[:, 0:n], -2.0, prob[:, 0:n],
                                             ALU.is_lt, ALU.mult).then_inc(self.w_ready, 1)
                else:
                    st.mark(dve.scalar_tensor_tensor(W[:], marked[:, 0:n], -2.0, prob[:, 0:n],
                                                     ALU.is_lt, ALU.mult))
                    st.wait()
                    st.mark(dve.reduce_sum(ex_sum[:], W[:], axis=AX_X))
                    st.wait()
                    st.mark(dve.reciprocal(tmp1[:, 0:1], ex_sum[:]))
                    st.wait()
                    dve.tensor_scalar(W[:], W[:], tmp1[:, 0:1], None, ALU.mult).then_inc(self.w_ready, 1)
                    dve.tensor_scalar(chosen[:], marked[:, 0:n], -2.0, None, ALU.is_lt).then_inc(self.chosen, 1)
                assert st.n == self.RSTEPS[self.layer], st.n

            def p_tensor(self, pe, b):
                pe.wait_ge(self.chosen, b + 1)
                pe.wait_ge(self.pread, b + 1)
                pe.matmul(ps[:, 7, 384:384 + E1], before[:], chosen[:], start=True, stop=False)
                pe.matmul(ps[:, 7, 384:384 + E1], ones_bf[:], earlier[:], start=False, stop=True
                          ).then_inc(self.pos, 1)

            def p_vector(self, dve, b):
                dve.wait_ge(self.pos, b + 1)
                dve.wait_ge(self.w_ready, b + 1)
                dve.wait_ge(self.weighted, 1 + 8 * b)
                dve.scalar_tensor_tensor(WV[:], ps[:, 7, 384:384 + E1], float(CAP), W[:],
                                         ALU.is_lt, ALU.mult).then_inc(self.valid, 1)
                dve.tensor_tensor(earlier[:], earlier[:], chosen[:], ALU.add).then_inc(self.pread, 1)

            def bank_turn(self, u):
                if u >= 4:
                    return self.nu + u - 4 + 1
                last = max(v for v in range(self.nu) if v % 4 == u)
                return last + 1

            def u_tensor(self, pe, b, u):
                c0, width, _, _ = self.units[u]
                pe.wait_ge(self.used, b * self.nu + self.bank_turn(u))
                for kc in range(KC):
                    at = kc * UPW + c0
                    mm = split3(pe, ps[:, u % 4, 0:width], xt_hi[:, kc, :], xt_lo[:, kc, :],
                                w_hi[:, at:at + width], w_lo[:, at:at + width], kc == 0, kc == KC - 1)
                mm.then_inc(self.up, 1)

            def parts(self, u):
                bank = ps[:, u % 4, :]
                if self.layer == 0:
                    return bank[:, 0:I0], bank[:, I0:2 * I0]
                if u == 8:
                    return bank[:, SHARED1:2 * SHARED1], bank[:, 0:SHARED1]
                both = bank.rearrange("p (e t d) -> p e t d", e=8, t=2)
                return both[:, :, 0, :], both[:, :, 1, :]

            def silu_of(self, u):
                hw = self.units[u][3]
                s = SG[:, u % 4, 0:hw]
                return s.rearrange("p (e d) -> p e d", e=8) if self.layer == 1 and u < 8 else s

            def hid_of(self, u):
                _, _, h0, hw = self.units[u]
                s = HID[:, h0:h0 + hw]
                return s.rearrange("p (e d) -> p e d", e=8) if self.layer == 1 and u < 8 else s

            def u_scalar(self, act, b, u):
                act.wait_ge(self.up, b * self.nu + u + 1)
                act.activation(self.silu_of(u), self.parts(u)[0], ACT.Silu).then_inc(self.silu, 1)

            def u_vector(self, dve, b, u):
                if u == 0:
                    dve.wait_ge(self.ht, 1 + NTG * b)
                    if self.layer == 0:
                        dve.wait_ge(self.w_ready, b + 1)
                        dve.wait_ge(self.pread, b + 1)
                dve.wait_ge(self.silu, b * self.nu + u + 1)
                if self.layer == 0:
                    e = E0 if u < 4 else u - 4
                    dve.scalar_tensor_tensor(self.hid_of(u), self.silu_of(u), W[:, e:e + 1], self.parts(u)[1],
                                             ALU.mult, ALU.mult).then_inc(self.used, 1)
                else:
                    dve.tensor_tensor(self.hid_of(u), self.silu_of(u), self.parts(u)[1], ALU.mult
                                      ).then_inc(self.used, 1)

            def u_gpsimd(self, pool, b, u):
                if u == 0:
                    pool.wait_ge(self.valid, b + 1)
                pool.wait_ge(self.used, self.nu * (b + 1) + u + 1)
                h = self.hid_of(u)
                pool.tensor_tensor(h, h, WV[:, 8 * u:8 * u + 8].unsqueeze(2).to_broadcast([P, 8, I1]), ALU.mult
                                   ).then_inc(self.weighted, 1)

            def ht_turn(self, g):
                if g >= 2:
                    return NTG + g - 2 + 1
                return max(v for v in range(NTG) if v % 2 == g) + 1

            def t_tensor(self, pe, b, g):
                if self.layer == 1 and g < 4:
                    pe.wait_ge(self.weighted, 1 + 8 * b + self.need[g])
                else:
                    pe.wait_ge(self.used, self.nu * (b + 1) + self.need[g])
                pe.wait_ge(self.hl, NTG * b + self.ht_turn(g))
                k0, nk = TGROUPS[g]
                settled(pe, passed)
                for j in range(nk):
                    w = P if k0 + j < KT - 1 else KLAST
                    mm = pe.transpose(ps[0:w, 4 + g % 2, j * P:(j + 1) * P],
                                      HID[:, (k0 + j) * P:(k0 + j) * P + w], ident[:])
                mm.then_inc(self.ht, 1)

            def ht_parts(self, g):
                k0, nk = TGROUPS[g]
                w = P if k0 + nk < KT else KLAST
                flat = "p k s -> p (k s)"
                return (ps[0:w, 4 + g % 2, 0:nk * P], ht_hi[0:w, k0:k0 + nk, :].rearrange(flat),
                        ht_lo[0:w, k0:k0 + nk, :].rearrange(flat))

            def t_scalar(self, act, b, g):
                act.wait_ge(self.ht, 1 + NTG * b + g + 1)
                act.wait_ge(self.down, 1 + b)
                src, hi, _ = self.ht_parts(g)
                act.copy(hi, src).then_inc(self.hh, 1)

            def t_vector(self, dve, b, g):
                dve.wait_ge(self.hh, NTG * b + g + 1)
                src, hi, lo = self.ht_parts(g)
                dve.tensor_tensor(lo, src, hi.bitcast(F32), ALU.subtract).then_inc(self.hl, 1)

            def d_tensor(self, pe, b, g):
                pe.wait_ge(self.hl, NTG * (b + 1) + g + 1)
                if g == 0:
                    pe.wait_ge(self.res, 1 + b)
                k0, nk = TGROUPS[g]
                for k in range(k0, k0 + nk):
                    w = P if k < KT - 1 else KLAST
                    at = DOWN_AT + k * C
                    mm = split3(pe, ps[:, 6, 0:C], ht_hi[0:w, k, :], ht_lo[0:w, k, :],
                                w_hi[0:w, at:at + C], w_lo[0:w, at:at + C], k == 0, k == KT - 1)
                if g == NTG - 1:
                    mm.then_inc(self.down, 1)

            def res_vector(self, dve, b):
                dve.wait_ge(self.down, 1 + b + 1)
                dve.scalar_tensor_tensor(X[:, b, :], ps[:, 6, 0:C], TG[:, self.tg:self.tg + 1], X[:, b, :],
                                         ALU.mult, ALU.add).then_inc(self.res, 1)

            def tensor(self, pe):
                pe.sem_inc(self.used, self.nu)
                pe.sem_inc(self.hl, NTG)
                for s in (self.ht, self.down, self.res, self.weighted):
                    pe.sem_inc(s, 1)
                if self.layer == 0:
                    pe.wait_ge(chunk_lo, 2 + GROUPS)
                else:
                    pe.wait_ge(later_lo, 1 + GROUPS)
                self.x_tensor(pe, FIRST)
                self.r_tensor(pe, 0)

                def body(b, last):
                    for what in self.order:
                        kind, n = what[0], int(what[1:] or 0)
                        if kind == "u":
                            self.u_tensor(pe, b, n)
                        elif kind == "T":
                            self.t_tensor(pe, b, n)
                        elif kind == "D":
                            self.d_tensor(pe, b, n)
                        elif kind == "P":
                            self.p_tensor(pe, b)
                        elif kind == "X" and not last:
                            self.x_tensor(pe, b + 1)
                        elif kind == "R" and not last:
                            self.r_tensor(pe, b + 1)

                with pe.Fori(0, NSEQ - 1) as b:
                    body(b, False)
                body(NSEQ - 1, True)

            def scalar(self, act):
                self.x_scalar(act, 0)
                self.r_scalar(act, 0)

                def body(b, last):
                    for what in self.order:
                        kind, n = what[0], int(what[1:] or 0)
                        if kind == "u":
                            self.u_scalar(act, b, n)
                        elif kind == "T":
                            self.t_scalar(act, b, n)
                        elif kind == "X" and not last:
                            self.x_scalar(act, b + 1)
                        elif kind == "R" and not last:
                            self.r_scalar(act, b + 1)

                with act.Fori(0, NSEQ - 1) as b:
                    body(b, False)
                body(NSEQ - 1, True)

            def vector(self, dve):
                n, top = ((E0, TOP0), (E1, TOP1))[self.layer]
                dve.memset(prob[:, n:n + 8], -1.0).then_inc(consts, 1)
                dve.memset(sel8[:], -1.0).then_inc(consts, 1)
                if self.layer == 1:
                    dve.memset(earlier[:], 0.0).then_inc(self.pread, 1)
                dve.wait_ge(consts, 6 if self.layer == 0 else 8)
                self.norm.vector(dve, 0, lambda: None)
                self.x_vector(dve, 0)
                self.r_vector(dve, 0)

                def body(b, last):
                    for what in self.order:
                        kind, n = what[0], int(what[1:] or 0)
                        if kind == "u":
                            self.u_vector(dve, b, n)
                            if n == 2 and not last:
                                self.norm.vector(dve, b + 1, lambda: dve.wait_ge(self.xt, b + 1))
                        elif kind == "T":
                            self.t_vector(dve, b, n)
                        elif kind == "P":
                            self.p_vector(dve, b)
                        elif kind == "X" and not last:
                            self.x_vector(dve, b + 1)
                        elif kind == "R" and not last:
                            self.r_vector(dve, b + 1)
                    self.res_vector(dve, b)

                with dve.Fori(0, NSEQ - 1) as b:
                    body(b, False)
                body(NSEQ - 1, True)

            def gpsimd(self, pool):
                self.norm.gpsimd(pool, 0)

                def body(b, last):
                    if self.layer == 1:
                        for u in range(8):
                            self.u_gpsimd(pool, b, u)
                            if u == 2 and not last:
                                self.norm.gpsimd(pool, b + 1)
                    elif not last:
                        self.norm.gpsimd(pool, b + 1)

                with pool.Fori(0, NSEQ - 1) as b:
                    body(b, False)
                body(NSEQ - 1, True)

        class Attention:
            FX, FA, FQK, FV, FAT, FKT, FQT = 0, 1, 2, 3, 4, 6, 8

            def __init__(self):
                self.norm = Norm("at", xn_a)
                self.mdone = sem("at_fill")
                self.mread = [sem("at_read6"), sem("at_read7")]
                self.xh, self.ch, self.cl = sem("at_xh"), sem("at_ch"), sem("at_cl")
                self.roped, self.rsteps = sem("at_roped"), sem("at_rope_steps")
                self.akh, self.qkh, self.qkl = sem("at_akh"), sem("at_qkh"), sem("at_qkl")
                self.sq, self.sqread = sem("at_sq"), sem("at_sqread")
                self.msteps, self.maxed = sem("at_max_steps"), sem("at_maxed")
                self.mxt, self.mxt_sb = sem("at_mxt"), sem("at_mxt_sb")
                self.qb = sem("at_qb")
                self.sk, self.skread, self.pv = sem("at_sk"), sem("at_exp"), sem("at_pv")
                self.onorm, self.osteps, self.oh = sem("at_onorm"), sem("at_o_steps"), sem("at_oh")
                self.setup = sem("at_setup")
                self.mask_in = [sem("at_mask_in0"), sem("at_mask_in1")]
                self.mask_hi, self.mask_lo = sem("at_mask_hi"), sem("at_mask_lo")

            @staticmethod
            def half_front(b):
                return 6 * b - 1 if b is not FIRST else 0

            @staticmethod
            def half_out(b):
                return 6 * b + 10 if b is not NSEQ - 1 else 6 * b + 5

            def fill_ready(self, pe, half, f):
                pe.wait_ge(self.mread[f % 2], 1 + half + f // 2)
                return ps[:, 6 + f % 2, :]

            def filled(self, eng, half, f):
                eng.wait_ge(self.mdone, 2 * half + f + 1)
                return ps[:, 6 + f % 2, :]

            def used_up(self, eng, half, f):
                eng.wait_ge(self.mread[f % 2], 1 + half + f // 2 + 1)

            @staticmethod
            def max_heads(k):
                return k % 4, 2 * (k // 4)

            def masks_sync(self, sp, b, par):
                sp.dma_start(mask_q_sb[:, par, :], mask_q[b]).then_inc(self.mask_in[par], 16)
                sp.dma_start(mask_raw[:, par, :], mask_k[b]).then_inc(self.mask_in[par], 16)

            def blocks_sync(self, sp, b):
                half = self.half_front(b)
                if b is not FIRST:
                    sp.wait_ge(self.sk, 16 * b)
                for f in range(2):
                    self.used_up(sp, half, self.FQT + f)
                for t in range(4):
                    sp.dma_start(QB[32 * t:32 * t + 24, :, t, :].bitcast(F32), QT[32 * t:32 * t + 24, :, :].bitcast(F32)).then_inc(self.qb, 16)
                sp.wait_ge(self.mxt_sb, b + 1)
                for t in range(4):
                    sp.dma_start(QB[32 * t + 24:32 * t + 28, :, t, :].bitcast(F32),
                                 MXT[32 * t:32 * t + 32, :].bitcast(F32)).then_inc(self.qb, 16)

            def sync(self, sp):
                sp.wait_ge(self.setup, SETUP)
                self.masks_sync(sp, 0, 0)
                self.masks_sync(sp, 1, 1)
                self.blocks_sync(sp, FIRST)

                def body(b, par, masks, blocks):
                    if masks:
                        sp.wait_ge(self.sqread, 2 + 16 * (b + 1))
                        sp.wait_ge(self.mask_lo, b + 1)
                        self.masks_sync(sp, b + 2, par)
                    for slot in range(2):
                        sp.wait_ge(later_lo, 1 + 2 * b + slot)
                        sp.dma_start(raw[:, slot, :], w_ffn1[2 * b + slot]).then_inc(in_raw[slot], 16)
                    if blocks:
                        self.blocks_sync(sp, b + 1)

                with sp.Fori(0, NSEQ // 2 - 1) as i:
                    for par in range(2):
                        body(2 * i + par, par, True, True)
                body(NSEQ - 2, 0, False, True)
                body(NSEQ - 1, 1, False, False)

            def weights_scalar(self, act):
                act.wait_ge(in_late, 16)
                act.copy(wa_hi[:], wa_raw[:]).then_inc(chunk_hi, 1)

            def weights_gpsimd(self, pool):
                pool.wait_ge(chunk_hi, GROUPS + 1)
                pool.tensor_tensor(wa_lo[:], wa_raw[:], wa_hi[:].bitcast(F32), ALU.subtract).then_inc(later_lo, 1)

            def next_weights(self, b, slot):
                return bass.ds((2 * b + slot) * WCHUNK, WCHUNK)

            def front_tensor(self, pe, b, half):
                bank = self.fill_ready(pe, half, self.FX)
                pe.wait_ge(self.norm.xn_ready, b + 1)
                for kb in range(KC):
                    mm = pe.transpose(bank[:, kb * P:(kb + 1) * P], xn_a[:, kb * P:(kb + 1) * P], ident[:])
                mm.then_inc(self.mdone, 1)
                pe.wait_ge(self.cl, b + 1)
                bank = self.fill_ready(pe, half, self.FA)
                for kc in range(KC):
                    mm = split3(pe, bank, ca_hi[:, kc, :], ca_lo[:, kc, :],
                                wa_hi[:, kc, C:3 * C], wa_lo[:, kc, C:3 * C], kc == 0, kc == KC - 1)
                mm.then_inc(self.mdone, 1)
                self.used_up(pe, half, self.FX)
                for f, lo, width in ((self.FQK, 0, 2 * C), (self.FV, 2 * C, C)):
                    bank = self.fill_ready(pe, half, f)
                    for kc in range(KC):
                        mm = split3(pe, bank[:, 0:width], xa_hi[:, kc, :], xa_lo[:, kc, :],
                                    wa_hi[:, kc, lo:lo + width], wa_lo[:, kc, lo:lo + width], kc == 0, kc == KC - 1)
                    mm.then_inc(self.mdone, 1)
                self.used_up(pe, half, self.FA)
                self.stack_transposes(pe, half, self.FAT, AS)
                pe.wait_ge(self.qkl, 2 * b + 1)
                self.stack_transposes(pe, half, self.FKT, KS)
                pe.wait_ge(self.qkl, 2 * b + 2)
                self.stack_transposes(pe, half, self.FQT, QS)

            def stack_transposes(self, pe, half, f0, stack):
                for f in range(2):
                    bank = self.fill_ready(pe, half, f0 + f)
                    for q in range(4):
                        g = 4 * f + q
                        mm = pe.transpose(bank[:, q * P:(q + 1) * P],
                                          stack[:, 4 * g:4 * g + 4, :].rearrange("p h d -> p (h d)"), ident[:])
                    mm.then_inc(self.mdone, 1)

            def sq_tensor(self, pe, b, par, k):
                if k == 0:
                    for f in range(2):
                        self.used_up(pe, self.half_front(b), self.FQT + f)
                r, g0 = self.max_heads(k)
                rows = slice(32 * r, 32 * r + 32)
                pe.wait_ge(self.sqread, 16 * b + k + 1)
                for j in range(2):
                    mm = pe.matmul(ps[:, k % 2, 256 * j:256 * j + 256], QT[rows, g0 + j, :],
                                   KAT[rows, par, g0 + j, :, :], start=True, stop=True)
                mm.then_inc(self.sq, 1)

            def max_tensor(self, pe, b):
                pe.wait_ge(self.maxed, b + 1)
                pe.transpose(ps[:, 5, 384:512], MXS[:].rearrange("p t a g -> p (t a g)"), ident[:]
                             ).then_inc(self.mxt, 1)

            def sk_tensor(self, pe, b, par, k):
                a, g = k // 8, k % 8
                if k == 0:
                    pe.wait_ge(self.qb, 128 * (b + 1))
                    pe.wait_ge(self.mask_lo, b + 1)
                pe.wait_ge(self.skread, 16 * b + k + 1)
                bank = ps[:, 2 + k % 2, :]
                if a == 0:
                    for n, m in enumerate((mask_hi, mask_lo)):
                        pe.matmul(bank.rearrange("p (t q) -> p t q", t=4), ident_r[:],
                                  m[:, par, :].unsqueeze(1).to_broadcast([P, 4, TOK]), start=(n == 0), stop=False)
                pe.matmul(bank, KAT[:, par, g, a, :], QB[:, g, :, :].rearrange("p t q -> p (t q)"),
                          start=(a == 1), stop=True).then_inc(self.sk, 1)

            def pv_tensor(self, pe, b, par, k):
                a, g = k // 8, k % 8
                pe.wait_ge(self.skread, 2 + 16 * b + k + 1)
                if k == 0:
                    pe.wait_ge(self.onorm, 1 + b)
                for t in range(4):
                    h = 4 * g + t
                    mm = pe.matmul(ps[:, 4 + a, 9 * h:9 * h + 9], PR[:, k % 4, t, :], V9[:, par, a, h, :],
                                   start=True, stop=True, skip_group_check=True)
                mm.then_inc(self.pv, 1)

            def out_tensor(self, pe, b, half, next_max):
                pe.wait_ge(self.onorm, 1 + b + 1)
                bank = self.fill_ready(pe, half, 0)
                for kb in range(KC):
                    mm = pe.transpose(bank[:, kb * P:(kb + 1) * P], ON[:, kb * P:(kb + 1) * P], ident[:])
                mm.then_inc(self.mdone, 1)
                if next_max:
                    self.max_tensor(pe, b + 1)
                self.used_up(pe, half, 0)
                bank = self.fill_ready(pe, half, 1)
                for kc in range(KC):
                    mm = split3(pe, bank[:, 0:C], ot_hi[:, kc, :], ot_lo[:, kc, :],
                                wa_hi[:, kc, 3 * C:], wa_lo[:, kc, 3 * C:], kc == 0, kc == KC - 1)
                mm.then_inc(self.mdone, 1)

            def tensor(self, pe):
                pe.sem_inc(self.sqread, 2)
                pe.sem_inc(self.skread, 2)
                pe.sem_inc(self.pv, 4)
                for s in (*self.mread, self.onorm):
                    pe.sem_inc(s, 1)
                pe.wait_ge(later_lo, 1)
                pe.wait_ge(self.setup, SETUP)
                self.front_tensor(pe, FIRST, 0)
                for k in range(16):
                    self.sq_tensor(pe, FIRST, 0, k)
                self.max_tensor(pe, FIRST)
                self.front_tensor(pe, 1, self.half_front(1))

                def body(b, par, maxima, front):
                    for g in range(8):
                        for k in (2 * g, 2 * g + 1):
                            if maxima:
                                self.sq_tensor(pe, b + 1, 1 - par, k)
                        for k in (2 * g, 2 * g + 1):
                            self.sk_tensor(pe, b, par, k)
                        if g:
                            self.pv_tensor(pe, b, par, 2 * g - 2)
                            self.pv_tensor(pe, b, par, 2 * g - 1)
                    self.pv_tensor(pe, b, par, 14)
                    self.pv_tensor(pe, b, par, 15)
                    self.out_tensor(pe, b, self.half_out(b), maxima)
                    if front:
                        self.front_tensor(pe, b + 2, self.half_front(b + 2))

                with pe.Fori(0, NSEQ // 2 - 1) as i:
                    for par in range(2):
                        body(2 * i + par, par, True, True)
                body(NSEQ - 2, 0, True, False)
                body(NSEQ - 1, 1, False, False)

            def adapter_scalar(self, act, b):
                if b is not FIRST:
                    self.filled(act, self.half_front(b - 1) if b is not 1 else 0, self.FA)
                act.copy(ca_hi[:], CTXT[:, :, b, :]).then_inc(self.ch, 1)

            def front_scalar(self, act, b, par, half):
                flat = "p k s -> p (k s)"
                heads = "p (h d) -> p h d"
                bank = self.filled(act, half, self.FX)
                act.copy(xa_hi[:].rearrange(flat), bank[:, 0:C]).then_inc(self.xh, 1)
                bank = self.filled(act, half, self.FA)
                for at in (0, 16):
                    act.copy(AS[:, :, at:at + HD].bitcast(F32R), bank[:, 0:C].rearrange(heads, d=HD)
                             ).then_inc(self.akh, 1)
                act.copy(V9[:, par, 1, :, 0:HD], bank[:, C:2 * C].rearrange(heads, d=HD)).then_inc(self.akh, 1)
                bank = self.filled(act, half, self.FV)
                act.copy(V9[:, par, 0, :, 0:HD], bank[:, 0:C].rearrange(heads, d=HD)
                         ).then_inc(self.mread[self.FV % 2], 1)
                act.wait_ge(self.roped, b + 1)
                for at in (0, 16):
                    act.copy(KS[:, :, at:at + HD].bitcast(F32R), T1[:, 1]).then_inc(self.qkh, 1)
                for at in (0, 8):
                    act.copy(QS[:, :, at:at + HD].bitcast(F32R), T1[:, 0]).then_inc(self.qkh, 1)
                for f0, which in ((self.FAT, 1), (self.FKT, 0)):
                    for f in range(2):
                        bank = self.filled(act, half, f0 + f)
                        act.copy(KAT[:, par, 4 * f:4 * f + 4, which, :], bank.rearrange("p (q s) -> p q s", q=4)
                                 ).then_inc(self.mread[f], 1)
                if b is not FIRST:
                    act.wait_ge(self.qb, 128 * b)
                for f in range(2):
                    bank = self.filled(act, half, self.FQT + f)
                    act.copy(QT[:, 4 * f:4 * f + 4, :].rearrange("p q s -> p (q s)"), bank
                             ).then_inc(self.mread[f], 1)

            def max_scalar(self, act, b):
                act.wait_ge(self.mxt, b + 1)
                if b is not FIRST:
                    act.wait_ge(self.qb, 128 * b)
                act.copy(MXT[:], ps[:, 5, 384:512]).then_inc(self.mxt_sb, 1)

            def scalar(self, act):
                act.wait_ge(self.setup, SETUP)
                self.adapter_scalar(act, FIRST)
                self.front_scalar(act, FIRST, 0, 0)
                self.adapter_scalar(act, 1)
                self.max_scalar(act, FIRST)
                self.front_scalar(act, 1, 1, self.half_front(1))

                def body(b, par, maxima, front):
                    for k in range(16):
                        act.wait_ge(self.sk, 16 * b + k + 1)
                        act.wait_ge(self.pv, 16 * b + k + 1)
                        act.activation(PR[:, k % 4, :, :].rearrange("p t q -> p (t q)"), ps[:, 2 + k % 2, :],
                                       ACT.Exp).then_inc(self.skread, 1)
                        if k == 6 and front:
                            self.adapter_scalar(act, b + 2)
                        if k in (8, 12):
                            slot = (k - 8) // 4
                            split_hi(act, slot, GROUPS // 2 + b + 1, w_hi[:, self.next_weights(b, slot)], WCHUNK)
                    bank = self.filled(act, self.half_out(b), 0)
                    act.copy(ot_hi[:].rearrange("p k s -> p (k s)"), bank[:, 0:C]).then_inc(self.oh, 1)
                    if maxima:
                        self.max_scalar(act, b + 1)
                    if front:
                        self.front_scalar(act, b + 2, par, self.half_front(b + 2))

                with act.Fori(0, NSEQ // 2 - 1) as i:
                    for par in range(2):
                        body(2 * i + par, par, True, True)
                body(NSEQ - 2, 0, True, False)
                body(NSEQ - 1, 1, False, False)

            RSTEPS, OSTEPS = 2, 5

            def adapter_vector(self, dve, b):
                dve.wait_ge(self.ch, b + 1)
                dve.tensor_tensor(ca_lo[:], CTXT[:, :, b, :], ca_hi[:].bitcast(F32), ALU.subtract
                                  ).then_inc(self.cl, 1)

            def mask_vector(self, dve, b, par):
                dve.wait_ge(self.mask_in[par], 32 * (b // 2 + 1) if isinstance(b, int) else 16 * (b - par) + 32)
                dve.tensor_copy(mask_hi[:, par, :], mask_raw[:, par, :]).then_inc(self.mask_hi, 1)
                dve.wait_ge(self.mask_hi, b + 1)
                dve.tensor_tensor(mask_lo[:, par, :], mask_raw[:, par, :], mask_hi[:, par, :].bitcast(F32),
                                  ALU.subtract).then_inc(self.mask_lo, 1)

            def front_vector(self, dve, b, half):
                flat = "p k s -> p (k s)"
                heads = "p (h d) -> p h d"
                dve.wait_ge(self.xh, b + 1)
                bank = self.filled(dve, half, self.FX)
                dve.tensor_tensor(xa_lo[:].rearrange(flat), bank[:, 0:C], xa_hi[:].rearrange(flat).bitcast(F32),
                                  ALU.subtract).then_inc(self.mread[0], 1)
                dve.wait_ge(self.akh, 3 * b + 3)
                bank = self.filled(dve, half, self.FA)
                dve.tensor_tensor(AS[:, :, 8:16], bank[:, 0:C].rearrange(heads, d=HD), AS[:, :, 0:8],
                                  ALU.subtract).then_inc(self.mread[self.FA % 2], 1)
                st = Steps(dve, self.rsteps, b * self.RSTEPS)
                qk = self.filled(dve, half, self.FQK).rearrange("p (w h d) -> p w h d", w=2, d=HD)
                mid = HD // 2
                sin = rope[:, 1].unsqueeze(2).to_broadcast([P, 2, HEADS, HD])
                st.mark(dve.tensor_tensor(T1[:], qk, rope[:, 0].unsqueeze(2).to_broadcast([P, 2, HEADS, HD]), ALU.mult))
                st.mark(dve.tensor_tensor(T2[:, :, :, 0:mid], qk[:, :, :, mid:HD], sin[:, :, :, 0:mid], ALU.mult))
                dve.tensor_tensor(T2[:, :, :, mid:HD], qk[:, :, :, 0:mid], sin[:, :, :, mid:HD], ALU.mult
                                  ).then_inc(self.mread[self.FQK % 2], 1)
                assert st.n == self.RSTEPS, st.n
                dve.wait_ge(self.qkh, 4 * b + 2)
                dve.tensor_tensor(KS[:, :, 8:16], T1[:, 1], KS[:, :, 0:8], ALU.subtract).then_inc(self.qkl, 1)
                dve.wait_ge(self.qkh, 4 * b + 4)
                dve.tensor_tensor(QS[:, :, 16:24], T1[:, 0], QS[:, :, 0:8], ALU.subtract).then_inc(self.qkl, 1)

            def sq_vector(self, dve, b, par, k):
                r, g0 = self.max_heads(k)
                if k == 0:
                    dve.wait_ge(self.mask_lo, b + 1)
                dve.wait_ge(self.sq, 16 * b + k + 1)
                bank = ps[:, k % 2, :]
                dve.tensor_reduce(MX[:, r, 1, g0:g0 + 2], bank.rearrange("p (j w s) -> p j w s", j=2, w=2)[:, :, 1, :],
                                  AX_X, ALU.max)
                for j in range(2):
                    ins = dve.tensor_tensor_reduce(junk[:, 2 * (k % 2) + j, :], bank[:, 256 * j:256 * j + P],
                                                   mask_q_sb[:, par, :], 1.0, -3.4e38, ALU.add, ALU.max,
                                                   MX[:, r, 0, g0 + j:g0 + j + 1])
                ins.then_inc(self.sqread, 1)

            def max_vector(self, dve, b):
                dve.wait_ge(self.sqread, 2 + 16 * (b + 1))
                parts = MXS[:].rearrange("p t (a w) g -> p w (t a) g", w=2)
                mx = MX[:].rearrange("p t a g -> p (t a) g")
                dve.tensor_scalar(parts[:, 0].bitcast(F32R), mx, -1.0, None, ALU.mult).then_inc(self.msteps, 1)
                dve.wait_ge(self.msteps, b + 1)
                dve.scalar_tensor_tensor(parts[:, 1], mx, -1.0, parts[:, 0], ALU.mult, ALU.subtract
                                         ).then_inc(self.maxed, 1)

            def out_vector(self, dve, b):
                dve.wait_ge(self.pv, 4 + 16 * (b + 1))
                st = Steps(dve, self.osteps, b * self.OSTEPS)
                outs = [ps[:, 4 + a, 0:9 * HEADS].rearrange("p (h d) -> p h d", d=9) for a in range(2)]
                dens = [den[:, a, :].unsqueeze(2).to_broadcast([P, HEADS, HD]) for a in range(2)]
                o1, o2 = (t[:, 0] for t in (T1, T2))
                for a in range(2):
                    st.mark(dve.reciprocal(den[:, a, :], outs[a][:, :, HD]))
                st.wait()
                st.mark(dve.tensor_tensor(den[:, 1, :], den[:, 1, :], THG[:], ALU.mult))
                st.wait()
                st.mark(dve.tensor_tensor(o1, outs[0][:, :, 0:HD], dens[0], ALU.mult))
                st.mark(dve.tensor_tensor(o2, outs[1][:, :, 0:HD], dens[1], ALU.mult))
                st.wait()
                dve.tensor_tensor(ON[:].rearrange("p (h d) -> p h d", d=HD), o1, o2, ALU.add).then_inc(self.onorm, 1)
                assert st.n == self.OSTEPS, st.n

            def residual_vector(self, dve, b, half):
                flat = "p k s -> p (k s)"
                dve.wait_ge(self.oh, b + 1)
                bank = ps[:, 6, :]
                dve.tensor_tensor(ot_lo[:].rearrange(flat), bank[:, 0:C], ot_hi[:].rearrange(flat).bitcast(F32),
                                  ALU.subtract).then_inc(self.mread[0], 1)
                bank = self.filled(dve, half, 1)
                dve.scalar_tensor_tensor(X[:, b, :], bank[:, 0:C], TG[:, 2:3], X[:, b, :], ALU.mult, ALU.add
                                         ).then_inc(self.mread[1], 1)

            def vector(self, dve):
                dve.wait_ge(ffn0.res, 1 + NSEQ)
                dve.memset(KS[:], 0.0).then_inc(self.setup, 1)
                dve.memset(AS[:], 0.0).then_inc(self.setup, 1)
                dve.memset(QS[:], 0.0).then_inc(self.setup, 1)
                dve.memset(QB[:].bitcast(F32), 0.0).then_inc(self.setup, 1)
                dve.memset(V9[:], 1.0).then_inc(self.setup, 1)
                dve.wait_ge(self.setup, 2)
                dve.memset(KS[:, :, 24:26], 1.0).then_inc(self.setup, 1)
                dve.memset(AS[:, :, 26:28], 1.0).then_inc(self.setup, 1)
                self.norm.vector(dve, FIRST, lambda: None)
                dve.wait_ge(self.setup, SETUP)
                self.adapter_vector(dve, FIRST)
                self.front_vector(dve, FIRST, 0)
                self.mask_vector(dve, 0, 0)
                self.mask_vector(dve, 1, 1)
                for k in range(16):
                    self.sq_vector(dve, FIRST, 0, k)
                    if k == 2:
                        self.norm.vector(dve, 1, lambda: self.filled(dve, 0, self.FX))
                        self.adapter_vector(dve, 1)
                self.max_vector(dve, FIRST)
                self.front_vector(dve, 1, self.half_front(1))

                def body(b, par, maxima, front):
                    for k in range(16):
                        if maxima:
                            self.sq_vector(dve, b + 1, 1 - par, k)
                        if k == 6 and front:
                            self.norm.vector(dve, b + 2, lambda: self.filled(dve, self.half_front(b + 1), self.FX))
                            self.adapter_vector(dve, b + 2)
                    if maxima:
                        self.max_vector(dve, b + 1)
                    self.out_vector(dve, b)
                    self.residual_vector(dve, b, self.half_out(b))
                    if front:
                        self.front_vector(dve, b + 2, self.half_front(b + 2))
                        self.mask_vector(dve, b + 2, par)

                with dve.Fori(0, NSEQ // 2 - 1) as i:
                    for par in range(2):
                        body(2 * i + par, par, True, True)
                body(NSEQ - 2, 0, True, False)
                body(NSEQ - 1, 1, False, False)

            def front_gpsimd(self, pool, b, half):
                self.used_up(pool, half, self.FQK)
                pool.tensor_tensor(T1[:], T1[:], T2[:], ALU.add).then_inc(self.roped, 1)

            def gpsimd(self, pool):
                self.norm.gpsimd(pool, FIRST)
                self.front_gpsimd(pool, FIRST, 0)
                self.norm.gpsimd(pool, 1)
                self.front_gpsimd(pool, 1, self.half_front(1))

                def body(b, front):
                    if front:
                        self.norm.gpsimd(pool, b + 2)
                    for slot in range(2):
                        split_lo(pool, slot, GROUPS + 1 + 2 * b + slot + 1, w_lo[:, self.next_weights(b, slot)],
                                 w_hi[:, self.next_weights(b, slot)], WCHUNK, later_lo)
                    if front:
                        self.front_gpsimd(pool, b + 2, self.half_front(b + 2))

                with pool.Fori(0, NSEQ - 2) as b:
                    body(b, True)
                body(NSEQ - 2, False)
                body(NSEQ - 1, False)

        ffn0 = Ffn(0)
        attn = Attention()
        ffn1 = Ffn(1)

        block = ctx.enter_context(nc.Block())

        @block.sync
        def _(sp):
            mixer_sync(sp)
            attn.sync(sp)
            with sp.Fori(0, NSEQ) as b:
                sp.wait_ge(ffn1.res, 1 + b + 1)
                sp.dma_start(out[b], X[:, b, :]).then_inc(out_stored, 16)
            sp.wait_ge(out_stored, 16 * NSEQ)

        @block.scalar
        def _(act):
            mixer_scalar(act)
            attn.weights_scalar(act)
            ffn0.scalar(act)
            attn.scalar(act)
            ffn1.scalar(act)

        @block.gpsimd
        def _(pool):
            mixer_gpsimd(pool)
            attn.weights_gpsimd(pool)
            ffn0.gpsimd(pool)
            attn.gpsimd(pool)
            ffn1.gpsimd(pool)

        @block.tensor
        def _(pe):
            mixer_tensor(pe)
            ffn0.tensor(pe)
            attn.tensor(pe)
            ffn1.tensor(pe)

        @block.vector
        def _(dve):
            mixer_vector(dve)
            dve.wait_ge(a_res, 4)
            ffn0.vector(dve)
            attn.vector(dve)
            ffn1.vector(dve)


def layouts(inp):
    f = {k: np.asarray(v) for k, v in inp.items()}

    def rows(a):
        k = a.shape[0] // P
        return a.reshape(k, P, a.shape[1]).transpose(1, 0, 2).reshape(P, k * a.shape[1])

    def pad_rows(a, n):
        return np.concatenate([a, np.zeros((n - a.shape[0], a.shape[1]), a.dtype)], 0)

    def chunks(a, n):
        a = np.concatenate([a, np.zeros((P, n * (-(-a.shape[1] // n)) - a.shape[1]), a.dtype)], 1)
        return np.ascontiguousarray(a.reshape(P, n, -1).transpose(1, 0, 2))

    ctx = f["ctx_2048"]
    ctx_t = ctx.transpose(2, 0, 1).reshape(KC, P, NSEQ, TOK).transpose(1, 0, 2, 3).reshape(P, -1)
    k = f["L0_xattn_k"]
    k_pad = np.concatenate([np.zeros((GROUPS, C - 1), k.dtype), k], 1)
    toep = k_pad[:, C - 1 - np.arange(P)[:, None] + np.arange(C)[None, :]]

    gu = f["L0_ffn_shared_gate_up_w"]
    up = [gu[SHARED0 * t + I0 * n:SHARED0 * t + I0 * (n + 1)] for n in range(4) for t in range(2)]
    up0 = np.concatenate(up + [f["L0_ffn_w13"].reshape(-1, C)], 0).T
    down0 = np.concatenate([f["L0_ffn_shared_down_w"].T, f["L0_ffn_w2"].transpose(0, 2, 1).reshape(-1, C)], 0)
    route0 = np.concatenate([f["L0_ffn_gate_w"].T, f["L0_ffn_shared_gate_w"].T, np.zeros((C, 1), np.float32)], 1)
    up1 = np.concatenate([f["L1_ffn_w_up"].transpose(1, 0, 2).reshape(C, -1), f["L1_ffn_w_shared_up"]], 1)
    down1 = np.concatenate([f["L1_ffn_w_down"].reshape(-1, C), f["L1_ffn_w_shared_down"]], 0)

    def stream(up, down, route):
        a = np.concatenate([rows(up), rows(pad_rows(down, KT * P)), rows(route)], 1)
        a = np.concatenate([a, np.zeros((P, WCOLS - a.shape[1]), a.dtype)], 1)
        return chunks(a, 16)

    qkvo = np.concatenate([f["L1_xattn_Wq"], f["L1_xattn_Wk"], f["L1_xattn_Wv"], f["L1_xattn_Wo"]], 1)
    inv_freq = 1.0 / 10000.0 ** (np.arange(0, HD, 2, dtype=np.float32) / HD)
    emb = np.outer(np.arange(TOK, dtype=np.float32), inv_freq)
    emb = np.concatenate([emb, emb], -1)
    sign = np.where(np.arange(HD) < HD // 2, -1.0, 1.0)
    cos, sin = np.cos(emb), np.sin(emb) * sign
    scale = 1.0 / np.sqrt(np.float32(HD))
    rope = np.stack([np.stack([cos * scale, cos], 1), np.stack([sin * scale, sin], 1)], 1)
    mask = f["mask_Bx1xSxS_fk0"][:, 0]
    arrays = {
        "x": f["x"], "ctx_t": ctx_t, "toep": toep, "bias": f["fside_S2_0"],
        "gates": np.stack([f["g_xattn"][0], f["g_ffn"][0], f["g_xattn"][1], f["g_ffn"][1]]),
        "head_gate": f["L1_xattn_gate"].reshape(-1),
        "mask_q": mask, "mask_k": mask.transpose(0, 2, 1),
        "w_ffn0": stream(up0, down0, route0), "w_attn": rows(qkvo),
        "w_ffn1": stream(up1, down1, f["L1_ffn_w_gate"]),
        "ident_d": np.eye(P, dtype=np.float32),
        "before_d": np.triu(np.ones((P, P), np.float32), 1),
        "rope_d": rope.reshape(P, -1).astype(np.float32),
    }
    return {n: np.ascontiguousarray(a) for n, a in arrays.items()}


def kernel(**inputs):
    import concourse.bacc as bacc
    from concourse.bass_utils import run_bass_kernel_spmd

    nc = bacc.Bacc("TRN2", target_bir_lowering=False, num_devices=1, dynamic_dma_scratch_size=2048)
    arrays = layouts(inputs)
    args = {n: nc.dram_tensor(f"in_{n}", a.shape, mybir.dt.from_np(a.dtype), kind="ExternalInput").ap()
            for n, a in arrays.items()}
    out = nc.dram_tensor("out_0", (NSEQ, TOK, C), F32, kind="ExternalOutput").ap()
    program(nc, out=out, **args)
    r = run_bass_kernel_spmd(nc, [{f"in_{n}": a for n, a in arrays.items()}], core_ids=[0])
    return r.results[0]["out_0"]
```

```python
from contextlib import ExitStack

import numpy as np

import concourse.bass as bass
from concourse import mybir

ALU = mybir.AluOpType
ACT = mybir.ActivationFunctionType
AX_X = mybir.AxisListType.X
F32 = mybir.dt.float32
F32R = mybir.dt.float32r
BF16 = mybir.dt.bfloat16

P = 128
FIRST = 0
SETUP = 7
NSEQ = 8
TOK = 128
C = 256
KC = C // P
EPS = 1e-5

GROUPS = 16
GI = TOK // GROUPS

HIDDEN = 2112
UPW = 2 * HIDDEN
KT = -(-HIDDEN // P)
KLAST = HIDDEN - (KT - 1) * P
TGROUPS = [(g, min(4, KT - g)) for g in range(0, KT, 4)]
NTG = len(TGROUPS)
E0, I0, SHARED0 = 8, 176, 704
E1, I1, SHARED1 = 64, 32, 64
TOP0, TOP1, CAP = 2, 6, 128
ROUTE0 = E0 + 2
ROUTE1 = E1
WCOLS = KC * UPW + KT * C + KC * ROUTE1
DOWN_AT = KC * UPW
ROUTE_AT = DOWN_AT + KT * C
WCHUNK = WCOLS // 16

HEADS = 32
HD = C // HEADS
QUADS = HEADS // 4
ATTNW = 4 * C
LOWEST = -(2.0 - 2.0 ** -10) * 2.0 ** 127


class Steps:

    def __init__(self, eng, sem, base):
        self.eng, self.sem, self.base, self.n = eng, sem, base, 0

    def mark(self, ins):
        ins.then_inc(self.sem, 1)
        self.n += 1

    def wait(self):
        self.eng.wait_ge(self.sem, self.base + self.n)


def settled(eng, passed):
    eng.sem_inc(passed, 1)


def split3(pe, out, hi, lo, w_hi, w_lo, first, last):
    pe.matmul(out, hi, w_hi, start=first, stop=False)
    pe.matmul(out, hi, w_lo, start=False, stop=False)
    return pe.matmul(out, lo, w_hi, start=False, stop=last)


def program(nc, x, ctx_t, toep, bias, gates, head_gate, mask_q, mask_k, w_ffn0, w_attn, w_ffn1,
            ident_d, before_d, rope_d, out):
    with ExitStack() as ctx:
        def sem(name):
            return ctx.enter_context(nc.semaphore(name))

        def sb_in(scope):
            return lambda name, shape, dt=F32: scope.enter_context(nc.sbuf_tensor(name, shape, dt))

        sb = sb_in(ctx)
        ps = ctx.enter_context(nc.psum_tensor("ps", [P, 8, 512], F32))

        X = sb("residual", [P, NSEQ, C])
        CTXT = sb("ctx_t", [P, KC, NSEQ, TOK])
        ident = sb("ident", [P, P])
        ident_r = sb("ident_r", [P, P], F32R)
        before = sb("before", [P, P], BF16)
        ones_bf = sb("ones_bf", [P, P], BF16)
        rope = sb("rope", [P, 2, 2, HD])
        G = sb("gates", [P, 4])
        TG = sb("tanh_gates", [P, 4])
        HG = sb("head_gate", [P, HEADS])
        THG = sb("tanh_head_gate", [P, HEADS])
        w_hi = sb("w_hi", [P, WCOLS], F32R)
        w_lo = sb("w_lo", [P, WCOLS], F32R)
        wa_hi = sb("wa_hi", [P, KC, ATTNW], F32R)
        wa_lo = sb("wa_lo", [P, KC, ATTNW], F32R)
        raw = sb("raw_weights", [P, 2, WCHUNK])
        mhalf = sb("minus_half", [P, NSEQ])
        stats = sb("stats", [P, NSEQ, 6])
        mv = sb("mean_var", [P, NSEQ, 2])
        veps = sb("var_eps", [P, NSEQ])
        rstd = sb("rstd", [P, NSEQ])

        with ExitStack() as scope:
            sa = sb_in(scope)
            xn_u = sa("xn_then_skip", [P, NSEQ * C])
            XN = xn_u[:].rearrange("p (b c) -> p b c", b=NSEQ)
            U = xn_u[:].rearrange("p (k b s) -> p k b s", k=KC, b=NSEQ)
            VT = sa("v_t", [P, KC, NSEQ, TOK])
            R = sa("mixed_t", [P, KC, NSEQ, TOK])
            T = sa("toeplitz", [P, 2, C])
            KV = sa("kv", [P, 2, KC, 512])
            Z = sa("z", [P, 2, KC, 512])
            SK = sa("skip_sum", [P, KC * NSEQ * GROUPS])
            bias_b = sa("bias_b", [P, TOK])
            before_f = sa("before_f", [P, P])

        with ExitStack() as scope:
            sf = sb_in(scope)
            xn_f = sf("xn_f", [P, C])
            wa_raw = sf("wa_raw", [P, KC, ATTNW])
            xt_hi = sf("xt_hi", [P, KC, TOK], F32R)
            xt_lo = sf("xt_lo", [P, KC, TOK], F32R)
            SG = sf("silu_gate", [P, 4, 256])
            HID = sf("hidden", [P, HIDDEN])
            ht_hi = sf("hidden_t_hi", [P, KT, TOK], F32R)
            ht_lo = sf("hidden_t_lo", [P, KT, TOK], F32R)
            top8 = sf("top8", [P, 8])
            sel8 = sf("select8", [P, 8])
            neg_max = sf("neg_max", [P, 1])
            ex = sf("exps", [P, E1 + 2])
            ex_sum = sf("exp_sum", [P, 1])
            prob = sf("prob", [P, E1 + 8])
            marked = sf("marked", [P, E1 + 8])
            W = sf("route_w", [P, E1])
            WV = sf("route_w_valid", [P, E1])
            tmp1 = sf("tmp1", [P, E1])
            chosen = sf("chosen", [P, E1], BF16)
            earlier = sf("earlier", [P, E1], BF16)

        with ExitStack() as scope:
            sc = sb_in(scope)
            xa_hi = sc("xa_hi", [P, KC, TOK], F32R)
            xa_lo = sc("xa_lo", [P, KC, TOK], F32R)
            ca_hi = sc("ctx_then_out_t_hi", [P, KC, TOK], F32R)
            ca_lo = sc("ctx_then_out_t_lo", [P, KC, TOK], F32R)
            ot_hi, ot_lo = ca_hi, ca_lo
            T1 = sc("xn_then_rope", [P, 2, HEADS, HD])
            xn_a = T1[:, 0].rearrange("p h d -> p (h d)")
            T2 = sc("rope_sin_then_out", [P, 2, HEADS, HD])
            KAT = sc("ka_t", [P, 2, QUADS, 2, TOK], F32R)
            QT = sc("q_t", [P, 2, QUADS, TOK], F32R)
            VS = sc("v_staged", [P, 2, HEADS, HD])
            MX = sc("row_max", [P, 4, 2, 2, QUADS // 2])
            MXS = sc("max_split", [P, 4, 2, 2, QUADS])
            MXT = sc("max_t", [P, TOK], F32R)
            mask_q_sb = sc("mask_q", [P, 2, TOK])
            mask_raw = sc("mask_raw", [P, 2, TOK])
            mask_hi = sc("mask_hi", [P, 2, TOK], F32R)
            mask_lo = sc("mask_lo", [P, 2, TOK], F32R)
            PR = sc("probs", [P, 4, 4, TOK])
            den = sc("den", [P, 2, HEADS])
            QS = sc("q_stack", [P, HEADS, 32])
            KS = sc("k_stack", [P, HEADS, 32])
            AS = sc("a_stack", [P, HEADS, 32])
            QB = sc("q_blocks", [P, QUADS, 4, TOK], F32R)
            V9 = sc("v_ones", [P, 2, 2, HEADS, HD + 1])

        in_x = [sem("in_x0"), sem("in_x1")]
        in_ctx, in_const, in_late = sem("in_ctx"), sem("in_const"), sem("in_late")
        in_toep = [sem("in_toep0"), sem("in_toep1")]
        in_raw = [sem("in_raw0"), sem("in_raw1")]
        chunk_hi, chunk_lo, later_lo = sem("chunk_hi"), sem("chunk_lo"), sem("later_lo")
        consts = sem("consts")
        passed = sem("passed")
        gates_ready = sem("gates_ready")
        out_stored = sem("out_stored")
        a_steps, a_var, a_rstd, a_xn = sem("a_steps"), sem("a_var"), sem("a_rstd"), sem("a_xn")
        a_xt, a_vt = sem("a_xt"), sem("a_vt")
        a_kv, a_y, a_zread, a_red = sem("a_kv"), sem("a_y"), sem("a_zread"), sem("a_red")
        a_skip, a_u, a_rt, a_res = sem("a_skip"), sem("a_u"), sem("a_rt"), sem("a_res")
        a_rsum = sem("a_rsum")

        def split_hi(act, slot, landed, dst, width):
            act.wait_ge(in_raw[slot], 16 * landed)
            act.copy(dst, raw[:, slot, 0:width]).then_inc(chunk_hi, 1)

        def split_lo(eng, slot, n1, dst, hi, width, done):
            eng.wait_ge(chunk_hi, n1)
            eng.tensor_tensor(dst, raw[:, slot, 0:width], hi.bitcast(F32), ALU.subtract).then_inc(done, 1)

        def mixer_sync(sp):
            sp.dma_start(X[:, 0:4, :], x[0:4].rearrange("b s c -> s b c")).then_inc(in_x[0], 16)
            sp.dma_start(X[:, 4:8, :], x[4:8].rearrange("b s c -> s b c")).then_inc(in_x[1], 16)
            sp.dma_start(ident[:], ident_d).then_inc(in_const, 16)
            sp.dma_start(CTXT[:], ctx_t.rearrange("p (k b s) -> p k b s", k=KC, b=NSEQ)).then_inc(in_ctx, 16)
            sp.dma_start(bias_b[:], bias.partition_broadcast(P)).then_inc(in_const, 16)
            sp.dma_start(G[:], gates.partition_broadcast(P)).then_inc(in_const, 16)
            sp.dma_start(HG[:], head_gate.partition_broadcast(P)).then_inc(in_const, 16)
            sp.dma_start(rope[:], rope_d.rearrange("p (a b d) -> p a b d", a=2, b=2)).then_inc(in_const, 16)
            sp.dma_start(before_f[:], before_d).then_inc(in_const, 16)
            with sp.Fori(0, GROUPS // 2) as i:
                for par in range(2):
                    h = 2 * i + par
                    sp.wait_ge(a_y, h + 1)
                    sp.dma_start(T[:, par, :], toep[h]).then_inc(in_toep[par], 16)
                    sp.wait_ge(chunk_lo, h + 1)
                    sp.dma_start(raw[:, par, 0:WCHUNK], w_ffn0[h]).then_inc(in_raw[par], 16)
            sp.wait_ge(a_res, 4)
            sp.dma_start(wa_raw[:], w_attn.rearrange("p (k n) -> p k n", k=KC)).then_inc(in_late, 16)

        def mixer_scalar(act):
            act.wait_ge(in_const, 16 * 6)
            act.activation(TG[:], G[:], ACT.Tanh).then_inc(gates_ready, 1)
            act.activation(THG[:], HG[:], ACT.Tanh).then_inc(gates_ready, 1)
            for n in range(4):
                act.wait_ge(a_xt, n + 1)
                act.copy(VT[:, :, 2 * n:2 * n + 2, :],
                         ps[:, n, :].rearrange("p (k b s) -> p k b s", k=KC, b=2)).then_inc(a_vt, 1)
            with act.Fori(0, GROUPS // 2) as i:
                for par in range(2):
                    h = 2 * i + par
                    split_hi(act, par, i + 1, w_hi[:, bass.ds(h * WCHUNK, WCHUNK)], WCHUNK)

        def mixer_gpsimd(pool):
            for half in range(2):
                pool.wait_ge(a_var, half + 1)
                four = slice(4 * half, 4 * half + 4)
                pool.tensor_tensor(rstd[:, four], veps[:, four], mhalf[:, four], ALU.pow).then_inc(a_rstd, 1)
            pool.wait_ge(a_vt, 4)
            pool.wait_ge(in_ctx, 16)
            with pool.Fori(0, GROUPS // 2) as i:
                for par in range(2):
                    h = 2 * i + par
                    pool.wait_ge(a_y, h + 1)
                    for mb in range(KC):
                        v = VT[:, mb, :, bass.ds(h * GI, GI)].unsqueeze(3).to_broadcast([P, NSEQ, GI, GI])
                        k = CTXT[:, mb, :, bass.ds(h * GI, GI)].unsqueeze(2).to_broadcast([P, NSEQ, GI, GI])
                        pool.tensor_tensor(
                            KV[:, par, mb, :].rearrange("p (b i j) -> p b i j", b=NSEQ, i=GI), v, k, ALU.mult,
                        ).then_inc(a_kv, 1)
            pool.wait_ge(a_skip, 1)
            pool.tensor_tensor(
                U[:].rearrange("p k b (h j) -> p (k b h) j", j=GI),
                CTXT[:].rearrange("p k b (h j) -> p (k b h) j", j=GI),
                SK[:].unsqueeze(2).to_broadcast([P, KC * NSEQ * GROUPS, GI]), ALU.mult).then_inc(a_u, 1)

        def mixer_tensor(pe):
            pe.sem_inc(a_y, 2)
            pe.sem_inc(a_zread, 2)
            pe.wait_ge(in_const, 16 * 6)
            for n in range(4):
                pe.wait_ge(a_xn, 2 * n + 2)
                for kb in range(KC):
                    for b2 in range(2):
                        at = (kb * 2 + b2) * TOK
                        mm = pe.transpose(ps[:, n, at:at + TOK], XN[:, 2 * n + b2, kb * P:(kb + 1) * P], ident[:])
                mm.then_inc(a_xt, 1)
            with pe.Fori(0, GROUPS // 2) as i:
                for par in range(2):
                    h = 2 * i + par
                    y0, y1 = ps[:, 4 + 2 * par, :], ps[:, 5 + 2 * par, :]
                    pe.wait_ge(in_toep[par], 16 * i + 16)
                    pe.wait_ge(a_kv, 2 * h + 2)
                    pe.wait_ge(a_zread, h + 1)
                    pe.matmul(y0, T[:, par, 0:P], KV[:, par, 0, :], start=True, stop=True)
                    pe.matmul(y1, T[:, par, P:C], KV[:, par, 0, :], start=True, stop=False)
                    pe.matmul(y1, T[:, par, 0:P], KV[:, par, 1, :], start=False, stop=True).then_inc(a_y, 1)
            for n in range(4):
                pe.wait_ge(a_rsum, n + 1)
                for b2 in range(2):
                    for lb in range(KC):
                        at = b2 * C + lb * P
                        mm = pe.transpose(ps[:, n, at:at + P], R[:, lb, 2 * n + b2, :], ident[:])
                mm.then_inc(a_rt, 1)

        def mixer_vector(dve):
            st = Steps(dve, a_steps, 0)
            dve.sem_inc(chunk_lo, 2)
            dve.memset(mhalf[:], -0.5).then_inc(consts, 1)
            dve.memset(ones_bf[:], 1.0).then_inc(consts, 1)
            for half in range(2):
                four = range(4 * half, 4 * half + 4)
                dve.wait_ge(in_x[half], 16)
                for b in four:
                    st.mark(dve.bn_stats(stats[:, b, :], X[:, b, :]))
                for b in four:
                    dve.wait_ge(a_steps, 8 * half + b - four[0] + 1)
                    st.mark(dve.bn_aggr(mv[:, b, :], stats[:, b, :]))
                st.wait()
                dve.tensor_scalar(veps[:, 4 * half:4 * half + 4], mv[:, 4 * half:4 * half + 4, 1], EPS, None,
                                  ALU.add).then_inc(a_var, 1)
            for b in range(NSEQ):
                if b % 4 == 0:
                    dve.wait_ge(a_rstd, b // 4 + 1)
                dve.tensor_scalar(XN[:, b, :], X[:, b, :], mv[:, b, 0:1], rstd[:, b:b + 1],
                                  ALU.subtract, ALU.mult).then_inc(a_xn, 1)
            dve.wait_ge(in_const, 16 * 6)
            dve.tensor_copy(ident_r[:], ident[:]).then_inc(consts, 1)
            dve.tensor_copy(before[:], before_f[:]).then_inc(consts, 1)
            dve.wait_ge(in_ctx, 16)
            dve.wait_ge(a_xt, 4)
            for half in range(2):
                four = slice(4 * half, 4 * half + 4)
                dve.wait_ge(a_vt, 2 * half + 2)
                st.mark(dve.tensor_tensor(U[:, :, four, :], VT[:, :, four, :], CTXT[:, :, four, :], ALU.mult))
            st.wait()
            flat = "p k b s -> p (k b) s"
            st.mark(dve.tensor_tensor(U[:].rearrange(flat), U[:].rearrange(flat),
                                      bias_b[:].unsqueeze(1).to_broadcast([P, KC * NSEQ, TOK]), ALU.mult))
            st.wait()
            dve.tensor_reduce(SK[:], U[:].rearrange("p k b (h j) -> p (k b h) j", j=GI), AX_X, ALU.add
                              ).then_inc(a_skip, 1)
            with dve.Fori(0, GROUPS // 2) as i:
                for par in range(2):
                    h = 2 * i + par
                    dve.wait_ge(a_y, 2 + h + 1)
                    for lb in range(KC):
                        x1 = CTXT[:, lb, :, bass.ds(h * GI, GI)].unsqueeze(3).to_broadcast([P, NSEQ, GI, GI])
                        four = "p (b i j) -> p b i j"
                        ins = dve.tensor_tensor(
                            Z[:, par, lb, :].rearrange(four, b=NSEQ, i=GI),
                            ps[:, 4 + 2 * par + lb, :].rearrange(four, b=NSEQ, i=GI), x1, ALU.mult)
                    ins.then_inc(a_zread, 1)
                    split_lo(dve, par, h + 1, w_lo[:, bass.ds(h * WCHUNK, WCHUNK)],
                             w_hi[:, bass.ds(h * WCHUNK, WCHUNK)], WCHUNK, chunk_lo)
                    dve.wait_ge(a_zread, 2 + h + 1)
                    for lb in range(KC):
                        dve.tensor_reduce(R[:, lb, :, bass.ds(h * GI, GI)],
                                          Z[:, par, lb, :].rearrange("p (b i j) -> p b j i", b=NSEQ, i=GI),
                                          AX_X, ALU.add).then_inc(a_red, 1)
            dve.wait_ge(a_u, 1)
            dve.wait_ge(a_red, 2 * GROUPS)
            for n in range(4):
                two = slice(2 * n, 2 * n + 2)
                dve.tensor_tensor(R[:, :, two, :], R[:, :, two, :], U[:, :, two, :], ALU.add).then_inc(a_rsum, 1)
            dve.wait_ge(gates_ready, 2)
            for n in range(4):
                dve.wait_ge(a_rt, n + 1)
                xs = X[:, 2 * n:2 * n + 2, :].rearrange("p b c -> p (b c)")
                dve.scalar_tensor_tensor(xs, ps[:, n, :], TG[:, 0:1], xs, ALU.mult, ALU.add).then_inc(a_res, 1)

        class Norm:
            STEPS = 2

            def __init__(self, tag, xn):
                self.steps, self.var, self.rstd, self.xn_ready = (
                    sem(f"{tag}_norm_steps"), sem(f"{tag}_var"), sem(f"{tag}_rstd"), sem(f"{tag}_xn"))
                self.xn = xn

            def stats(self, dve, b):
                dve.bn_stats(stats[:, 0, :], X[:, b, :]).then_inc(self.steps, 1)

            def aggregate(self, dve, b):
                dve.wait_ge(self.steps, self.STEPS * b + 1)
                settled(dve, passed)
                dve.bn_aggr(mv[:, 0, :], stats[:, 0, :]).then_inc(self.steps, 1)

            def variance(self, dve, b):
                dve.wait_ge(self.steps, self.STEPS * b + 2)
                dve.tensor_scalar(veps[:, 0:1], mv[:, 0, 1:2], EPS, None, ALU.add).then_inc(self.var, 1)

            def scale(self, dve, b):
                dve.wait_ge(self.rstd, b + 1)
                dve.tensor_scalar(self.xn, X[:, b, :], mv[:, 0, 0:1], rstd[:, 0:1],
                                  ALU.subtract, ALU.mult).then_inc(self.xn_ready, 1)

            def vector(self, dve, b, xn_free):
                self.stats(dve, b)
                self.aggregate(dve, b)
                self.variance(dve, b)
                xn_free()
                self.scale(dve, b)

            def gpsimd(self, pool, b):
                pool.wait_ge(self.var, b + 1)
                pool.tensor_tensor(rstd[:, 0:1], veps[:, 0:1], mhalf[:, 0:1], ALU.pow).then_inc(self.rstd, 1)

        class Ffn:
            def __init__(self, layer):
                tag = f"f{layer}"
                self.layer = layer
                self.norm = Norm(tag, xn_f[:])
                self.xt, self.xh, self.xl = sem(f"{tag}_xt"), sem(f"{tag}_xh"), sem(f"{tag}_xl")
                self.logit, self.neg, self.exps = sem(f"{tag}_logit"), sem(f"{tag}_neg"), sem(f"{tag}_exps")
                self.w_ready, self.chosen, self.pos = sem(f"{tag}_w_ready"), sem(f"{tag}_chosen"), sem(f"{tag}_pos")
                self.valid, self.up, self.used = sem(f"{tag}_valid"), sem(f"{tag}_up"), sem(f"{tag}_used")
                self.silu, self.weighted, self.ht = sem(f"{tag}_silu"), sem(f"{tag}_weighted"), sem(f"{tag}_ht")
                self.hh, self.hl, self.down = sem(f"{tag}_hh"), sem(f"{tag}_hl"), sem(f"{tag}_down")
                self.res, self.rsteps, self.pread = sem(f"{tag}_res"), sem(f"{tag}_rsteps"), sem(f"{tag}_pread")
                if layer == 0:
                    self.units = [(2 * I0 * n, 2 * I0, I0 * n, I0) for n in range(12)]
                    self.need = [3, 6, 9, 12, 12]
                    self.order = ["u0", "u1", "u2", "u3", "u4", "T0", "u5", "u6", "u7", "T1", "u8", "D0", "u9",
                                  "u10", "T2", "u11", "D1", "X", "T3", "D2", "T4", "R", "D3", "D4"]
                    self.tg = 1
                    self.nroute = ROUTE0
                else:
                    self.units = [(512 * n, 512, 256 * n, 256) for n in range(8)] + [(4096, 128, 2048, 64)]
                    self.need = [2, 4, 6, 8, 9]
                    self.order = ["u0", "u1", "P", "u2", "u3", "T0", "u4", "u5", "T1", "D0", "u6", "u7", "T2", "u8",
                                  "X", "D1", "T3", "D2", "T4", "R", "D3", "D4"]
                    self.tg = 3
                    self.nroute = ROUTE1
                self.nu = len(self.units)

            def x_tensor(self, pe, b):
                pe.wait_ge(self.norm.xn_ready, b + 1)
                if b is not FIRST:
                    pe.wait_ge(self.w_ready, b)
                    if self.layer == 1:
                        pe.wait_ge(self.valid, b)
                for kb in range(KC):
                    mm = pe.transpose(ps[:, 7, kb * P:(kb + 1) * P], xn_f[:, kb * P:(kb + 1) * P], ident[:])
                mm.then_inc(self.xt, 1)

            def x_scalar(self, act, b):
                act.wait_ge(self.xt, b + 1)
                act.copy(xt_hi[:].rearrange("p k s -> p (k s)"), ps[:, 7, 0:C]).then_inc(self.xh, 1)

            def x_vector(self, dve, b):
                dve.wait_ge(self.xh, b + 1)
                dve.tensor_tensor(xt_lo[:].rearrange("p k s -> p (k s)"), ps[:, 7, 0:C],
                                  xt_hi[:].rearrange("p k s -> p (k s)").bitcast(F32), ALU.subtract
                                  ).then_inc(self.xl, 1)

            def r_tensor(self, pe, b):
                pe.wait_ge(self.xl, b + 1)
                for kc in range(KC):
                    at = ROUTE_AT + kc * self.nroute
                    mm = split3(pe, ps[:, 7, C:C + self.nroute], xt_hi[:, kc, :], xt_lo[:, kc, :],
                                w_hi[:, at:at + self.nroute], w_lo[:, at:at + self.nroute], kc == 0, kc == KC - 1)
                mm.then_inc(self.logit, 1)

            def r_scalar(self, act, b):
                if self.layer == 0:
                    act.wait_ge(self.neg, b + 1)
                    act.activation(ex[:, 0:E0], ps[:, 7, C:C + E0], ACT.Exp, bias=neg_max[:, 0:1],
                                   accum_out=ex_sum[:]).then_inc(self.exps, 1)
                    act.activation(ex[:, E0:E0 + 1], ps[:, 7, C + E0:C + E0 + 1], ACT.Exp, scale=-1.0
                                   ).then_inc(self.exps, 1)
                else:
                    act.wait_ge(self.logit, b + 1)
                    act.activation(ex[:, 0:E1], ps[:, 7, C:C + E1], ACT.Exp, scale=-1.0).then_inc(self.exps, 1)

            RSTEPS = (7, 8)

            def r_vector(self, dve, b):
                n, top = ((E0, TOP0), (E1, TOP1))[self.layer]
                width = n + 8 - top
                st = Steps(dve, self.rsteps, b * self.RSTEPS[self.layer])
                if self.layer == 0:
                    dve.wait_ge(self.logit, b + 1)
                    settled(dve, passed)
                    st.mark(dve.max(top8[:], ps[:, 7, C:C + E0]))
                    st.wait()
                    dve.tensor_scalar(neg_max[:], top8[:, 0:1], -1.0, None, ALU.mult).then_inc(self.neg, 1)
                    dve.wait_ge(self.exps, 2 * b + 2)
                    st.mark(dve.reciprocal(tmp1[:, 0:1], ex_sum[:]))
                    st.mark(dve.tensor_scalar(tmp1[:, 1:2], ex[:, E0:E0 + 1], 1.0, None, ALU.add))
                    st.wait()
                    st.mark(dve.tensor_scalar(prob[:, 0:n], ex[:, 0:n], tmp1[:, 0:1], None, ALU.mult))
                else:
                    dve.wait_ge(self.exps, b + 1)
                    st.mark(dve.tensor_scalar(tmp1[:], ex[:, 0:n], 1.0, None, ALU.add))
                    st.wait()
                    st.mark(dve.reciprocal(prob[:, 0:n], tmp1[:]))
                st.wait()
                settled(dve, passed)
                st.mark(dve.max(top8[:], prob[:, 0:n]))
                st.wait()
                st.mark(dve.tensor_copy(sel8[:, 0:top], top8[:, 0:top]))
                st.wait()
                settled(dve, passed)
                st.mark(dve.match_replace(marked[:, 0:width], sel8[:], prob[:, 0:width], -3.0))
                st.wait()
                if self.layer == 0:
                    dve.reciprocal(W[:, n:n + 1], tmp1[:, 1:2]).then_inc(self.pread, 1)
                    dve.scalar_tensor_tensor(W[:, 0:n], marked[:, 0:n], -2.0, prob[:, 0:n],
                                             ALU.is_lt, ALU.mult).then_inc(self.w_ready, 1)
                else:
                    st.mark(dve.scalar_tensor_tensor(W[:], marked[:, 0:n], -2.0, prob[:, 0:n],
                                                     ALU.is_lt, ALU.mult))
                    st.wait()
                    st.mark(dve.reduce_sum(ex_sum[:], W[:], axis=AX_X))
                    st.wait()
                    st.mark(dve.reciprocal(tmp1[:, 0:1], ex_sum[:]))
                    st.wait()
                    dve.tensor_scalar(W[:], W[:], tmp1[:, 0:1], None, ALU.mult).then_inc(self.w_ready, 1)
                    dve.tensor_scalar(chosen[:], marked[:, 0:n], -2.0, None, ALU.is_lt).then_inc(self.chosen, 1)
                assert st.n == self.RSTEPS[self.layer], st.n

            def p_tensor(self, pe, b):
                pe.wait_ge(self.chosen, b + 1)
                pe.wait_ge(self.pread, b + 1)
                pe.matmul(ps[:, 7, 384:384 + E1], before[:], chosen[:], start=True, stop=False)
                pe.matmul(ps[:, 7, 384:384 + E1], ones_bf[:], earlier[:], start=False, stop=True
                          ).then_inc(self.pos, 1)

            def p_vector(self, dve, b):
                dve.wait_ge(self.pos, b + 1)
                dve.wait_ge(self.w_ready, b + 1)
                dve.wait_ge(self.weighted, 1 + 8 * b)
                dve.scalar_tensor_tensor(WV[:], ps[:, 7, 384:384 + E1], float(CAP), W[:],
                                         ALU.is_lt, ALU.mult).then_inc(self.valid, 1)
                dve.tensor_tensor(earlier[:], earlier[:], chosen[:], ALU.add).then_inc(self.pread, 1)

            def bank_turn(self, u):
                if u >= 4:
                    return self.nu + u - 4 + 1
                last = max(v for v in range(self.nu) if v % 4 == u)
                return last + 1

            def u_tensor(self, pe, b, u):
                c0, width, _, _ = self.units[u]
                pe.wait_ge(self.used, b * self.nu + self.bank_turn(u))
                for kc in range(KC):
                    at = kc * UPW + c0
                    mm = split3(pe, ps[:, u % 4, 0:width], xt_hi[:, kc, :], xt_lo[:, kc, :],
                                w_hi[:, at:at + width], w_lo[:, at:at + width], kc == 0, kc == KC - 1)
                mm.then_inc(self.up, 1)

            def parts(self, u):
                bank = ps[:, u % 4, :]
                if self.layer == 0:
                    return bank[:, 0:I0], bank[:, I0:2 * I0]
                if u == 8:
                    return bank[:, SHARED1:2 * SHARED1], bank[:, 0:SHARED1]
                both = bank.rearrange("p (e t d) -> p e t d", e=8, t=2)
                return both[:, :, 0, :], both[:, :, 1, :]

            def silu_of(self, u):
                hw = self.units[u][3]
                s = SG[:, u % 4, 0:hw]
                return s.rearrange("p (e d) -> p e d", e=8) if self.layer == 1 and u < 8 else s

            def hid_of(self, u):
                _, _, h0, hw = self.units[u]
                s = HID[:, h0:h0 + hw]
                return s.rearrange("p (e d) -> p e d", e=8) if self.layer == 1 and u < 8 else s

            def u_scalar(self, act, b, u):
                act.wait_ge(self.up, b * self.nu + u + 1)
                act.activation(self.silu_of(u), self.parts(u)[0], ACT.Silu).then_inc(self.silu, 1)

            def u_vector(self, dve, b, u):
                if u == 0:
                    dve.wait_ge(self.ht, 1 + NTG * b)
                    if self.layer == 0:
                        dve.wait_ge(self.w_ready, b + 1)
                        dve.wait_ge(self.pread, b + 1)
                dve.wait_ge(self.silu, b * self.nu + u + 1)
                if self.layer == 0:
                    e = E0 if u < 4 else u - 4
                    dve.scalar_tensor_tensor(self.hid_of(u), self.silu_of(u), W[:, e:e + 1], self.parts(u)[1],
                                             ALU.mult, ALU.mult).then_inc(self.used, 1)
                else:
                    dve.tensor_tensor(self.hid_of(u), self.silu_of(u), self.parts(u)[1], ALU.mult
                                      ).then_inc(self.used, 1)

            def u_gpsimd(self, pool, b, u):
                if u == 0:
                    pool.wait_ge(self.valid, b + 1)
                pool.wait_ge(self.used, self.nu * (b + 1) + u + 1)
                h = self.hid_of(u)
                pool.tensor_tensor(h, h, WV[:, 8 * u:8 * u + 8].unsqueeze(2).to_broadcast([P, 8, I1]), ALU.mult
                                   ).then_inc(self.weighted, 1)

            def ht_turn(self, g):
                if g >= 2:
                    return NTG + g - 2 + 1
                return max(v for v in range(NTG) if v % 2 == g) + 1

            def t_tensor(self, pe, b, g):
                if self.layer == 1 and g < 4:
                    pe.wait_ge(self.weighted, 1 + 8 * b + self.need[g])
                else:
                    pe.wait_ge(self.used, self.nu * (b + 1) + self.need[g])
                pe.wait_ge(self.hl, NTG * b + self.ht_turn(g))
                k0, nk = TGROUPS[g]
                settled(pe, passed)
                for j in range(nk):
                    w = P if k0 + j < KT - 1 else KLAST
                    mm = pe.transpose(ps[0:w, 4 + g % 2, j * P:(j + 1) * P],
                                      HID[:, (k0 + j) * P:(k0 + j) * P + w], ident[:])
                mm.then_inc(self.ht, 1)

            def ht_parts(self, g):
                k0, nk = TGROUPS[g]
                w = P if k0 + nk < KT else KLAST
                flat = "p k s -> p (k s)"
                return (ps[0:w, 4 + g % 2, 0:nk * P], ht_hi[0:w, k0:k0 + nk, :].rearrange(flat),
                        ht_lo[0:w, k0:k0 + nk, :].rearrange(flat))

            def t_scalar(self, act, b, g):
                act.wait_ge(self.ht, 1 + NTG * b + g + 1)
                act.wait_ge(self.down, 1 + b)
                src, hi, _ = self.ht_parts(g)
                act.copy(hi, src).then_inc(self.hh, 1)

            def t_vector(self, dve, b, g):
                dve.wait_ge(self.hh, NTG * b + g + 1)
                src, hi, lo = self.ht_parts(g)
                dve.tensor_tensor(lo, src, hi.bitcast(F32), ALU.subtract).then_inc(self.hl, 1)

            def d_tensor(self, pe, b, g):
                pe.wait_ge(self.hl, NTG * (b + 1) + g + 1)
                if g == 0:
                    pe.wait_ge(self.res, 1 + b)
                k0, nk = TGROUPS[g]
                for k in range(k0, k0 + nk):
                    w = P if k < KT - 1 else KLAST
                    at = DOWN_AT + k * C
                    mm = split3(pe, ps[:, 6, 0:C], ht_hi[0:w, k, :], ht_lo[0:w, k, :],
                                w_hi[0:w, at:at + C], w_lo[0:w, at:at + C], k == 0, k == KT - 1)
                if g == NTG - 1:
                    mm.then_inc(self.down, 1)

            def res_vector(self, dve, b):
                dve.wait_ge(self.down, 1 + b + 1)
                dve.scalar_tensor_tensor(X[:, b, :], ps[:, 6, 0:C], TG[:, self.tg:self.tg + 1], X[:, b, :],
                                         ALU.mult, ALU.add).then_inc(self.res, 1)

            def tensor(self, pe):
                pe.sem_inc(self.used, self.nu)
                pe.sem_inc(self.hl, NTG)
                for s in (self.ht, self.down, self.res, self.weighted):
                    pe.sem_inc(s, 1)
                if self.layer == 0:
                    pe.wait_ge(chunk_lo, 2 + GROUPS)
                else:
                    pe.wait_ge(later_lo, 1 + GROUPS)
                self.x_tensor(pe, FIRST)
                self.r_tensor(pe, 0)

                def body(b, last):
                    for what in self.order:
                        kind, n = what[0], int(what[1:] or 0)
                        if kind == "u":
                            self.u_tensor(pe, b, n)
                        elif kind == "T":
                            self.t_tensor(pe, b, n)
                        elif kind == "D":
                            self.d_tensor(pe, b, n)
                        elif kind == "P":
                            self.p_tensor(pe, b)
                        elif kind == "X" and not last:
                            self.x_tensor(pe, b + 1)
                        elif kind == "R" and not last:
                            self.r_tensor(pe, b + 1)

                with pe.Fori(0, NSEQ - 1) as b:
                    body(b, False)
                body(NSEQ - 1, True)

            def scalar(self, act, beside=None):
                self.x_scalar(act, 0)
                self.r_scalar(act, 0)
                if beside:
                    beside(act)

                def body(b, last):
                    for what in self.order:
                        kind, n = what[0], int(what[1:] or 0)
                        if kind == "u":
                            self.u_scalar(act, b, n)
                        elif kind == "T":
                            self.t_scalar(act, b, n)
                        elif kind == "X" and not last:
                            self.x_scalar(act, b + 1)
                        elif kind == "R" and not last:
                            self.r_scalar(act, b + 1)

                with act.Fori(0, NSEQ - 1) as b:
                    body(b, False)
                body(NSEQ - 1, True)

            def vector(self, dve):
                n, top = ((E0, TOP0), (E1, TOP1))[self.layer]
                dve.memset(prob[:, n:n + 8], -1.0).then_inc(consts, 1)
                dve.memset(sel8[:], -1.0).then_inc(consts, 1)
                if self.layer == 1:
                    dve.memset(earlier[:], 0.0).then_inc(self.pread, 1)
                dve.wait_ge(consts, 6 if self.layer == 0 else 8)
                self.norm.vector(dve, 0, lambda: None)
                self.x_vector(dve, 0)
                self.r_vector(dve, 0)

                def body(b, last):
                    for what in self.order:
                        kind, n = what[0], int(what[1:] or 0)
                        if kind == "u":
                            self.u_vector(dve, b, n)
                            if n == 2 and not last:
                                self.norm.vector(dve, b + 1, lambda: dve.wait_ge(self.xt, b + 1))
                        elif kind == "T":
                            self.t_vector(dve, b, n)
                        elif kind == "P":
                            self.p_vector(dve, b)
                        elif kind == "X" and not last:
                            self.x_vector(dve, b + 1)
                        elif kind == "R" and not last:
                            self.r_vector(dve, b + 1)
                    self.res_vector(dve, b)

                with dve.Fori(0, NSEQ - 1) as b:
                    body(b, False)
                body(NSEQ - 1, True)

            def gpsimd(self, pool, beside=None):
                self.norm.gpsimd(pool, 0)
                if beside:
                    beside(pool)

                def body(b, last):
                    if self.layer == 1:
                        for u in range(8):
                            self.u_gpsimd(pool, b, u)
                            if u == 2 and not last:
                                self.norm.gpsimd(pool, b + 1)
                    elif not last:
                        self.norm.gpsimd(pool, b + 1)

                with pool.Fori(0, NSEQ - 1) as b:
                    body(b, False)
                body(NSEQ - 1, True)

        class Attention:
            FX, FQK, FV, FA, FQT0, FQT1, FKT0, FAT0, FKT1, FAT1 = range(10)
            TWO_MAXIMA = (6, 7, 9, 10)

            def maxima_beside(self, step):
                first = step + sum(s < step for s in self.TWO_MAXIMA)
                return [] if step > 11 else list(range(first, first + 1 + (step in self.TWO_MAXIMA)))

            def products_beside(self, step):
                if step in (2, 3):
                    return []
                if step in (8, 11):
                    return {8: [4, 5], 11: [8, 9]}[step]
                return [(step - (4 if step in range(4, 8) else 3 if step in (9, 10) else 2)) % 16]

            def __init__(self):
                self.norm = Norm("at", xn_a)
                self.mdone = sem("at_fill")
                self.mread = [sem("at_read6"), sem("at_read7")]
                self.xh, self.ch, self.cl = sem("at_xh"), sem("at_ch"), sem("at_cl")
                self.roped, self.rsteps = sem("at_roped"), sem("at_rope_steps")
                self.akh, self.qkh, self.qkl = sem("at_akh"), sem("at_qkh"), sem("at_qkl")
                self.sq, self.sqread = sem("at_sq"), sem("at_sqread")
                self.msteps, self.maxed = sem("at_max_steps"), sem("at_maxed")
                self.mxt, self.mxt_sb = sem("at_mxt"), sem("at_mxt_sb")
                self.qb = [sem("at_qb0"), sem("at_qb1")]
                self.sk, self.skread, self.pv = sem("at_sk"), sem("at_exp"), sem("at_pv")
                self.onorm, self.osteps, self.oh = sem("at_onorm"), sem("at_o_steps"), sem("at_oh")
                self.setup, self.vdone = sem("at_setup"), sem("at_values")
                self.mask_in = [sem("at_mask_in0"), sem("at_mask_in1")]
                self.mask_kept, self.mask_hi, self.mask_lo = sem("at_mask_kept"), sem("at_mask_hi"), sem("at_mask_lo")

            @staticmethod
            def half_front(b):
                return 6 * b

            @staticmethod
            def half_out(b):
                return 6 * b + 17 if not isinstance(b, int) or b < NSEQ - 2 else 5 * NSEQ + b + 2

            def no_out_tensor(self, pe, b):
                for f in (self.FKT1, self.FAT1):
                    self.used_up(pe, self.half_front(b + 2), f)
                pe.sem_inc(self.mdone, 2)

            def no_out_scalar(self, act, b):
                self.filled(act, self.half_out(b), 1)
                for s in self.mread:
                    act.sem_inc(s, 1)

            def fill_ready(self, pe, half, f):
                pe.wait_ge(self.mread[f % 2], 1 + half + f // 2)
                return ps[:, 6 + f % 2, :]

            def filled(self, eng, half, f):
                eng.wait_ge(self.mdone, 2 * half + f + 1)
                return ps[:, 6 + f % 2, :]

            def used_up(self, eng, half, f):
                eng.wait_ge(self.mread[f % 2], 1 + half + f // 2 + 1)

            @staticmethod
            def max_heads(k):
                return k % 4, 2 * (k // 4)

            def masks_sync(self, sp, b, par):
                sp.dma_start(mask_q_sb[:, par, :], mask_q[b]).then_inc(self.mask_in[par], 16)
                sp.dma_start(mask_raw[:, par, :], mask_k[b]).then_inc(self.mask_in[par], 16)

            def query_blocks_sync(self, sp, b, par, part):
                quads = slice(4 * part, 4 * part + 4)
                if b is not FIRST:
                    sp.wait_ge(self.sk, 16 * (b - 1) + 8 * (part + 1))
                self.used_up(sp, self.half_front(b), self.FQT1)
                for t in range(4):
                    sp.dma_start(QB[32 * t:32 * t + 24, quads, t, :].bitcast(F32),
                                 QT[32 * t:32 * t + 24, par, quads, :].bitcast(F32)).then_inc(self.qb[part], 16)

            def maxima_blocks_sync(self, sp, b, part):
                sp.wait_ge(self.mxt_sb, b + 1)
                for t in range(4):
                    at = 32 * t + 16 * part
                    sp.dma_start(QB[32 * t + 24:32 * t + 28, 4 * part:4 * part + 4, t, :].bitcast(F32),
                                 MXT[at:at + 16, :].bitcast(F32)).then_inc(self.qb[part], 16)

            def sync(self, sp):
                sp.wait_ge(ffn0.res, 1 + NSEQ)
                self.masks_sync(sp, 0, 0)
                self.masks_sync(sp, 1, 1)
                sp.wait_ge(self.setup, SETUP)
                for part in range(2):
                    self.query_blocks_sync(sp, FIRST, 0, part)
                    self.maxima_blocks_sync(sp, FIRST, part)

                def body(b, par, front, blocks):
                    if front:
                        sp.wait_ge(self.sqread, 2 + 16 * (b + 1))
                        sp.wait_ge(self.mask_lo, b + 1)
                        self.masks_sync(sp, b + 2, par)
                    for slot in range(2):
                        sp.wait_ge(later_lo, 1 + 2 * b + slot)
                        sp.dma_start(raw[:, slot, :], w_ffn1[2 * b + slot]).then_inc(in_raw[slot], 16)
                    if blocks:
                        for part in range(2):
                            self.query_blocks_sync(sp, b + 1, 1 - par, part)
                            self.maxima_blocks_sync(sp, b + 1, part)

                body(0, 0, True, True)
                with sp.Fori(0, NSEQ // 2 - 2) as i:
                    for par in (1, 0):
                        body(2 * i + (2 - par), par, True, True)
                body(NSEQ - 3, 1, True, True)
                body(NSEQ - 2, 0, False, True)
                body(NSEQ - 1, 1, False, False)

            def weights_scalar(self, act):
                act.wait_ge(in_late, 16)
                act.copy(wa_hi[:], wa_raw[:]).then_inc(chunk_hi, 1)

            def weights_gpsimd(self, pool):
                pool.wait_ge(chunk_hi, GROUPS + 1)
                pool.tensor_tensor(wa_lo[:], wa_raw[:], wa_hi[:].bitcast(F32), ALU.subtract).then_inc(later_lo, 1)

            def constants_gpsimd(self, pool):
                for tile, value in ((QS[:], 0.0), (AS[:], 0.0), (KS[:], 0.0), (QB[:].bitcast(F32), 0.0), (V9[:], 1.0)):
                    pool.memset(tile, value).then_inc(self.setup, 1)
                pool.wait_ge(self.setup, 3)
                pool.memset(KS[:, :, 24:27:2], 1.0).then_inc(self.setup, 1)
                pool.memset(AS[:, :, 25:28:2], 1.0).then_inc(self.setup, 1)

            def next_weights(self, b, slot):
                return bass.ds((2 * b + slot) * WCHUNK, WCHUNK)

            def turn_x_tensor(self, pe, b):
                bank = self.fill_ready(pe, self.half_front(b), self.FX)
                pe.wait_ge(self.norm.xn_ready, b + 1)
                for kb in range(KC):
                    mm = pe.transpose(bank[:, kb * P:(kb + 1) * P], xn_a[:, kb * P:(kb + 1) * P], ident[:])
                mm.then_inc(self.mdone, 1)

            def project_a_tensor(self, pe, b):
                pe.wait_ge(self.cl, b + 1)
                bank = self.fill_ready(pe, self.half_front(b), self.FA)
                for kc in range(KC):
                    mm = split3(pe, bank, ca_hi[:, kc, :], ca_lo[:, kc, :],
                                wa_hi[:, kc, C:3 * C], wa_lo[:, kc, C:3 * C], kc == 0, kc == KC - 1)
                mm.then_inc(self.mdone, 1)

            def project_x_tensor(self, pe, b, f, lo, width):
                half = self.half_front(b)
                self.used_up(pe, half, self.FX)
                bank = self.fill_ready(pe, half, f)
                for kc in range(KC):
                    mm = split3(pe, bank[:, 0:width], xa_hi[:, kc, :], xa_lo[:, kc, :],
                                wa_hi[:, kc, lo:lo + width], wa_lo[:, kc, lo:lo + width], kc == 0, kc == KC - 1)
                mm.then_inc(self.mdone, 1)

            def project_qk_tensor(self, pe, b):
                self.project_x_tensor(pe, b, self.FQK, 0, 2 * C)

            def project_v_tensor(self, pe, b):
                self.project_x_tensor(pe, b, self.FV, 2 * C, C)

            def turn_tensor(self, pe, b, fills):
                half = self.half_front(b)
                for f in fills:
                    if f in (self.FAT0, self.FAT1):
                        self.used_up(pe, half, self.FA)
                        stack, g0 = AS, 4 * (f == self.FAT1)
                    elif f in (self.FQT0, self.FQT1):
                        pe.wait_ge(self.qkl, 2 * b + 1)
                        stack, g0 = QS, 4 * (f == self.FQT1)
                    else:
                        pe.wait_ge(self.qkl, 2 * b + 2)
                        stack, g0 = KS, 4 * (f == self.FKT1)
                    bank = self.fill_ready(pe, half, f)
                    for q in range(4):
                        g = g0 + q
                        mm = pe.transpose(bank[:, q * P:(q + 1) * P],
                                          stack[:, 4 * g:4 * g + 4, :].rearrange("p h d -> p (h d)"), ident[:])
                    mm.then_inc(self.mdone, 1)

            def sq_tensor(self, pe, b, par, k):
                if k == 0:
                    for f in (self.FKT0, self.FAT0):
                        self.used_up(pe, self.half_front(b), f)
                    if b is not FIRST:
                        pe.wait_ge(self.mxt_sb, b)
                if k == 8:
                    for f in (self.FKT1, self.FAT1):
                        self.used_up(pe, self.half_front(b), f)
                r, g0 = self.max_heads(k)
                rows = slice(32 * r, 32 * r + 32)
                pe.wait_ge(self.sqread, 16 * b + k + 1)
                for j in range(2):
                    mm = pe.matmul(ps[:, k % 2, 256 * j:256 * j + 256], QT[rows, par, g0 + j, :],
                                   KAT[rows, par, g0 + j, :, :], start=True, stop=True)
                mm.then_inc(self.sq, 1)

            def max_tensor(self, pe, b):
                pe.wait_ge(self.maxed, b + 1)
                pe.transpose(ps[:, 0, 0:P], MXS[:].rearrange("p t h w n -> p (t h w n)"), ident[:]
                             ).then_inc(self.mxt, 1)

            def sk_tensor(self, pe, b, par, k):
                g, a = k // 2, k % 2
                if k % 8 == 0:
                    pe.wait_ge(self.qb[k // 8], 128 * (b + 1))
                if k == 0:
                    pe.wait_ge(self.mask_lo, b + 1)
                pe.wait_ge(self.skread, 16 * b + k + 1)
                bank = ps[:, 2 + k % 2, :]
                if a == 0:
                    for n, m in enumerate((mask_hi, mask_lo)):
                        pe.matmul(bank.rearrange("p (t q) -> p t q", t=4), ident_r[:],
                                  m[:, par, :].unsqueeze(1).to_broadcast([P, 4, TOK]), start=(n == 0), stop=False)
                pe.matmul(bank, KAT[:, par, g, a, :], QB[:, g, :, :].rearrange("p t q -> p (t q)"),
                          start=(a == 1), stop=True).then_inc(self.sk, 1)

            def pv_tensor(self, pe, b, par, k):
                g, a = k // 2, k % 2
                pe.wait_ge(self.skread, 2 + 16 * b + k + 1)
                if k == 0 and b is not FIRST:
                    pe.wait_ge(self.osteps, self.OSTEPS * b)
                for t in range(4):
                    h = 4 * g + t
                    mm = pe.matmul(ps[:, 4 + a, 9 * h:9 * h + 9], PR[:, k % 4, t, :], V9[:, par, a, h, :],
                                   start=True, stop=True, skip_group_check=True)
                mm.then_inc(self.pv, 1)

            def turn_out_tensor(self, pe, b):
                pe.wait_ge(self.onorm, b + 1)
                bank = self.fill_ready(pe, self.half_out(b), 0)
                for kb in range(KC):
                    mm = pe.transpose(bank[:, kb * P:(kb + 1) * P],
                                      T2[:, 0, 16 * kb:16 * kb + 16, :].rearrange("p h d -> p (h d)"), ident[:])
                mm.then_inc(self.mdone, 1)

            def project_out_tensor(self, pe, b):
                self.used_up(pe, self.half_out(b), 0)
                bank = self.fill_ready(pe, self.half_out(b), 1)
                for kc in range(KC):
                    mm = split3(pe, bank[:, 0:C], ot_hi[:, kc, :], ot_lo[:, kc, :],
                                wa_hi[:, kc, 3 * C:], wa_lo[:, kc, 3 * C:], kc == 0, kc == KC - 1)
                mm.then_inc(self.mdone, 1)

            def tensor(self, pe):
                pe.sem_inc(self.sqread, 2)
                pe.sem_inc(self.skread, 2)
                pe.sem_inc(self.pv, 4)
                for s in self.mread:
                    pe.sem_inc(s, 1)
                pe.wait_ge(later_lo, 1)
                turns = range(self.FQT0, self.FAT1 + 1)
                self.turn_x_tensor(pe, FIRST)
                self.project_qk_tensor(pe, FIRST)
                self.project_v_tensor(pe, FIRST)
                self.project_a_tensor(pe, FIRST)
                pe.wait_ge(self.setup, SETUP)
                self.turn_tensor(pe, FIRST, turns)
                self.no_out_tensor(pe, -2)
                self.turn_x_tensor(pe, 1)
                for k in range(16):
                    self.sq_tensor(pe, FIRST, 0, k)
                    if k == 3:
                        self.project_qk_tensor(pe, 1)
                    if k == 6:
                        self.project_v_tensor(pe, 1)
                    if k == 10:
                        self.project_a_tensor(pe, 1)
                self.turn_tensor(pe, 1, turns[:2])
                self.max_tensor(pe, FIRST)
                self.turn_tensor(pe, 1, turns[2:])
                self.no_out_tensor(pe, -1)

                def body(b, par, late, out, maxima, front):
                    for k in range(16):
                        self.sk_tensor(pe, b, par, k)
                        maxima_beside = [(b + 1, 1 - par, j) for j in self.maxima_beside(k)] if maxima else []
                        if len(maxima_beside) == 2:
                            self.sq_tensor(pe, *maxima_beside.pop(0))
                        if k > 1 or out:
                            of, slot = (b, par) if k > 1 else (b - 1, 1 - par)
                            for j in self.products_beside(k):
                                self.pv_tensor(pe, of, slot, j)
                        if k in (0, 3) and late:
                            self.turn_tensor(pe, b + 1, [self.FAT1 if k else self.FKT1])
                        if k == 4 and out:
                            self.turn_out_tensor(pe, b - 1)
                        if k == 6 and out:
                            self.project_out_tensor(pe, b - 1)
                        if k == 6 and front:
                            self.turn_x_tensor(pe, b + 2)
                        if k == 8 and front:
                            self.project_qk_tensor(pe, b + 2)
                        if k == 9 and front:
                            self.project_v_tensor(pe, b + 2)
                        if k == 11 and front:
                            self.project_a_tensor(pe, b + 2)
                        if k == 12 and maxima:
                            self.max_tensor(pe, b + 1)
                        if k in (13, 14) and front:
                            self.turn_tensor(pe, b + 2, [(self.FQT0, self.FQT1)[k - 13]])
                        if k == 15 and front:
                            self.turn_tensor(pe, b + 2, [self.FKT0, self.FAT0])
                        for fill in maxima_beside:
                            self.sq_tensor(pe, *fill)

                body(0, 0, False, False, True, True)
                with pe.Fori(0, NSEQ // 2 - 2) as i:
                    for par in (1, 0):
                        body(2 * i + (2 - par), par, True, True, True, True)
                body(NSEQ - 3, 1, True, True, True, True)
                body(NSEQ - 2, 0, True, True, True, False)
                body(NSEQ - 1, 1, False, True, False, False)
                for k in (14, 15):
                    self.pv_tensor(pe, NSEQ - 1, 1, k)
                self.turn_out_tensor(pe, NSEQ - 1)
                self.project_out_tensor(pe, NSEQ - 1)

            def adapter_scalar(self, act, b):
                if b is not FIRST:
                    self.filled(act, self.half_front(b - 1), self.FA)
                if not isinstance(b, int) or b > 2:
                    self.filled(act, self.half_out(b - 3), 1)
                act.copy(ca_hi[:], CTXT[:, :, b, :]).then_inc(self.ch, 1)

            def mask_scalar(self, act, b, par):
                act.wait_ge(self.mask_kept, b + 1)
                act.copy(mask_hi[:, par, :], mask_raw[:, par, :]).then_inc(self.mask_hi, 1)

            def x_scalar(self, act, b):
                bank = self.filled(act, self.half_front(b), self.FX)
                act.copy(xa_hi[:].rearrange("p k s -> p (k s)"), bank[:, 0:C]).then_inc(self.xh, 1)

            def project_a_scalar(self, act, b):
                heads = "p (h d) -> p h d"
                bank = self.filled(act, self.half_front(b), self.FA)
                for at in (0, 16):
                    act.copy(AS[:, :, at:at + HD].bitcast(F32R), bank[:, 0:C].rearrange(heads, d=HD)
                             ).then_inc(self.akh, 1)
                act.copy(VS[:, 1], bank[:, C:2 * C].rearrange(heads, d=HD)).then_inc(self.akh, 1)

            def project_v_scalar(self, act, b):
                bank = self.filled(act, self.half_front(b), self.FV)
                if b is not FIRST:
                    act.wait_ge(self.vdone, b)
                act.copy(VS[:, 0], bank[:, 0:C].rearrange("p (h d) -> p h d", d=HD)
                         ).then_inc(self.mread[self.FV % 2], 1)

            def stack_q_scalar(self, act, b):
                act.wait_ge(self.roped, b + 1)
                for at in (0, 8):
                    act.copy(QS[:, :, at:at + HD].bitcast(F32R), T1[:, 0]).then_inc(self.qkh, 1)

            def stack_k_scalar(self, act):
                for at in (0, 16):
                    act.copy(KS[:, :, at:at + HD].bitcast(F32R), T1[:, 1]).then_inc(self.qkh, 1)

            def turn_scalar(self, act, b, par, fills):
                for f in fills:
                    bank = self.filled(act, self.half_front(b), f)
                    four = "p (q s) -> p q s"
                    g0 = 4 * (f in (self.FAT1, self.FQT1, self.FKT1))
                    if f in (self.FQT0, self.FQT1):
                        dst = QT[:, par, g0:g0 + 4, :]
                    else:
                        dst = KAT[:, par, g0:g0 + 4, int(f in (self.FAT0, self.FAT1)), :]
                    act.copy(dst, bank.rearrange(four, q=4)).then_inc(self.mread[f % 2], 1)

            def max_scalar(self, act, b):
                act.wait_ge(self.mxt, b + 1)
                if b is not FIRST:
                    for part in range(2):
                        act.wait_ge(self.qb[part], 128 * b)
                act.copy(MXT[:], ps[:, 0, 0:P]).then_inc(self.mxt_sb, 1)

            def turned_out_scalar(self, act, b):
                bank = self.filled(act, self.half_out(b), 0)
                act.copy(ot_hi[:].rearrange("p k s -> p (k s)"), bank[:, 0:C]).then_inc(self.oh, 1)

            def scalar(self, act):
                act.wait_ge(self.norm.xn_ready, 1)
                turns = range(self.FQT0, self.FAT1 + 1)
                for b in range(2):
                    self.adapter_scalar(act, b)
                    self.x_scalar(act, b)
                    self.mask_scalar(act, b, b)
                    self.project_v_scalar(act, b)
                    if b == 0:
                        act.wait_ge(self.setup, SETUP)
                    self.stack_q_scalar(act, b)
                    self.stack_k_scalar(act)
                    self.project_a_scalar(act, b)
                    self.turn_scalar(act, b, b, turns[:2])
                    if b == 1:
                        self.max_scalar(act, FIRST)
                    self.turn_scalar(act, b, b, turns[2:])
                    self.no_out_scalar(act, b - 2)

                def body(b, par, late, out, maxima, front):
                    for k in range(16):
                        act.wait_ge(self.sk, 16 * b + k + 1)
                        act.wait_ge(self.pv, 16 * b + k + 1)
                        act.activation(PR[:, k % 4, :, :].rearrange("p t q -> p (t q)"), ps[:, 2 + k % 2, :],
                                       ACT.Exp).then_inc(self.skread, 1)
                        if k in (0, 3) and late:
                            self.turn_scalar(act, b + 1, 1 - par, [self.FAT1 if k else self.FKT1])
                        if k in (5, 9):
                            slot = int(k == 9)
                            split_hi(act, slot, GROUPS // 2 + b + 1, w_hi[:, self.next_weights(b, slot)], WCHUNK)
                        if k == 4 and out:
                            self.turned_out_scalar(act, b - 1)
                        if k == 6 and front:
                            self.x_scalar(act, b + 2)
                        if k == 7 and front:
                            self.adapter_scalar(act, b + 2)
                        if k == 10 and front:
                            self.project_v_scalar(act, b + 2)
                        if k == 11 and front:
                            self.stack_q_scalar(act, b + 2)
                        if k == 12 and front:
                            self.stack_k_scalar(act)
                        if k == 12 and maxima:
                            self.max_scalar(act, b + 1)
                        if k == 13 and front:
                            self.project_a_scalar(act, b + 2)
                        if k in (13, 14) and front:
                            self.turn_scalar(act, b + 2, par, [(self.FQT0, self.FQT1)[k - 13]])
                    if front:
                        self.turn_scalar(act, b + 2, par, [self.FKT0, self.FAT0])
                        self.mask_scalar(act, b + 2, par)

                body(0, 0, False, False, True, True)
                with act.Fori(0, NSEQ // 2 - 2) as i:
                    for par in (1, 0):
                        body(2 * i + (2 - par), par, True, True, True, True)
                body(NSEQ - 3, 1, True, True, True, True)
                body(NSEQ - 2, 0, True, True, True, False)
                body(NSEQ - 1, 1, False, True, False, False)
                self.turned_out_scalar(act, NSEQ - 1)

            RSTEPS, OSTEPS = 2, 5

            def x_vector(self, dve, b):
                flat = "p k s -> p (k s)"
                dve.wait_ge(self.xh, b + 1)
                bank = self.filled(dve, self.half_front(b), self.FX)
                dve.tensor_tensor(xa_lo[:].rearrange(flat), bank[:, 0:C], xa_hi[:].rearrange(flat).bitcast(F32),
                                  ALU.subtract).then_inc(self.mread[0], 1)

            def adapter_keys_vector(self, dve, b):
                dve.wait_ge(self.akh, 3 * b + 3)
                bank = self.filled(dve, self.half_front(b), self.FA)
                dve.tensor_tensor(AS[:, :, 8:16], bank[:, 0:C].rearrange("p (h d) -> p h d", d=HD), AS[:, :, 0:8],
                                  ALU.subtract).then_inc(self.mread[self.FA % 2], 1)

            def rope_vector(self, dve, b):
                st = Steps(dve, self.rsteps, b * self.RSTEPS)
                qk = self.filled(dve, self.half_front(b), self.FQK).rearrange("p (w h d) -> p w h d", w=2, d=HD)
                mid = HD // 2
                sin = rope[:, 1].unsqueeze(2).to_broadcast([P, 2, HEADS, HD])
                st.mark(dve.tensor_tensor(T1[:], qk, rope[:, 0].unsqueeze(2).to_broadcast([P, 2, HEADS, HD]), ALU.mult))
                st.mark(dve.tensor_tensor(T2[:, :, :, 0:mid], qk[:, :, :, mid:HD], sin[:, :, :, 0:mid], ALU.mult))
                dve.tensor_tensor(T2[:, :, :, mid:HD], qk[:, :, :, 0:mid], sin[:, :, :, mid:HD], ALU.mult
                                  ).then_inc(self.mread[self.FQK % 2], 1)
                assert st.n == self.RSTEPS, st.n

            def sq_vector(self, dve, b, par, k):
                r, g0 = self.max_heads(k)
                if k == 0:
                    dve.wait_ge(self.mask_in[par], 32 * (b // 2 + 1) if isinstance(b, int) else 16 * (b - par) + 32)
                dve.wait_ge(self.sq, 16 * b + k + 1)
                bank = ps[:, k % 2, :]
                part, at = g0 // 4, g0 % 4
                dve.tensor_reduce(MX[:, r, part, 1, at:at + 2], bank.rearrange("p (j w s) -> p j w s", j=2, w=2)[:, :, 1, :],
                                  AX_X, ALU.max)
                for j in range(2):
                    ins = dve.tensor_tensor_reduce(bank[:, 256 * j:256 * j + P], bank[:, 256 * j:256 * j + P],
                                                   mask_q_sb[:, par, :], 1.0, LOWEST, ALU.add, ALU.max,
                                                   MX[:, r, part, 0, at + j:at + j + 1])
                ins.then_inc(self.sqread, 1)

            def max_vector(self, dve, b):
                dve.wait_ge(self.sqread, 2 + 16 * (b + 1))
                parts = MXS[:].rearrange("p t h w n -> p w (t h) n")
                mx = MX[:].rearrange("p t h a g -> p (t h) (a g)")
                dve.tensor_scalar(parts[:, 0].bitcast(F32R), mx, -1.0, None, ALU.mult).then_inc(self.msteps, 1)
                dve.wait_ge(self.msteps, b + 1)
                dve.scalar_tensor_tensor(parts[:, 1], mx, -1.0, parts[:, 0], ALU.mult, ALU.subtract
                                         ).then_inc(self.maxed, 1)

            def out_vector(self, dve, b, part):
                outs = [ps[:, 4 + a, 0:9 * HEADS].rearrange("p (h d) -> p h d", d=9) for a in range(2)]
                dens = [den[:, a, :].unsqueeze(2).to_broadcast([P, HEADS, HD]) for a in range(2)]
                o1, o2 = T2[:, 0], T2[:, 1]
                done = self.OSTEPS * b
                if part == 0:
                    dve.wait_ge(self.pv, 4 + 16 * (b + 1))
                    for a in range(2):
                        dve.reciprocal(den[:, a, :], outs[a][:, :, HD]).then_inc(self.osteps, 1)
                if part == 1:
                    dve.wait_ge(self.osteps, done + 2)
                    dve.tensor_tensor(den[:, 1, :], den[:, 1, :], THG[:], ALU.mult).then_inc(self.osteps, 1)
                    dve.tensor_tensor(o1, outs[0][:, :, 0:HD], dens[0], ALU.mult).then_inc(self.osteps, 1)
                    dve.wait_ge(self.osteps, done + 3)
                    dve.tensor_tensor(o2, outs[1][:, :, 0:HD], dens[1], ALU.mult).then_inc(self.osteps, 1)
                if part == 2:
                    dve.wait_ge(self.osteps, done + 5)
                    dve.tensor_tensor(o1, o1, o2, ALU.add).then_inc(self.onorm, 1)

            def turned_out_vector(self, dve, b):
                flat = "p k s -> p (k s)"
                dve.wait_ge(self.oh, b + 1)
                bank = self.filled(dve, self.half_out(b), 0)
                dve.tensor_tensor(ot_lo[:].rearrange(flat), bank[:, 0:C], ot_hi[:].rearrange(flat).bitcast(F32),
                                  ALU.subtract).then_inc(self.mread[0], 1)

            def residual_vector(self, dve, b):
                bank = self.filled(dve, self.half_out(b), 1)
                dve.scalar_tensor_tensor(X[:, b, :], bank[:, 0:C], TG[:, 2:3], X[:, b, :], ALU.mult, ALU.add
                                         ).then_inc(self.mread[1], 1)

            def vector(self, dve):
                dve.wait_ge(ffn0.res, 1 + NSEQ)
                self.norm.vector(dve, FIRST, lambda: None)
                self.x_vector(dve, FIRST)
                self.rope_vector(dve, FIRST)
                self.adapter_keys_vector(dve, FIRST)
                dve.wait_ge(self.qkl, 2)
                self.norm.vector(dve, 1, lambda: None)
                for k in range(16):
                    self.sq_vector(dve, FIRST, 0, k)
                    if k == 2:
                        self.x_vector(dve, 1)
                    if k == 6:
                        self.rope_vector(dve, 1)
                self.max_vector(dve, FIRST)
                self.adapter_keys_vector(dve, 1)
                self.norm.stats(dve, 2)
                self.norm.aggregate(dve, 2)
                self.norm.variance(dve, 2)

                def body(b, par, out, maxima, front, stats_ahead):
                    for k in range(16):
                        if maxima:
                            self.sq_vector(dve, b + 1, 1 - par, k)
                        if k == 1 and out:
                            self.out_vector(dve, b - 1, 0)
                            self.out_vector(dve, b - 1, 1)
                        if k == 2 and out:
                            self.out_vector(dve, b - 1, 2)
                        if k == 4 and front:
                            dve.wait_ge(self.qkl, 2 * b + 4)
                            self.norm.scale(dve, b + 2)
                        if k == 5 and out:
                            self.turned_out_vector(dve, b - 1)
                        if k == 8 and out:
                            self.residual_vector(dve, b - 1)
                        if k == 9 and front:
                            self.x_vector(dve, b + 2)
                        if k == 11 and front:
                            self.rope_vector(dve, b + 2)
                        if k == 13 and stats_ahead:
                            self.norm.stats(dve, b + 3)
                        if k == 14 and stats_ahead:
                            self.norm.aggregate(dve, b + 3)
                        if k == 15 and maxima:
                            self.max_vector(dve, b + 1)
                        if k == 15 and stats_ahead:
                            self.norm.variance(dve, b + 3)
                    if front:
                        self.adapter_keys_vector(dve, b + 2)

                body(0, 0, False, True, True, True)
                with dve.Fori(0, NSEQ // 2 - 2) as i:
                    for par in (1, 0):
                        body(2 * i + (2 - par), par, True, True, True, True)
                body(NSEQ - 3, 1, True, True, True, False)
                body(NSEQ - 2, 0, True, True, False, False)
                body(NSEQ - 1, 1, True, False, False, False)
                for part in range(3):
                    self.out_vector(dve, NSEQ - 1, part)
                self.turned_out_vector(dve, NSEQ - 1)
                self.residual_vector(dve, NSEQ - 1)

            def rope_gpsimd(self, pool, b):
                self.used_up(pool, self.half_front(b), self.FQK)
                pool.tensor_tensor(T1[:], T1[:], T2[:], ALU.add).then_inc(self.roped, 1)

            def values_gpsimd(self, pool, b, par):
                self.used_up(pool, self.half_front(b), self.FV)
                pool.wait_ge(self.akh, 3 * b + 3)
                if not isinstance(b, int) or b > 1:
                    pool.wait_ge(self.pv, 4 + 16 * (b - 1))
                settled(pool, passed)
                pool.tensor_copy(V9[:, par, :, :, 0:HD], VS[:]).then_inc(self.vdone, 1)

            def adapter_gpsimd(self, pool, b):
                pool.wait_ge(self.ch, b + 1)
                pool.tensor_tensor(ca_lo[:], CTXT[:, :, b, :], ca_hi[:].bitcast(F32), ALU.subtract
                                   ).then_inc(self.cl, 1)

            def bound_mask_gpsimd(self, pool, b, par):
                pool.wait_ge(self.mask_in[par], 32 * (b // 2 + 1) if isinstance(b, int) else 16 * (b - par) + 32)
                settled(pool, passed)
                pool.tensor_scalar(mask_raw[:, par, :], mask_raw[:, par, :], LOWEST, None, ALU.max
                                   ).then_inc(self.mask_kept, 1)

            def mask_gpsimd(self, pool, b, par):
                pool.wait_ge(self.mask_hi, b + 1)
                pool.tensor_tensor(mask_lo[:, par, :], mask_raw[:, par, :], mask_hi[:, par, :].bitcast(F32),
                                   ALU.subtract).then_inc(self.mask_lo, 1)

            def stack_gpsimd(self, pool, b):
                pool.wait_ge(self.qkh, 4 * b + 2)
                pool.tensor_tensor(QS[:, :, 16:24], T1[:, 0], QS[:, :, 0:8], ALU.subtract).then_inc(self.qkl, 1)
                pool.wait_ge(self.qkh, 4 * b + 4)
                pool.tensor_tensor(KS[:, :, 8:16], T1[:, 1], KS[:, :, 0:8], ALU.subtract).then_inc(self.qkl, 1)

            def gpsimd(self, pool):
                self.norm.gpsimd(pool, FIRST)
                for b in range(2):
                    if b == 1:
                        self.norm.gpsimd(pool, 1)
                    self.bound_mask_gpsimd(pool, b, b)
                    self.adapter_gpsimd(pool, b)
                    self.rope_gpsimd(pool, b)
                    self.stack_gpsimd(pool, b)
                    self.mask_gpsimd(pool, b, b)
                    self.values_gpsimd(pool, b, b)
                self.norm.gpsimd(pool, 2)

                def body(b, par, late, front, stats_ahead):
                    def split(slot):
                        split_lo(pool, slot, GROUPS + 1 + 2 * b + slot + 1, w_lo[:, self.next_weights(b, slot)],
                                 w_hi[:, self.next_weights(b, slot)], WCHUNK, later_lo)

                    if late:
                        self.values_gpsimd(pool, b + 1, 1 - par)
                    split(0)
                    if front:
                        self.adapter_gpsimd(pool, b + 2)
                        self.rope_gpsimd(pool, b + 2)
                        self.stack_gpsimd(pool, b + 2)
                    split(1)
                    if front:
                        self.bound_mask_gpsimd(pool, b + 2, par)
                    if stats_ahead:
                        self.norm.gpsimd(pool, b + 3)
                    if front:
                        self.mask_gpsimd(pool, b + 2, par)

                body(0, 0, False, True, True)
                with pool.Fori(0, NSEQ // 2 - 2) as i:
                    for par in (1, 0):
                        body(2 * i + (2 - par), par, True, True, True)
                body(NSEQ - 3, 1, True, True, False)
                body(NSEQ - 2, 0, True, False, False)
                body(NSEQ - 1, 1, False, False, False)

        ffn0 = Ffn(0)
        attn = Attention()
        ffn1 = Ffn(1)

        block = ctx.enter_context(nc.Block())

        @block.sync
        def _(sp):
            mixer_sync(sp)
            attn.sync(sp)
            with sp.Fori(0, NSEQ) as b:
                sp.wait_ge(ffn1.res, 1 + b + 1)
                sp.dma_start(out[b], X[:, b, :]).then_inc(out_stored, 16)
            sp.wait_ge(out_stored, 16 * NSEQ)

        @block.scalar
        def _(act):
            mixer_scalar(act)
            ffn0.scalar(act, attn.weights_scalar)
            attn.scalar(act)
            ffn1.scalar(act)

        @block.gpsimd
        def _(pool):
            mixer_gpsimd(pool)
            ffn0.gpsimd(pool, attn.weights_gpsimd)
            attn.constants_gpsimd(pool)
            attn.gpsimd(pool)
            ffn1.gpsimd(pool)

        @block.tensor
        def _(pe):
            mixer_tensor(pe)
            ffn0.tensor(pe)
            attn.tensor(pe)
            ffn1.tensor(pe)

        @block.vector
        def _(dve):
            mixer_vector(dve)
            dve.wait_ge(a_res, 4)
            ffn0.vector(dve)
            attn.vector(dve)
            ffn1.vector(dve)


def layouts(inp):
    f = {k: np.asarray(v) for k, v in inp.items()}

    def rows(a):
        k = a.shape[0] // P
        return a.reshape(k, P, a.shape[1]).transpose(1, 0, 2).reshape(P, k * a.shape[1])

    def pad_rows(a, n):
        return np.concatenate([a, np.zeros((n - a.shape[0], a.shape[1]), a.dtype)], 0)

    def chunks(a, n):
        a = np.concatenate([a, np.zeros((P, n * (-(-a.shape[1] // n)) - a.shape[1]), a.dtype)], 1)
        return np.ascontiguousarray(a.reshape(P, n, -1).transpose(1, 0, 2))

    ctx = f["ctx_2048"]
    ctx_t = ctx.transpose(2, 0, 1).reshape(KC, P, NSEQ, TOK).transpose(1, 0, 2, 3).reshape(P, -1)
    k = f["L0_xattn_k"]
    k_pad = np.concatenate([np.zeros((GROUPS, C - 1), k.dtype), k], 1)
    toep = k_pad[:, C - 1 - np.arange(P)[:, None] + np.arange(C)[None, :]]

    gu = f["L0_ffn_shared_gate_up_w"]
    up = [gu[SHARED0 * t + I0 * n:SHARED0 * t + I0 * (n + 1)] for n in range(4) for t in range(2)]
    up0 = np.concatenate(up + [f["L0_ffn_w13"].reshape(-1, C)], 0).T
    down0 = np.concatenate([f["L0_ffn_shared_down_w"].T, f["L0_ffn_w2"].transpose(0, 2, 1).reshape(-1, C)], 0)
    route0 = np.concatenate([f["L0_ffn_gate_w"].T, f["L0_ffn_shared_gate_w"].T, np.zeros((C, 1), np.float32)], 1)
    up1 = np.concatenate([f["L1_ffn_w_up"].transpose(1, 0, 2).reshape(C, -1), f["L1_ffn_w_shared_up"]], 1)
    down1 = np.concatenate([f["L1_ffn_w_down"].reshape(-1, C), f["L1_ffn_w_shared_down"]], 0)

    def stream(up, down, route):
        a = np.concatenate([rows(up), rows(pad_rows(down, KT * P)), rows(route)], 1)
        a = np.concatenate([a, np.zeros((P, WCOLS - a.shape[1]), a.dtype)], 1)
        return chunks(a, 16)

    qkvo = np.concatenate([f["L1_xattn_Wq"], f["L1_xattn_Wk"], f["L1_xattn_Wv"], f["L1_xattn_Wo"]], 1)
    inv_freq = 1.0 / 10000.0 ** (np.arange(0, HD, 2, dtype=np.float32) / HD)
    emb = np.outer(np.arange(TOK, dtype=np.float32), inv_freq)
    emb = np.concatenate([emb, emb], -1)
    sign = np.where(np.arange(HD) < HD // 2, -1.0, 1.0)
    cos, sin = np.cos(emb), np.sin(emb) * sign
    scale = 1.0 / np.sqrt(np.float32(HD))
    rope = np.stack([np.stack([cos * scale, cos], 1), np.stack([sin * scale, sin], 1)], 1)
    mask = f["mask_Bx1xSxS_fk0"][:, 0]
    arrays = {
        "x": f["x"], "ctx_t": ctx_t, "toep": toep, "bias": f["fside_S2_0"],
        "gates": np.stack([f["g_xattn"][0], f["g_ffn"][0], f["g_xattn"][1], f["g_ffn"][1]]),
        "head_gate": f["L1_xattn_gate"].reshape(-1),
        "mask_q": mask, "mask_k": mask.transpose(0, 2, 1),
        "w_ffn0": stream(up0, down0, route0), "w_attn": rows(qkvo),
        "w_ffn1": stream(up1, down1, f["L1_ffn_w_gate"]),
        "ident_d": np.eye(P, dtype=np.float32),
        "before_d": np.triu(np.ones((P, P), np.float32), 1),
        "rope_d": rope.reshape(P, -1).astype(np.float32),
    }
    return {n: np.ascontiguousarray(a) for n, a in arrays.items()}


def kernel(**inputs):
    import concourse.bacc as bacc
    from concourse.bass_utils import run_bass_kernel_spmd

    nc = bacc.Bacc("TRN2", target_bir_lowering=False, num_devices=1, dynamic_dma_scratch_size=2048)
    arrays = layouts(inputs)
    args = {n: nc.dram_tensor(f"in_{n}", a.shape, mybir.dt.from_np(a.dtype), kind="ExternalInput").ap()
            for n, a in arrays.items()}
    out = nc.dram_tensor("out_0", (NSEQ, TOK, C), F32, kind="ExternalOutput").ap()
    program(nc, out=out, **args)
    r = run_bass_kernel_spmd(nc, [{f"in_{n}": a for n, a in arrays.items()}], core_ids=[0])
    return r.results[0]["out_0"]
```
